# Optimizing a Trainium2 kernel written in Bass

```python
import numpy as np
import jax
import jax.numpy as jnp

def _softmax(x, axis=-1):
    return jax.nn.softmax(x, axis=axis)

def _gelu(x):
    return jax.nn.gelu(x, approximate=True)

def _silu(x):
    return jax.nn.silu(x)

def _sigmoid(x):
    return jax.nn.sigmoid(x)

def _layernorm(x, axis=-1, eps=1e-05):
    m = jnp.mean(x, axis=axis, keepdims=True)
    v = jnp.var(x, axis=axis, keepdims=True)
    return (x - m) / jnp.sqrt(v + eps)

def _scatter_add(tgt, idx, src, axis=0):
    return tgt.at[idx].add(src)

def _segment_sum(src, seg, n):
    return jax.ops.segment_sum(src, seg, n)
kernel_name = 'mk_gnn_resnorm_d2_gnn_r32_d5fca1'

def setup_inputs(seed: int=0):
    np.random.seed(seed)
    _w = jnp.asarray

    def _rec_inputs():
        import jax
        import jax.numpy as jnp
        _gk = jax.random.key(seed)
        x = -0.000202 + 1 * jax.random.normal(jax.random.fold_in(_gk, 1), (50000, 128), jnp.float32)
        src = jax.random.randint(jax.random.fold_in(_gk, 2), (25000,), 0, 50000, jnp.int32)
        dst = jax.random.randint(jax.random.fold_in(_gk, 3), (25000,), 0, 50000, jnp.int32)
        _o = jnp.argsort(dst, stable=True)
        src = src[_o]
        dst = dst[_o]
        edge_attr_32 = 0.000283511 + 1.00007 * jax.random.normal(jax.random.fold_in(_gk, 12), (25000, 32), jnp.float32)
        edge_type_32 = jax.random.randint(jax.random.fold_in(_gk, 14), (25000,), 0, 32, jnp.int32)
        edge_weight1 = jax.random.uniform(jax.random.fold_in(_gk, 15), (25000, 1), jnp.float32, 0.0, 0.999998)
        return (x, src, dst, edge_attr_32, edge_type_32, edge_weight1)
    x, src, dst, edge_attr_32, edge_type_32, edge_weight1 = _rec_inputs()

    def _L0_gnn_setup():
        import jax, jax.numpy as jnp
        import numpy as np
        N, E, D, F, R, B = (50000, 50000, 128, 128, 32, 8)
        key = jax.random.key(seed)
        ks = jax.random.split(key, 9)
        h = jax.random.normal(ks[0], (N, D), dtype=jnp.float32)
        src = jax.random.randint(ks[1], (E,), 0, N, dtype=jnp.int32)
        dst = jax.random.randint(ks[2], (E,), 0, N, dtype=jnp.int32)
        etype = jax.random.randint(ks[3], (E,), 0, R, dtype=jnp.int32)
        norm = jax.random.uniform(ks[4], (E, 1), dtype=jnp.float32)
        weight = jax.random.normal(ks[5], (B, D, F), dtype=jnp.float32) * (2.0 / (D + F)) ** 0.5
        w_comp = jax.random.normal(ks[6], (R, B), dtype=jnp.float32) * (2.0 / (R + B)) ** 0.5
        loop_weight = jax.random.normal(ks[7], (D, F), dtype=jnp.float32) * (2.0 / (D + F)) ** 0.5
        h_bias = jnp.zeros((F,), dtype=jnp.float32)
        return {'h': h, 'src': src, 'dst': dst, 'etype': etype, 'norm': norm, 'weight': weight, 'w_comp': w_comp, 'loop_weight': loop_weight, 'h_bias': h_bias}
    _L0_gnn_all = _L0_gnn_setup()
    _L0_gnn_in = {k: v for k, v in _L0_gnn_all.items() if k in ('weight', 'w_comp', 'loop_weight', 'h_bias')}
    del _L0_gnn_all

    def _L1_gnn_setup():
        import jax, jax.numpy as jnp
        import numpy as np
        N = 3125
        E = 18750
        DIM = 128
        EDGE_DIM = 32
        key = jax.random.key(seed)
        ks = jax.random.split(key, 10)
        s = 1.0 / np.sqrt(DIM)
        se = 1.0 / np.sqrt(EDGE_DIM)
        return {'x': jax.random.normal(ks[0], (N, DIM), dtype=jnp.float32), 'edge_index': jax.random.randint(ks[1], (2, E), 0, N, dtype=jnp.int64), 'edge_attr': jax.random.normal(ks[2], (E, EDGE_DIM), dtype=jnp.float32), 'We': jax.random.uniform(ks[3], (EDGE_DIM, DIM), minval=-se, maxval=se, dtype=jnp.float32), 'be': jnp.zeros((DIM,), dtype=jnp.float32), 'W1': jax.random.uniform(ks[4], (DIM, DIM), minval=-s, maxval=s, dtype=jnp.float32), 'b1': jnp.zeros((DIM,), dtype=jnp.float32), 'W2': jax.random.uniform(ks[5], (DIM, DIM), minval=-s, maxval=s, dtype=jnp.float32), 'b2': jnp.zeros((DIM,), dtype=jnp.float32), 'eps': jnp.float32(0.0), 'gamma': jnp.ones((DIM,), dtype=jnp.float32), 'beta': jnp.zeros((DIM,), dtype=jnp.float32)}
    _L1_gnn_all = _L1_gnn_setup()
    _L1_gnn_in = {k: v for k, v in _L1_gnn_all.items() if k in ('We', 'be', 'W1', 'b1', 'W2', 'b2', 'eps', 'gamma', 'beta')}
    del _L1_gnn_all
    return {'x': x, 'src': src, 'dst': dst, 'edge_attr_32': edge_attr_32, 'edge_type_32': edge_type_32, 'edge_weight1': edge_weight1, 'L0_gnn_weight': _L0_gnn_in['weight'], 'L0_gnn_w_comp': _L0_gnn_in['w_comp'], 'L0_gnn_loop_weight': _L0_gnn_in['loop_weight'], 'L0_gnn_h_bias': _L0_gnn_in['h_bias'], 'L1_gnn_We': _L1_gnn_in['We'], 'L1_gnn_be': _L1_gnn_in['be'], 'L1_gnn_W1': _L1_gnn_in['W1'], 'L1_gnn_b1': _L1_gnn_in['b1'], 'L1_gnn_W2': _L1_gnn_in['W2'], 'L1_gnn_b2': _L1_gnn_in['b2'], 'L1_gnn_eps': _L1_gnn_in['eps'], 'L1_gnn_gamma': _L1_gnn_in['gamma'], 'L1_gnn_beta': _L1_gnn_in['beta']}

def reference(x, src, dst, edge_attr_32, edge_type_32, edge_weight1, L0_gnn_weight, L0_gnn_w_comp, L0_gnn_loop_weight, L0_gnn_h_bias, L1_gnn_We, L1_gnn_be, L1_gnn_W1, L1_gnn_b1, L1_gnn_W2, L1_gnn_b2, L1_gnn_eps, L1_gnn_gamma, L1_gnn_beta):
    import jax
    import jax.numpy as jnp

    def _L0_gnn_ref(h, src, dst, etype, norm, weight, w_comp, loop_weight, h_bias):
        import jax, jax.numpy as jnp
        import numpy as np
        N, E, D, F, R, B = (50000, 50000, 128, 128, 32, 8)
        n_nodes, d_in = h.shape
        n_rels = w_comp.shape[0]
        W_rel = jnp.einsum('rb,bdf->rdf', w_comp, weight)
        seg = etype * n_nodes + dst
        agg = jax.ops.segment_sum(h[src] * norm, seg, num_segments=n_rels * n_nodes)
        agg = agg.reshape(n_rels, n_nodes, d_in)
        node_repr = jnp.einsum('rnd,rdf->nf', agg, W_rel)
        node_repr = node_repr + h_bias + h @ loop_weight
        return jax.nn.relu(node_repr)

    def _L1_gnn_ref(x, edge_index, edge_attr, We, be, W1, b1, W2, b2, eps, gamma, beta):
        import jax, jax.numpy as jnp
        import numpy as np
        N = 3125
        E = 18750
        DIM = 128
        EDGE_DIM = 32
        i, j = (edge_index[0], edge_index[1])
        msg = x[j] + (edge_attr @ We + be)
        agg = jax.ops.segment_sum(msg, i, num_segments=x.shape[0])
        h = (1.0 + eps) * x + agg
        out = jax.nn.relu(h @ W1 + b1) @ W2 + b2
        mu = jnp.mean(out, axis=-1, keepdims=True)
        var = jnp.var(out, axis=-1, keepdims=True)
        out = (out - mu) * jax.lax.rsqrt(var + 1e-05) * gamma + beta
        return out
    edge_index = jnp.stack([src, dst])
    x = _layernorm(x + _L0_gnn_ref(x, src, dst, edge_type_32, edge_weight1, L0_gnn_weight, L0_gnn_w_comp, L0_gnn_loop_weight, L0_gnn_h_bias), axis=-1)
    x = _layernorm(x + _L1_gnn_ref(x, edge_index, edge_attr_32, L1_gnn_We, L1_gnn_be, L1_gnn_W1, L1_gnn_b1, L1_gnn_W2, L1_gnn_b2, L1_gnn_eps, L1_gnn_gamma, L1_gnn_beta), axis=-1)
    return x

_drawn_inputs = setup_inputs


def setup_inputs(seed=0):
    import zlib

    import numpy as np

    out = dict(_drawn_inputs(seed))
    spreads = {'L0_gnn_h_bias': (0.0, 0.1),
     'L1_gnn_be': (0.0, 0.1),
     'L1_gnn_b1': (0.0, 0.1),
     'L1_gnn_b2': (0.0, 0.1),
     'L1_gnn_gamma': (1.0, 0.2),
     'L1_gnn_beta': (0.0, 0.1)}
    factors = {}
    for name, (base, spread) in spreads.items():
        noise = np.random.default_rng([zlib.crc32(name.encode()), seed]).standard_normal(out[name].shape)
        drawn = base * np.exp(spread * noise) if base else spread * noise
        out[name] = jnp.asarray(drawn.astype(out[name].dtype))
    for name, factor in factors.items():
        out[name] = (out[name] * factor).astype(out[name].dtype)
    return out
```

```python
import concourse.bass as bass
from concourse import mybir
from contextlib import ExitStack


def gnn_two_layers(
    nc: bass.Bass,
    x: bass.AP,
    src: bass.AP,
    dst: bass.AP,
    edge_attr: bass.AP,
    edge_type: bass.AP,
    edge_weight: bass.AP,
    basis: bass.AP,
    w_comp: bass.AP,
    loop_weight: bass.AP,
    h_bias: bass.AP,
    We: bass.AP,
    be: bass.AP,
    W1: bass.AP,
    b1: bass.AP,
    W2: bass.AP,
    b2: bass.AP,
    eps: bass.AP,
    gamma: bass.AP,
    beta: bass.AP,
    out: bass.AP,
):
    f32 = mybir.dt.float32
    i32 = mybir.dt.int32
    bf16 = mybir.dt.bfloat16
    ALU = mybir.AluOpType
    ACT = mybir.ActivationFunctionType
    AX = mybir.AxisListType

    P = 128
    N, D = x.shape
    E = src.shape[0]
    ED = edge_attr.shape[1]
    R, B = w_comp.shape
    T = 4
    GP = T * P
    NG = -(-N // GP)
    NT = NG * T
    LAST = (NG - 1) * GP
    LAST_T = (N - LAST) // P
    LAST_R = N - LAST - LAST_T * P
    EG = -(-E // GP)
    ET = EG * T
    EROWS = (ET + 1) * P
    FULL = E // P
    REST = E - FULL * P
    NONE = 1 << 16
    LN_EPS = 1e-5
    MC = D + 4
    DCOL = D
    ONE, ENODE, EFROM, EC = ED, ED + 1, ED + 2, ED + 4
    QR = ET // 2
    QC = 2 * P
    QREST = E - (QR - 1) * QC
    A_OF = -(-(N // P + 1) // 32)
    CH = 7
    NCH = ET // CH
    SKIP = 1 << 20
    SEED = 2

    msg_rows = nc.dram_tensor("msg_rows", [EROWS + NT * P, MC], f32).ap()
    edge_rows = nc.dram_tensor("edge_rows", [EROWS + NT * P, EC], f32).ap()
    sum_rows = nc.dram_tensor("sum_rows", [NT * P, D], f32).ap()
    x1_rows = nc.dram_tensor("x1_rows", [N, D], f32).ap()
    counts_dram = nc.dram_tensor("counts_dram", [2, A_OF, 32], f32).ap()

    ctx = ExitStack()
    with ctx:
        def sb(name, shape, dt=f32):
            return ctx.enter_context(nc.sbuf_tensor(name, shape, dt))

        def sem(name):
            return ctx.enter_context(nc.semaphore(name))

        def sems(name, n):
            return [sem(f"{name}{i}") for i in range(n)]

        basis_sb = sb("basis_sb", [P, B, D])
        w_comp_sb = sb("w_comp_sb", [R, B])
        loop_sb = sb("loop_sb", [P, D])
        we_sb = sb("we_sb", [ED + 1, D])
        w1_sb = sb("w1_sb", [P, D])
        w2_sb = sb("w2_sb", [P, D])
        h_bias_sb = sb("h_bias_sb", [P, 1])
        b1_sb = sb("b1_sb", [P, 1])
        b2_sb = sb("b2_sb", [P, 1])
        gamma_sb = sb("gamma_sb", [P, D])
        beta_sb = sb("beta_sb", [P, D])
        eps_sb = sb("eps_sb", [P, 1])
        eps1_sb = sb("eps1_sb", [P, 1])
        ident = sb("ident", [P, P])
        self_diag = sb("self_diag", [P, P])
        count_up = sb("count_up", [P, GP])
        part_no = sb("part_no", [P, 1])
        group_start = sb("group_start", [P, NG])
        ones_bf = sb("ones_bf", [P, CH * 32], bf16)
        ones_col = sb("ones_col", [P, 1])
        dst_q = sb("dst_q", [QR, QC], i32)
        next_q = sb("next_q", [QR, QC], i32)
        src_q = sb("src_q", [QR, QC], i32)
        norm_q = sb("norm_q", [QR, QC])
        dst_qf = sb("dst_qf", [QR, QC])
        src_qf = sb("src_qf", [QR, QC])
        next_qf = sb("next_qf", [QR, QC])
        falls_q = sb("falls_q", [QR, QC])
        stat_q = sb("stat_q", [QR, 1])
        dst_t = sb("dst_t", [P, ET + 1])
        src_t = sb("src_t", [P, ET + 1])
        src_row = sb("src_row", [P, ET], i32)
        dst_row = sb("dst_row", [P, ET + 1], i32)
        norm_t = sb("norm_t", [P, ET])
        skip_t = sb("skip_t", [P, ET])
        node_i = sb("node_i", [P, 2, ET], i32)
        a_i = sb("a_i", [P, 2, ET], i32)
        b_i = sb("b_i", [P, 2, ET], i32)
        b_m = sb("b_m", [P, 2, ET], i32)
        a_f = sb("a_f", [P, 2, ET])
        b_f = sb("b_f", [P, 2, ET])
        tile_f = sb("tile_f", [P, ET])
        pairs_sb = sb("pairs_sb", [CH * A_OF, 2, CH * 32])
        counts_sb = sb("counts_sb", [A_OF, 2, 32])
        count_row = sb("count_row", [1, 2, A_OF * 32])
        stat_row = sb("stat_row", [1, 1])
        sums_start = sb("sums_start", [1, 2, NT])
        win_d = sb("win_d", [1, 2, NT])
        win_g = sb("win_g", [1, 2, NT])
        most = sb("most", [1, 2])
        fits = sb("fits", [1, 2])
        no_falls = sb("no_falls", [1, 1])
        win_row = sb("win_row", [1, 2, NT], i32)
        ok_i = sb("ok_i", [1, 2], i32)
        edge_out = sb("edge_out", [P, ET + 1, EC])
        pad_msgs = sb("pad_msgs", [P, MC])
        pad_edges = sb("pad_edges", [P, EC])
        steps_a = sb("steps_a", [A_OF, A_OF])
        before = sb("before", [P, P])
        a_from = sb("a_from", [A_OF, 1])
        srcs = sb("srcs", [P, 4, GP], i32)
        tiles_bc = sb("tiles_bc", [P, 2, GP], i32)
        same_tile = sb("same_tile", [P, 2, T, P], bf16)
        a_ge = sb("a_ge", [A_OF, 2, GP])
        a_hot = sb("a_hot", [P, 2, T, A_OF + 1], bf16)
        b_bf = sb("b_bf", [P, 2, T, 32], bf16)
        a_step = sb("a_step", [P, 2, T, A_OF], bf16)
        b_hot = sb("b_hot", [P, 4, T, 32])
        taken = sb("taken", [A_OF, 2, T + 1, 32])
        looked = sb("looked", [P, 2, T, 32])
        place_f = sb("place_f", [P, 2, T])
        place_s = sb("place_s", [P, 2, T])
        place_t = sb("place_t", [P, ET], i32)
        place_now = sb("place_now", [P, 2, T], i32)
        edge_now = sb("edge_now", [P, 2, T, EC])
        types = sb("types", [R, 4, GP], i32)
        type_hot = sb("type_hot", [R, 2, GP])
        src_now = sb("src_now", [P, 4, T], i32)
        xg = sb("xg", [P, 4, T, D])
        xg_t = sb("xg_t", [P, 2, GP])
        coef = sb("coef", [P, 2, T, B])
        seeds = sb("seeds", [P, 2, SEED, D])
        seed_sum = sb("seed_sum", [P, 2, D])
        msgs = sb("msgs", [P, 2, T, MC])
        marks = sb("marks", [P, 2, ET * (2 * A_OF + 32)], bf16)
        a_eq = marks[:, :, 0:ET * A_OF]
        a_lt = marks[:, :, ET * A_OF:2 * ET * A_OF]
        b_lt = marks[:, :, 2 * ET * A_OF:]
        reused = marks[:, :, :].rearrange("p l c -> p (l c)").bitcast(f32)
        parts, at = [], 0
        for slots, cols in ((4, D), (4, MC), (4, EC), (2, D), (2, D), (2, D), (2, D), (1, MC), (1, EC)):
            size = slots * T * cols
            parts.append(reused[:, at:at + size].rearrange("p (s t c) -> p s t c", s=slots, t=T))
            at += size
        xin, mwin, ewin, y, z, xb, res, g_rows, g_edges = parts
        g_rows, g_edges = g_rows[:, 0], g_edges[:, 0]
        hot = sb("hot", [P, 2, T, P])
        lhs_t = sb("lhs_t", [P, 2, GP])
        act_t = sb("act_t", [P, 2, GP])
        out_t = sb("out_t", [P, 2, GP])
        ea_t = sb("ea_t", [ED + 1, 2, GP])
        st = sb("st", [P, 2, T, 6])
        mv = sb("mv", [P, 2, T, 2])
        rstd = sb("rstd", [P, 2, T])
        shift = sb("shift", [P, 2, T])
        st2 = sb("st2", [P, 2, T, 6])
        mv2 = sb("mv2", [P, 2, T, 2])
        rstd2 = sb("rstd2", [P, 2, T])
        sd = sb("sd", [P, 2, T])
        sd2 = sb("sd2", [P, 2, T])
        ln_eps = sb("ln_eps", [P, 1])

        g_node0 = sb("g_node0", [P, T])
        g_key = sb("g_key", [P, 1])
        g_key_wide = sb("g_key_wide", [P, P])
        g_same = sb("g_same", [P, P])
        g_earlier = sb("g_earlier", [P, P])
        g_attr = sb("g_attr", [P, ED + 1])
        g_attr_t = sb("g_attr_t", [ED + 1, P])
        g_from = sb("g_from", [P, 1], i32)
        g_x = sb("g_x", [P, D])
        g_msg = sb("g_msg", [P, D])
        g_again = sb("g_again", [P, 1])
        g_at = sb("g_at", [P, 1], i32)
        g_sum = sb("g_sum", [P, MC])

        bank = [ctx.enter_context(nc.psum_tensor(f"bank{i}", [P, GP], f32)) for i in range(8)]

        wait_passed = sem("wait_passed")
        consts_loaded = sem("consts_loaded")
        lists_loaded = sem("lists_loaded")
        attr_loaded = sem("attr_loaded")
        pads_set = sem("pads_set")
        consts_made = sem("consts_made")
        zeroed = sem("zeroed")
        dve0 = sem("dve0")
        lists_f = sem("lists_f")
        lists_turned = sem("lists_turned")
        lists_ready = sem("lists_ready")
        stats_ready = sem("stats_ready")
        srcs_loaded = sems("srcs_loaded", 4)
        place_marks = sem("place_marks")
        taken_done = sem("taken_done")
        taken_copied = sem("taken_copied")
        ranks_done = sem("ranks_done")
        tiles_shifted = sem("tiles_shifted")
        a_marked = sem("a_marked")
        looked_up = sem("looked_up")
        looked_picked = sem("looked_picked")
        looked_summed = sem("looked_summed")
        hots_marked = sem("hots_marked")
        windows0 = sem("windows0")
        ranks_added = sem("ranks_added")
        placed = sem("placed")
        edges_now = sem("edges_now")
        edges_scattered = sems("edges_scattered", 2)
        stats_summed = sem("stats_summed")
        marks_ready = sem("marks_ready")
        pairs_counted = sem("pairs_counted")
        pairs_copied = sem("pairs_copied")
        counts_added = sem("counts_added")
        counts_copied = sem("counts_copied")
        counts_out = sem("counts_out")
        counts_in = sem("counts_in")
        windows_ready = sem("windows_ready")
        edge_cols = sem("edge_cols")
        edge_rows_stored = sem("edge_rows_stored")
        pads_stored = sem("pads_stored")
        g_begun = sems("g_begun", 2)
        g_rows_set = sems("g_rows_set", 2)
        g_rows_out = sems("g_rows_out", 2)
        g_msg_in = sem("g_msg_in")
        g_from_set = sem("g_from_set")
        g_x_in = sem("g_x_in")
        g_cols_set = sems("g_cols_set", 2)
        g_turned = sems("g_turned", 2)
        g_compared = sems("g_compared", 2)
        g_marked = sems("g_marked", 2)
        g_attr_out = sem("g_attr_out")
        g_msg_made = sem("g_msg_made")
        g_combined = sems("g_combined", 2)
        g_again_set = sems("g_again_set", 2)
        g_at_set = sems("g_at_set", 2)
        g_fetched = sems("g_fetched", 2)
        g_added = sems("g_added", 2)
        g_stored = sems("g_stored", 2)
        types_loaded = sems("types_loaded", 4)
        src_placed = sem("src_placed")
        xg_loaded = sems("xg_loaded", 4)
        hot_types = sem("hot_types")
        xg_turned = sem("xg_turned")
        xg_t_ready = sem("xg_t_ready")
        coef_done = sem("coef_done")
        coef_ready = sem("coef_ready")
        products = sem("products")
        half_used = sem("half_used")
        seeds_ready = sem("seeds_ready")
        seeds_added = sem("seeds_added")
        chain1 = sem("chain1")
        msgs_ready = sem("msgs_ready")
        msgs_stored = sems("msgs_stored", 2)
        in2 = sems("in2_", 4)
        hot2 = sem("hot2")
        turned2 = sem("turned2")
        lhs2 = sem("lhs2")
        sum2 = sem("sum2")
        act2 = sem("act2")
        back2 = sem("back2")
        y2 = sem("y2")
        st2_done = sem("st2_done")
        mv2_done = sem("mv2_done")
        sd2_done = sem("sd2_done")
        rstd2_done = sem("rstd2_done")
        norm2 = sem("norm2")
        x1_done = sem("x1_done")
        x1_stored = sems("x1_stored", 2)
        in3 = sems("in3_", 4)
        xg3_loaded = sems("xg3_loaded", 4)
        hot3 = sem("hot3")
        ea3 = sem("ea3")
        ea3_copied = sem("ea3_copied")
        sum3 = sem("sum3")
        lhs3 = sem("lhs3")
        mid3 = sem("mid3")
        act3 = sem("act3")
        o3 = sem("o3")
        o3_copied = sem("o3_copied")
        back3 = sem("back3")
        xb3 = sem("xb3")
        st3a = sem("st3a")
        mv3a = sem("mv3a")
        sd3a = sem("sd3a")
        sd3b = sem("sd3b")
        rstd3a = sem("rstd3a")
        z3 = sem("z3")
        y3 = sem("y3")
        st3b = sem("st3b")
        mv3b = sem("mv3b")
        rstd3b = sem("rstd3b")
        norm3 = sem("norm3")
        out_done = sem("out_done")
        out_stored = sems("out_stored", 2)

        def need(eng, s, value):
            if not (isinstance(value, int) and value <= 0):
                eng.wait_ge(s, value)

        def each(eng, count, more, body):
            peeled = 1 if more <= 2 else 2
            end = (count - 1) // 4
            for i in range(4 * peeled):
                body(i // 4, i % 4)
            with eng.Fori(peeled, end) as k:
                for u in range(4):
                    body(k, u)
            for i in range(4 * end, count + more):
                body(i // 4, i % 4)

        def back(k, u, d):
            return k + (u - d) // 4, (u - d) % 4

        def valid(k, u, count):
            return not isinstance(k, int) or 0 <= 4 * k + u < count

        def node0(k, u):
            return (4 * k + u) * GP

        def last(k, u):
            return isinstance(k, int) and 4 * k + u == NG - 1

        def loaded_count(k, u):
            return 80 * (k + 1) + 16 * last(k, u)

        def rows_and_tiles(dram, tiles, k, u):
            if last(k, u):
                mid = LAST + LAST_T * P
                return [(tiles_of(dram[LAST:mid, :]), tiles[:, 0:LAST_T, :]),
                        (dram[mid:N, :], tiles[0:LAST_R, LAST_T, :])]
            return [(tiles_of(dram[bass.ds(node0(k, u), GP), :]), tiles)]

        def tiles_of(rows):
            return rows.rearrange("(j p) d -> p j d", p=P)

        g_table = (msg_rows, sum_rows)
        g_cols = (MC, D)
        g_base = (EROWS, 0)
        g_keys = (dst_t, src_t)

        def g_tiles(eng, body):
            body(0)
            with eng.Fori(1, ET) as t:
                body(t)

        def g_groups(eng, body):
            body(0)
            with eng.Fori(1, NG) as g:
                body(g)

        block = ctx.enter_context(nc.Block())

        CONSTS = 13

        @block.sync
        def _(sp):
            flat = (QR - 1) * QC
            sp.wait_ge(pads_set, 1)
            for q, a, n in ((dst_q, dst, E), (src_q, src, E), (next_q, dst[1:E], E - 1),
                            (norm_q, edge_weight.rearrange("e o -> (e o)"), E)):
                sp.dma_start(q[0:QR - 1, :], a[0:flat].rearrange("(q c) -> q c", c=QC)).then_inc(lists_loaded, 16)
                sp.dma_start(q[QR - 1:QR, 0:n - flat],
                             a[flat:n].rearrange("(q c) -> q c", q=1)).then_inc(lists_loaded, 16)
            sp.dma_start(basis_sb[:, :, :], basis.rearrange("b d f -> d b f")).then_inc(consts_loaded, 16)
            sp.dma_start(w_comp_sb[:, :], w_comp).then_inc(consts_loaded, 16)
            sp.dma_start(loop_sb[:, :], loop_weight).then_inc(consts_loaded, 16)
            sp.dma_start(we_sb[0:ED, :], We).then_inc(consts_loaded, 16)
            sp.dma_start(we_sb[ED:ED + 1, :], be.rearrange("(o d) -> o d", o=1)).then_inc(consts_loaded, 16)
            sp.dma_start(w1_sb[:, :], W1).then_inc(consts_loaded, 16)
            sp.dma_start(w2_sb[:, :], W2).then_inc(consts_loaded, 16)
            for c, a in ((h_bias_sb, h_bias), (b1_sb, b1), (b2_sb, b2)):
                sp.dma_start(c[:, :], a.rearrange("(d o) -> d o", o=1)).then_inc(consts_loaded, 16)
            for c, a in ((gamma_sb, gamma), (beta_sb, beta), (eps_sb, eps)):
                sp.dma_start(c[:, :], a.partition_broadcast(P)).then_inc(consts_loaded, 16)
            sp.wait_ge(zeroed, 1)
            sp.dma_start(edge_out[:, 0:FULL, 0:ED],
                         edge_attr[0:FULL * P, :].rearrange("(t p) c -> p t c", p=P)).then_inc(attr_loaded, 16)
            sp.dma_start(edge_out[0:REST, FULL, 0:ED], edge_attr[FULL * P:E, :]).then_inc(attr_loaded, 16)

            sp.wait_ge(edge_cols, 1)
            sp.dma_start(edge_rows[E:E + P, :], pad_edges[:, :]).then_inc(pads_stored, 16)
            sp.dma_start(edge_rows[E + P:EROWS, :], pad_edges[0:EROWS - E - P, :]).then_inc(pads_stored, 16)
            sp.wait_ge(counts_copied, 1)
            sp.dma_start(counts_dram.rearrange("l a b -> a l b"), counts_sb[:, :, :]).then_inc(counts_out, 16)
            sp.wait_ge(counts_out, 16)
            sp.dma_start(count_row[:, :, :], counts_dram.rearrange("(o l) a b -> o l (a b)", o=1))\
                .then_inc(counts_in, 16)

            def load_types(k, u):
                i = 4 * k + u
                need(sp, hot_types, i - 3)
                n = E - i * GP if isinstance(i, int) and i == EG - 1 else GP
                e0 = i * GP
                sp.dma_start(types[:, u, 0:n],
                             edge_type[bass.ds(e0, n)].partition_broadcast(R)).then_inc(types_loaded[u], 16)
                need(sp, tiles_shifted, i - 3)
                need(sp, a_marked, i - 3)
                sp.dma_start(srcs[:, u, 0:n],
                             src[bass.ds(e0, n)].partition_broadcast(P)).then_inc(srcs_loaded[u], 16)

            def store_msgs(k, u):
                i = 4 * k + u
                sp.wait_ge(msgs_ready, i + 1)
                sp.dma_start(tiles_of(msg_rows[bass.ds(i * GP, GP), :]), msgs[:, u % 2, :, :])\
                    .then_inc(msgs_stored[u % 2], 16)

            def stage1(k, u):
                if valid(k, u, EG):
                    load_types(k, u)
                if valid(*back(k, u, 2), EG):
                    store_msgs(*back(k, u, 2))
            each(sp, EG, 2, stage1)
            sp.dma_start(msg_rows[EROWS - P:EROWS, :], pad_msgs[:, :]).then_inc(pads_stored, 16)

            sp.wait_ge(windows_ready, 1)
            sp.wait_ge(pads_stored, 48)
            for s in range(2):
                sp.wait_ge(msgs_stored[s], 16 * len(range(s, EG, 2)))

            def general(n):
                def set_rows(g):
                    sp.wait_ge(g_rows_set[n], g + 1)
                    if n == 0:
                        sp.dma_start(tiles_of(msg_rows[bass.ds(EROWS + g * GP, GP), :]), g_rows[:, :, :])\
                            .then_inc(g_rows_out[n], 16)
                    else:
                        sp.dma_start(tiles_of(edge_rows[bass.ds(EROWS + g * GP, GP), :]), g_edges[:, :, :])\
                            .then_inc(g_rows_out[n], 16)
                        sp.dma_start(tiles_of(sum_rows[bass.ds(g * GP, GP), :]), g_rows[:, :, 0:D])\
                            .then_inc(g_rows_out[n], 16)

                def load_msgs(t):
                    need(sp, g_stored[n], 16 * t)
                    sp.dma_start(g_msg[:, :], msg_rows[bass.ds(t * P, P), 0:D]).then_inc(g_msg_in, 16)

                g_groups(sp, set_rows)
                if n == 0:
                    g_tiles(sp, load_msgs)
                sp.wait_ge(g_rows_out[n], 16 * (n + 1) * NG)
                sp.wait_ge(g_stored[n], 16 * ET)

            ok = sp.value_load(ok_i[0:1, 0:1], min_val=0, max_val=1)
            with sp.If(ok < 1):
                general(0)

            def load2(k, u):
                i = 4 * k + u
                need(sp, y2, i - 3)
                for rows, tiles in rows_and_tiles(x, xin[:, u, :, :], k, u):
                    sp.dma_start(tiles, rows).then_inc(in2[u], 16)
                for j in range(T):
                    row = sp.value_load(win_row[0:1, 0, bass.ds(i * T + j, 1)], min_val=0, max_val=EROWS + NT * P - P)
                    sp.dma_start(mwin[:, u, j, :], msg_rows[bass.ds(row, P), :]).then_inc(in2[u], 16)

            each(sp, NG, 0, load2)

            for s in range(2):
                sp.wait_ge(x1_stored[s], 16 * (NG // 2 + s))
                sp.wait_ge(edges_scattered[s], 64 * len(range(s, EG, 2)))

            ok = sp.value_load(ok_i[0:1, 1:2], min_val=0, max_val=1)
            with sp.If(ok < 1):
                general(1)

            def load3(k, u):
                i = 4 * k + u
                need(sp, xb3, i - 3)
                for rows, tiles in rows_and_tiles(x1_rows, xin[:, u, :, :], k, u):
                    sp.dma_start(tiles, rows).then_inc(in3[u], 16)
                for j in range(T):
                    row = sp.value_load(win_row[0:1, 1, bass.ds(i * T + j, 1)], min_val=0, max_val=EROWS + NT * P - P)
                    sp.dma_start(ewin[:, u, j, :], edge_rows[bass.ds(row, P), :]).then_inc(in3[u], 16)

            each(sp, NG, 0, load3)
            for s in range(2):
                sp.wait_ge(out_stored[s], 16 * (NG // 2 + s))

        @block.gpsimd
        def _(pool):
            pool.memset(edge_out[:, FULL:ET + 1, :], 0.0).then_inc(zeroed, 1)
            pool.memset(ident[:, :], 0.0).then_inc(consts_made, 1)
            pool.wait_ge(consts_made, 1)
            pool.affine_select(out=ident[:, :], in_=ident[:, :], compare_op=ALU.not_equal, fill=1.0,
                               base=0, pattern=[[-1, P]], channel_multiplier=1)
            pool.iota(count_up[:, :], pattern=[[1, GP]], base=0, channel_multiplier=0,
                      allow_small_or_imprecise_dtypes=True)
            pool.iota(part_no[:, :], pattern=[[1, 1]], base=0, channel_multiplier=1,
                      allow_small_or_imprecise_dtypes=True)
            pool.iota(group_start[:, :], pattern=[[GP, NG]], base=0, channel_multiplier=0,
                      allow_small_or_imprecise_dtypes=True)
            pool.iota(sums_start[:, :, :], pattern=[[0, 2], [P, NT]], base=EROWS, channel_multiplier=0,
                      allow_small_or_imprecise_dtypes=True)
            pool.iota(g_node0[:, :], pattern=[[P, T]], base=0, channel_multiplier=1,
                      allow_small_or_imprecise_dtypes=True)
            pool.iota(a_from[:, :], pattern=[[1, 1]], base=0, channel_multiplier=32 * P,
                      allow_small_or_imprecise_dtypes=True)
            pool.memset(before[:, :], 0.0)
            pool.memset(pad_edges[:, :], 0.0)
            pool.memset(a_hot[:, :, :, 0:1], 0.0)
            pool.memset(steps_a[:, :], 0.0).then_inc(consts_made, 1)
            pool.wait_ge(consts_made, 2)
            pool.memset(pad_edges[:, ENODE:ENODE + 1], float(NONE))
            pool.affine_select(out=before[:, :], in_=before[:, :], compare_op=ALU.is_ge, fill=1.0,
                               base=0, pattern=[[-1, P]], channel_multiplier=1)
            pool.affine_select(out=steps_a[:, :], in_=steps_a[:, :], compare_op=ALU.not_equal, fill=1.0,
                               base=0, pattern=[[-1, A_OF]], channel_multiplier=1).then_inc(consts_made, 1)
            pool.wait_ge(consts_made, 3)
            pool.affine_select(out=steps_a[:, :], in_=steps_a[:, :], compare_op=ALU.not_equal, fill=-1.0,
                               base=1, pattern=[[-1, A_OF]], channel_multiplier=1)
            pool.memset(ln_eps[:, :], LN_EPS)
            pool.memset(ones_bf[:, :], 1.0)
            pool.memset(ones_col[:, :], 1.0)
            pool.memset(pad_msgs[:, :], 0.0)
            pool.memset(edge_out[:, :, ONE:ONE + 1], 1.0)
            pool.memset(edge_out[:, :, EC - 1:EC], 0.0)
            pool.memset(msgs[:, :, :, DCOL:MC], 0.0).then_inc(consts_made, 1)
            pool.wait_ge(lists_ready, 1)

            def sources1(k, u):
                i = 4 * k + u
                need(pool, xg_turned, i - 3)
                pool.tensor_copy(src_now[:, u, :], src_row[:, bass.ds(i * T, T)]).then_inc(src_placed, 1)
                pool.wait_ge(src_placed, i + 1)
                pool.sem_inc(wait_passed, 1)

            def gather1(u, j):
                pool.indirect_dma_start(
                    out=xg[:, u, j, :], out_offset=None, in_=x,
                    in_offset=bass.IndirectOffsetOnAxis(ap=src_now[:, u, j:j + 1], axis=0),
                ).then_inc(xg_loaded[u], 16)

            def stage1(k, u):
                if valid(k, u, EG):
                    sources1(k, u)
                for j in range(T):
                    if valid(k, u, EG):
                        gather1(u, j)
                    pk, pu = back(k, u, 2)
                    if valid(pk, pu, EG):
                        t = (4 * pk + pu) * T + j
                        pool.wait_ge(seeds_ready, t + 1)
                        if isinstance(t, int) and t < 2:
                            pass
                        elif j % 2 == 0:
                            pool.wait_ge(chain1, (t // 2 if isinstance(t, int) else (4 * pk + pu) * 2 + j // 2) * 12)
                        pool.tensor_tensor(seed_sum[:, j % 2, :], seeds[:, j % 2, 0, :], seeds[:, j % 2, 1, :],
                                           ALU.add).then_inc(seeds_added, 1)

            each(pool, EG, 2, stage1)

            def general(n):
                def tile(t):
                    if n == 1:
                        need(pool, g_stored[n], 16 * t)
                        pool.tensor_copy(g_from[:, :], edge_out[:, bass.ds(t, 1), EFROM].bitcast(i32))\
                            .then_inc(g_from_set, 1)
                        pool.wait_ge(g_from_set, t + 1)
                        pool.sem_inc(wait_passed, 1)
                        pool.indirect_dma_start(
                            out=g_x[:, :], out_offset=None, in_=x1_rows,
                            in_offset=bass.IndirectOffsetOnAxis(ap=g_from[:, :], axis=0)).then_inc(g_x_in, 16)
                    pool.wait_ge(g_at_set[n], t + 1)
                    pool.sem_inc(wait_passed, 1)
                    pool.indirect_dma_start(
                        out=g_sum[:, 0:g_cols[n]], out_offset=None, in_=g_table[n],
                        in_offset=bass.IndirectOffsetOnAxis(ap=g_at[:, :], axis=0),
                        bounds_check=g_base[n] + N - 1, oob_is_err=False).then_inc(g_fetched[n], 16)
                    pool.wait_ge(g_added[n], t + 1)
                    pool.sem_inc(wait_passed, 1)
                    pool.indirect_dma_start(
                        out=g_table[n], out_offset=bass.IndirectOffsetOnAxis(ap=g_at[:, :], axis=0),
                        in_=g_sum[:, 0:g_cols[n]], in_offset=None,
                        bounds_check=g_base[n] + N - 1, oob_is_err=False).then_inc(g_stored[n], 16)
                    pool.wait_ge(g_stored[n], 16 * (t + 1))
                    pool.sem_inc(wait_passed, 1)

                pool.wait_ge(g_rows_out[n], 16 * (n + 1) * NG)
                if n == 0:
                    for s in range(2):
                        pool.wait_ge(msgs_stored[s], 16 * len(range(s, EG, 2)))
                    pool.wait_ge(pads_stored, 48)
                g_tiles(pool, tile)

            pool.wait_ge(windows_ready, 1)
            ok = pool.value_load(ok_i[0:1, 0:1], min_val=0, max_val=1)
            with pool.If(ok < 1):
                general(0)

            pool.wait_ge(edge_cols, 1)

            def scatter2(k, u):
                i = 4 * k + u
                s = u % 2
                if valid(*back(k, u, 2), EG):
                    pool.wait_ge(edges_scattered[s], 64 * (2 * k + u // 2))
                pool.wait_ge(placed, i + 1)
                pool.tensor_copy(edge_now[:, s, :, :], edge_out[:, bass.ds(i * T, T), :])
                pool.tensor_copy(place_now[:, s, :], place_t[:, bass.ds(i * T, T)]).then_inc(edges_now, 1)
                pool.wait_ge(edges_now, i + 1)
                pool.sem_inc(wait_passed, 1)
                for j in range(T):
                    pool.indirect_dma_start(
                        out=edge_rows, out_offset=bass.IndirectOffsetOnAxis(ap=place_now[:, s, j:j + 1], axis=0),
                        in_=edge_now[:, s, j, :], in_offset=None, bounds_check=E - 1, oob_is_err=False,
                    ).then_inc(edges_scattered[s], 16)

            each(pool, EG, 0, scatter2)
            for s in range(2):
                pool.wait_ge(x1_stored[s], 16 * (NG // 2 + s))

            ok1 = pool.value_load(ok_i[0:1, 1:2], min_val=0, max_val=1)
            with pool.If(ok1 < 1):
                general(1)

            def gather3(k, u):
                i = 4 * k + u
                need(pool, sum3, i - 3)
                pool.wait_ge(in3[u], loaded_count(k, u))
                pool.sem_inc(wait_passed, 1)
                with pool.If(ok1 < 1):
                    pool.dma_start(xg[:, u, :, :], tiles_of(sum_rows[bass.ds(node0(k, u), GP), :]))\
                        .then_inc(xg3_loaded[u], 64)
                with pool.Else():
                    for j in range(T):
                        pool.indirect_dma_start(
                            out=xg[:, u, j, :], out_offset=None, in_=x1_rows,
                            in_offset=bass.IndirectOffsetOnAxis(ap=ewin[:, u, j, EFROM:EFROM + 1].bitcast(i32),
                                                                axis=0)).then_inc(xg3_loaded[u], 16)

            each(pool, NG, 0, gather3)

        @block.vector
        def _(dve):
            steps = [0]

            def link(ins):
                steps[0] += 1
                ins.then_inc(dve0, 1)
                dve.wait_ge(dve0, steps[0])

            dve.memset(dst_q[96:QR, :], NONE)
            dve.memset(next_q[96:QR, :], NONE)
            dve.memset(src_q[96:QR, :], NONE)
            dve.memset(norm_q[96:QR, :], 0.0).then_inc(pads_set, 1)
            dve.wait_ge(lists_loaded, 16 * 8)
            dve.wait_ge(pads_set, 1)
            dve.tensor_copy(dst_qf[:, :], dst_q[:, :])
            dve.tensor_copy(src_qf[:, :], src_q[:, :]).then_inc(lists_f, 1)
            dve.tensor_copy(next_qf[:, :], next_q[:, :])
            dve.wait_ge(lists_turned, 1)
            for b, dest in enumerate((dst_t, src_t, norm_t)):
                dve.tensor_copy(dest[:, 0:ET].rearrange("p (q h) -> p q h", h=2),
                                bank[b][:, 0:ET].rearrange("p (h q) -> p q h", h=2))
            dve.memset(dst_t[:, ET:ET + 1], float(NONE))
            link(dve.memset(src_t[:, ET:ET + 1], float(NONE)))
            dve.tensor_scalar(src_row[:, :], src_t[:, 0:ET], float(N - 1), None, ALU.min)
            link(dve.tensor_scalar(dst_row[:, :], dst_t[:, :], float(N - 1), None, ALU.min))
            dve.tensor_scalar(skip_t[:, :], src_t[:, 0:ET], float(N), float(SKIP), ALU.is_ge, ALU.mult)\
                .then_inc(lists_ready, 1)
            dve.wait_ge(consts_made, 4)
            dve.tensor_copy(edge_out[:, :, ENODE:ENODE + 1], src_t[:, :].unsqueeze(2))
            dve.tensor_copy(edge_out[:, :, EFROM:EFROM + 1].bitcast(i32), dst_row[:, :].unsqueeze(2))
            dve.wait_ge(attr_loaded, 32)
            dve.wait_ge(consts_loaded, 16 * CONSTS)
            link(dve.tensor_scalar(eps1_sb[:, :], eps_sb[:, :], 1.0, None, ALU.add))
            dve.tensor_scalar(self_diag[:, :], ident[:, :], eps1_sb[:, 0:1], None, ALU.mult).then_inc(edge_cols, 1)
            link(dve.tensor_tensor(falls_q[:, :], dst_qf[:, :], next_qf[:, :], ALU.is_gt))
            dve.tensor_reduce(stat_q[:, :], falls_q[:, :], AX.X, ALU.add).then_inc(stats_ready, 1)
            dve.tensor_copy(node_i[:, 0, :], dst_t[:, 0:ET])
            link(dve.tensor_copy(node_i[:, 1, :], src_t[:, 0:ET]))
            dve.tensor_scalar(a_i[:, :, :], node_i[:, :, :], 12, None, ALU.logical_shift_right)
            link(dve.tensor_scalar(b_i[:, :, :], node_i[:, :, :], 7, None, ALU.logical_shift_right))
            link(dve.tensor_scalar(b_m[:, :, :], b_i[:, :, :], 31, None, ALU.bitwise_and))
            dve.tensor_copy(tile_f[:, :], b_i[:, 1, :])
            dve.tensor_copy(a_f[:, :, :], a_i[:, :, :])
            link(dve.tensor_copy(b_f[:, :, :], b_m[:, :, :]))
            ca = count_up[:, 0:A_OF].unsqueeze(1).to_broadcast([P, ET, A_OF])
            cb = count_up[:, 0:32].unsqueeze(1).to_broadcast([P, ET, 32])
            for n in range(2):
                av = a_f[:, n, :].unsqueeze(2).to_broadcast([P, ET, A_OF])
                bv = b_f[:, n, :].unsqueeze(2).to_broadcast([P, ET, 32])
                dve.tensor_tensor(a_eq[:, n, :].rearrange("p (t a) -> p t a", a=A_OF), av, ca, ALU.is_equal)
                dve.tensor_tensor(a_lt[:, n, :].rearrange("p (t a) -> p t a", a=A_OF), av, ca, ALU.is_lt)
                dve.tensor_tensor(b_lt[:, n, :].rearrange("p (t b) -> p t b", b=32), bv, cb, ALU.is_lt)\
                    .then_inc(marks_ready, 1)
            for n in range(2):
                dve.wait_ge(pairs_counted, n + 1)
                dve.tensor_copy(pairs_sb[:, n, :], bank[3 + n][0:CH * A_OF, 0:CH * 32]).then_inc(pairs_copied, 1)
            dve.wait_ge(counts_added, 1)
            dve.tensor_copy(counts_sb[:, :, :], bank[5][0:A_OF, 0:64].rearrange("a (l b) -> a l b", b=32))\
                .then_inc(counts_copied, 1)
            dve.wait_ge(stats_summed, 1)
            dve.tensor_copy(stat_row[:, :], bank[6][0:1, 0:1])
            dve.wait_ge(taken_done, 1)
            dve.tensor_copy(taken[:, 1, T, :], bank[7][0:A_OF, 0:32]).then_inc(taken_copied, 1)

            def stage1(k, u):
                if valid(k, u, EG):
                    i = 4 * k + u
                    s = u % 2
                    dve.wait_ge(types_loaded[u], 16 * (k + 1))
                    need(dve, coef_done, i - 1)
                    dve.tensor_scalar(type_hot[:, s, :], types[:, u, :], part_no[0:R, 0:1], None,
                                      ALU.is_equal).then_inc(hot_types, 1)
                    dve.wait_ge(srcs_loaded[u], 16 * (k + 1))
                    need(dve, looked_up, i - 1)
                    dve.tensor_scalar(tiles_bc[:, s, :], srcs[:, u, :], 7, None, ALU.logical_shift_right)\
                        .then_inc(tiles_shifted, 1)
                    dve.tensor_scalar(a_ge[:, s, :], srcs[0:A_OF, u, :], a_from[:, 0:1], None, ALU.is_ge)\
                        .then_inc(a_marked, 1)
                    dve.tensor_tensor(a_hot[:, s, :, 1:A_OF + 1],
                                      a_f[:, 1, bass.ds(i * T, T)].unsqueeze(2).to_broadcast([P, T, A_OF]),
                                      count_up[:, 0:A_OF].unsqueeze(1).to_broadcast([P, T, A_OF]), ALU.is_equal)
                    dve.tensor_tensor(b_hot[:, u, :, :],
                                      b_f[:, 1, bass.ds(i * T, T)].unsqueeze(2).to_broadcast([P, T, 32]),
                                      count_up[:, 0:32].unsqueeze(1).to_broadcast([P, T, 32]), ALU.is_equal)\
                        .then_inc(hots_marked, 1)
                    dve.tensor_tensor(b_bf[:, s, :, :],
                                      b_f[:, 1, bass.ds(i * T, T)].unsqueeze(2).to_broadcast([P, T, 32]),
                                      count_up[:, 0:32].unsqueeze(1).to_broadcast([P, T, 32]), ALU.is_equal)
                    dve.wait_ge(tiles_shifted, i + 1)
                    for j in range(T):
                        dve.scalar_tensor_tensor(
                            out=same_tile[:, s, j, :], in0=tiles_bc[:, s, j * P:(j + 1) * P],
                            scalar=tile_f[:, bass.ds(i * T + j, 1)], in1=before[:, :],
                            op0=ALU.is_equal, op1=ALU.mult)
                    dve.wait_ge(hots_marked, i + 1)
                    dve.tensor_tensor(a_step[:, s, :, :], a_hot[:, s, :, 1:A_OF + 1], a_hot[:, s, :, 0:A_OF],
                                      ALU.subtract).then_inc(place_marks, 1)
                pk, pu = back(k, u, 2)
                if valid(pk, pu, EG):
                    i = 4 * pk + pu
                    s = pu % 2
                    dve.wait_ge(looked_up, i + 1)
                    dve.tensor_tensor(looked[:, s, :, :], b_hot[:, pu, :, :],
                                      bank[7][:, P:P + 32 * T].rearrange("p (t b) -> p t b", b=32), ALU.mult)\
                        .then_inc(looked_picked, 1)
                    dve.wait_ge(looked_picked, i + 1)
                    dve.tensor_reduce(place_s[:, s, :], looked[:, s, :, :], AX.X, ALU.add).then_inc(looked_summed, 1)
                    dve.wait_ge(looked_summed, i + 1)
                    dve.tensor_tensor(place_f[:, s, :], place_s[:, s, :], skip_t[:, bass.ds(i * T, T)], ALU.add)\
                        .then_inc(ranks_added, 1)
                    dve.wait_ge(ranks_added, i + 1)
                    dve.tensor_tensor(place_t[:, bass.ds(i * T, T)], place_f[:, s, :], bank[7][:, 64:64 + T],
                                      ALU.add).then_inc(placed, 1)
                    dve.wait_ge(coef_ready, i + 1)
                    if valid(*back(pk, pu, 2), EG):
                        dve.wait_ge(msgs_stored[s], 16 * (2 * pk + pu // 2))
                    dve.tensor_copy(msgs[:, s, :, DCOL:DCOL + 1], dst_t[:, bass.ds(i * T, T)].unsqueeze(2))
                    for h in range(2):
                        pair = 2 * i + h
                        for b in range(SEED, B):
                            for w in range(2):
                                j = 2 * h + w
                                n = 2 * (b - SEED) + w
                                if b == SEED:
                                    dve.wait_ge(seeds_added, i * T + j + 1)
                                if b == 4:
                                    dve.wait_ge(products, 4 * pair + 3 + w)
                                if b > SEED:
                                    dve.wait_ge(chain1, 12 * pair + n - 1)
                                ins = dve.scalar_tensor_tensor(
                                    out=msgs[:, s, j, 0:D],
                                    in0=bank[w + 2 * (b // 4)][:, (b % 4) * D:(b % 4 + 1) * D],
                                    scalar=coef[:, s, j, b:b + 1],
                                    in1=seed_sum[:, w, :] if b == SEED else msgs[:, s, j, 0:D],
                                    op0=ALU.mult, op1=ALU.add).then_inc(chain1, 1)
                    dve.wait_ge(chain1, 12 * (2 * i + 2))
                    dve.sem_inc(msgs_ready, 1)
                if valid(k, u, EG):
                    i = 4 * k + u
                    s = u % 2
                    dve.wait_ge(coef_done, i + 1)
                    dve.tensor_tensor(coef[:, s, :, :], bank[5][:, 0:T * B].rearrange("p (t b) -> p t b", b=B),
                                      norm_t[:, bass.ds(i * T, T)].unsqueeze(2).to_broadcast([P, T, B]),
                                      ALU.mult).then_inc(coef_ready, 1)

            each(dve, EG, 2, stage1)

            dve.wait_ge(counts_in, 16)
            wsteps = [0]

            def wlink(ins):
                wsteps[0] += 1
                ins.then_inc(windows0, 1)
                dve.wait_ge(windows0, wsteps[0])

            wlink(dve.tensor_tensor(win_d[:, :, :], count_row[:, :, 1:NT + 1], count_row[:, :, 0:NT], ALU.subtract))
            dve.tensor_scalar(no_falls[:, :], stat_row[:, :], 0.0, None, ALU.is_equal)
            wlink(dve.tensor_reduce(most[:, :], win_d[:, :, :], AX.X, ALU.max))
            wlink(dve.tensor_scalar(fits[:, :], most[:, :], float(P), None, ALU.is_le))
            wlink(dve.tensor_tensor(fits[:, 0:1], fits[:, 0:1], no_falls[:, :], ALU.mult))
            dve.tensor_copy(ok_i[:, :], fits[:, :])
            wlink(dve.tensor_tensor(win_d[:, :, :], count_row[:, :, 0:NT], sums_start[:, :, :], ALU.subtract))
            for n in range(2):
                ins = dve.scalar_tensor_tensor(out=win_g[:, n, :], in0=win_d[:, n, :], scalar=fits[:, n:n + 1],
                                               in1=sums_start[:, n, :], op0=ALU.mult, op1=ALU.add)
            wlink(ins)
            dve.tensor_copy(win_row[:, :, :], win_g[:, :, :]).then_inc(windows_ready, 1)

            def general(n):
                b_key, b_attr, b_msg, b_sum, b_count = bank[0:5]
                if n == 1:
                    for s in range(2):
                        dve.wait_ge(x1_stored[s], 16 * (NG // 2 + s))

                def set_rows(g):
                    need(dve, g_rows_out[n], 16 * (n + 1) * g)
                    of, c = (g_rows, DCOL) if n == 0 else (g_edges, ENODE)
                    dve.tensor_scalar(of[:, :, c:c + 1], g_node0[:, :].unsqueeze(2),
                                      group_start[:, bass.ds(g, 1)], None, ALU.add).then_inc(g_rows_set[n], 1)

                def tile(t):
                    need(dve, g_stored[n], 16 * t)
                    dve.tensor_copy(g_key[:, :], g_keys[n][:, bass.ds(t, 1)])
                    if n == 1:
                        dve.tensor_copy(g_attr[:, :], edge_out[:, bass.ds(t, 1), 0:ED + 1].rearrange("p o c -> p (o c)"))
                    dve.tensor_copy(g_key_wide[:, :], g_keys[n][:, bass.ds(t, 1)].to_broadcast([P, P]))\
                        .then_inc(g_cols_set[n], 1)
                    dve.wait_ge(g_turned[n], t + 1)
                    if n == 1:
                        dve.tensor_copy(g_attr_t[:, :], b_attr[0:ED + 1, 0:P])
                    dve.tensor_scalar(g_same[:, :], b_key[:, 0:P], g_key[:, 0:1], None, ALU.is_equal)\
                        .then_inc(g_compared[n], 1)
                    dve.wait_ge(g_compared[n], t + 1)
                    dve.tensor_tensor(g_earlier[:, :], g_same[:, :], before[:, :], ALU.mult).then_inc(g_marked[n], 1)
                    if n == 1:
                        dve.wait_ge(g_attr_out, t + 1)
                        dve.wait_ge(g_x_in, 16 * (t + 1))
                        dve.tensor_tensor(g_msg[:, :], g_x[:, :], b_msg[:, 0:D], ALU.add).then_inc(g_msg_made, 1)
                    dve.wait_ge(g_combined[n], t + 1)
                    dve.tensor_scalar(g_again[:, :], b_count[:, 0:1], 0.0, float(SKIP), ALU.is_gt, ALU.mult)\
                        .then_inc(g_again_set[n], 1)
                    dve.wait_ge(g_again_set[n], t + 1)
                    dve.scalar_tensor_tensor(out=g_at[:, :], in0=g_again[:, :], scalar=float(g_base[n]),
                                             in1=g_key[:, :], op0=ALU.add, op1=ALU.add).then_inc(g_at_set[n], 1)
                    dve.wait_ge(g_fetched[n], 16 * (t + 1))
                    dve.tensor_tensor(g_sum[:, 0:D], g_sum[:, 0:D], b_sum[:, 0:D], ALU.add).then_inc(g_added[n], 1)

                dve.memset(g_rows[:, :, :], 0.0)
                dve.memset(g_edges[:, :, :], 0.0)
                dve.memset(g_sum[:, :], 0.0).then_inc(g_begun[n], 1)
                dve.wait_ge(g_begun[n], 1)
                g_groups(dve, set_rows)
                g_tiles(dve, tile)
                dve.wait_ge(g_stored[n], 16 * ET)

            dve.wait_ge(windows_ready, 1)
            ok = dve.value_load(ok_i[0:1, 0:1], min_val=0, max_val=1)
            with dve.If(ok < 1):
                general(0)

            def make_hot(i, k, u, loaded, used, dcol, win, done):
                dve.wait_ge(loaded[u], loaded_count(k, u))
                need(dve, used, i - 1)
                dve.scalar_tensor_tensor(
                    out=hot[:, u % 2, :, :], in0=count_up[:, :].rearrange("p (t n) -> p t n", n=P),
                    scalar=group_start[:, bass.ds(i, 1)],
                    in1=win[:, u, :, dcol:dcol + 1].to_broadcast([P, T, P]),
                    op0=ALU.add, op1=ALU.is_equal).then_inc(done, 1)

            def stage2(k, u):
                if valid(k, u, NG):
                    make_hot(4 * k + u, k, u, in2, sum2, DCOL, mwin, hot2)
                pk, pu = back(k, u, 3)
                if valid(pk, pu, NG):
                    i = 4 * pk + pu
                    s = pu % 2
                    dve.wait_ge(sd2_done, i + 1)
                    dve.reciprocal(rstd[:, s, :], sd[:, s, :]).then_inc(rstd2_done, 1)
                    dve.wait_ge(rstd2_done, i + 1)
                    dve.scalar_tensor_tensor(out=shift[:, s, :].unsqueeze(2), in0=mv[:, s, :, 0:1], scalar=-1.0,
                                             in1=rstd[:, s, :].unsqueeze(2), op0=ALU.mult, op1=ALU.mult)\
                        .then_inc(norm2, 1)
                pk, pu = back(k, u, 2)
                if valid(pk, pu, NG):
                    i = 4 * pk + pu
                    s = pu % 2
                    dve.wait_ge(back2, i + 1)
                    need(dve, x1_done, i - 1)
                    dve.tensor_tensor(y[:, s, :, :], xin[:, pu, :, :],
                                      bank[4 + s][:, :].rearrange("p (t d) -> p t d", d=D), ALU.add).then_inc(y2, 1)
                    dve.wait_ge(y2, i + 1)
                    for j in range(T):
                        ins = dve.bn_stats(st[:, s, j, :], y[:, s, j, :])
                    ins.then_inc(st2_done, 1)
                    dve.wait_ge(st2_done, i + 1)
                    dve.sem_inc(wait_passed, 1)
                    for j in range(T):
                        ins = dve.bn_aggr(mv[:, s, j, :], st[:, s, j, :])
                    ins.then_inc(mv2_done, 1)

            each(dve, NG, 3, stage2)

            ok1 = dve.value_load(ok_i[0:1, 1:2], min_val=0, max_val=1)
            with dve.If(ok1 < 1):
                general(1)

            def stage3(k, u):
                if valid(k, u, NG):
                    make_hot(4 * k + u, k, u, in3, sum3, ENODE, ewin, hot3)
                pk, pu = back(k, u, 5)
                if valid(pk, pu, NG):
                    i = 4 * pk + pu
                    s = pu % 2
                    dve.wait_ge(sd3b, i + 1)
                    dve.reciprocal(rstd[:, s, :], sd2[:, s, :]).then_inc(rstd3b, 1)
                    dve.wait_ge(rstd3b, i + 1)
                    dve.scalar_tensor_tensor(out=shift[:, s, :].unsqueeze(2), in0=mv2[:, s, :, 0:1], scalar=-1.0,
                                             in1=rstd[:, s, :].unsqueeze(2), op0=ALU.mult, op1=ALU.mult)\
                        .then_inc(norm3, 1)
                pk, pu = back(k, u, 4)
                if valid(pk, pu, NG):
                    i = 4 * pk + pu
                    s = pu % 2
                    dve.wait_ge(sd3a, i + 1)
                    dve.reciprocal(rstd2[:, s, :], sd[:, s, :]).then_inc(rstd3a, 1)
                    dve.wait_ge(rstd3a, i + 1)
                    need(dve, out_done, i - 1)
                    for j in range(T):
                        ins = dve.scalar_tensor_tensor(out=y[:, s, j, :], in0=z[:, s, j, :],
                                                       scalar=rstd2[:, s, j:j + 1], in1=xb[:, s, j, :],
                                                       op0=ALU.mult, op1=ALU.add)
                    ins.then_inc(y3, 1)
                    dve.wait_ge(y3, i + 1)
                    for j in range(T):
                        ins = dve.bn_stats(st2[:, s, j, :], y[:, s, j, :])
                    ins.then_inc(st3b, 1)
                    dve.wait_ge(st3b, i + 1)
                    dve.sem_inc(wait_passed, 1)
                    for j in range(T):
                        ins = dve.bn_aggr(mv2[:, s, j, :], st2[:, s, j, :])
                    ins.then_inc(mv3b, 1)
                pk, pu = back(k, u, 3)
                if valid(pk, pu, NG):
                    i = 4 * pk + pu
                    s = pu % 2
                    b = bank[6 + s]
                    dve.wait_ge(back3, i + 1)
                    dve.tensor_tensor(xb[:, s, :, :], xin[:, pu, :, :],
                                      beta_sb[:, :].unsqueeze(1).to_broadcast([P, T, D]), ALU.add).then_inc(xb3, 1)
                    for j in range(T):
                        ins = dve.bn_stats(st[:, s, j, :], b[:, j * D:(j + 1) * D])
                    ins.then_inc(st3a, 1)
                    dve.wait_ge(st3a, i + 1)
                    dve.sem_inc(wait_passed, 1)
                    for j in range(T):
                        ins = dve.bn_aggr(mv[:, s, j, :], st[:, s, j, :])
                    ins.then_inc(mv3a, 1)
                    dve.wait_ge(mv3a, i + 1)
                    for j in range(T):
                        ins = dve.scalar_tensor_tensor(out=z[:, s, j, :], in0=b[:, j * D:(j + 1) * D],
                                                       scalar=mv[:, s, j, 0:1], in1=gamma_sb[:, :],
                                                       op0=ALU.subtract, op1=ALU.mult)
                    ins.then_inc(z3, 1)

            each(dve, NG, 5, stage3)

        @block.tensor
        def _(pe):
            pe.wait_ge(consts_made, 4)
            pe.wait_ge(lists_f, 1)
            for b, q in enumerate((dst_qf, src_qf, norm_q)):
                for h in range(2):
                    ins = pe.transpose(bank[b][:, h * QR:(h + 1) * QR], q[:, h * P:(h + 1) * P],
                                       ident[0:QR, 0:QR])
            ins.then_inc(lists_turned, 1)
            pe.wait_ge(stats_ready, 1)
            pe.matmul(bank[6][0:1, 0:1], ones_col[0:QR, :], stat_q[:, :], start=True, stop=True)\
                .then_inc(stats_summed, 1)
            for n in range(2):
                pe.wait_ge(marks_ready, n + 1)
                for c in range(NCH):
                    ca = slice(c * CH * A_OF, (c + 1) * CH * A_OF)
                    pe.matmul(bank[3 + n][0:CH * A_OF, 0:CH * 32], a_lt[:, n, ca], ones_bf[:, :],
                              start=(c == 0), stop=False)
                    ins = pe.matmul(bank[3 + n][0:CH * A_OF, 0:CH * 32], a_eq[:, n, ca],
                                    b_lt[:, n, c * CH * 32:(c + 1) * CH * 32], start=False, stop=(c == NCH - 1))
                ins.then_inc(pairs_counted, 1)
            for n in range(2):
                pe.wait_ge(pairs_copied, n + 1)
                for c in range(CH):
                    ins = pe.matmul(bank[5][0:A_OF, n * 32:(n + 1) * 32],
                                    ident[0:CH * A_OF, c * A_OF:(c + 1) * A_OF],
                                    pairs_sb[:, n, c * 32:(c + 1) * 32], start=(c == 0), stop=(c == CH - 1))
            ins.then_inc(counts_added, 1)
            pe.wait_ge(counts_copied, 1)
            pe.matmul(bank[7][0:A_OF, 0:32], steps_a[:, :], counts_sb[:, 1, :], start=True, stop=True)\
                .then_inc(taken_done, 1)
            pe.wait_ge(consts_loaded, 16 * CONSTS)

            def stage1(k, u):
                i = 4 * k + u
                s = u % 2
                if valid(k, u, EG):
                    pe.wait_ge(xg_loaded[u], 64 * (k + 1))
                    need(pe, xg_t_ready, i)
                    for j in range(T):
                        ins = pe.transpose(bank[4][:, j * P:(j + 1) * P], xg[:, u, j, :], ident[:, :])
                    ins.then_inc(xg_turned, 1)
                    pe.wait_ge(hot_types, i + 1)
                    pe.wait_ge(place_marks, i + 1)
                    pe.wait_ge(taken_copied, i + 1)
                    need(pe, coef_ready, i)
                    for j in range(T):
                        ins = pe.matmul(bank[5][:, j * B:(j + 1) * B], type_hot[:, s, j * P:(j + 1) * P],
                                        w_comp_sb[:, :], start=True, stop=True)
                    ins.then_inc(coef_done, 1)
                    for j in range(T + 1):
                        part = bank[6][0:A_OF, 256 + 32 * j:256 + 32 * (j + 1)]
                        ins = pe.matmul(part, ident[0:A_OF, 0:A_OF], taken[:, 1 - s, T, :],
                                        start=True, stop=(j == 0))
                        for m in range(j):
                            ins = pe.matmul(part, a_step[:, s, m, :], b_bf[:, s, m, :],
                                            start=False, stop=(m == j - 1))
                    ins.then_inc(taken_done, 1)
                pk, pu = back(k, u, 1)
                if valid(pk, pu, EG):
                    i = 4 * pk + pu
                    s = pu % 2
                    pe.wait_ge(taken_copied, i + 2)
                    need(pe, placed, i)
                    for j in range(T):
                        pe.matmul(bank[7][:, 64 + j:65 + j], same_tile[:, s, j, :], ones_bf[:, 0:1],
                                  start=True, stop=True)
                        ins = pe.matmul(bank[7][:, P + 32 * j:P + 32 * (j + 1)],
                                        a_ge[:, s, j * P:(j + 1) * P], taken[:, s, j, :], start=True, stop=True)
                    ins.then_inc(looked_up, 1)
                    pe.wait_ge(xg_t_ready, i + 1)
                    for h in range(2):
                        pair = 2 * i + h
                        for half in range(2):
                            for w in range(2):
                                j = 2 * h + w
                                need(pe, chain1, 12 * (pair - 1) + (2 * (4 - SEED) if half == 0 else 12)
                                     - (1 - w))
                                pe.matmul(bank[w + 2 * half][:, :], xg_t[:, s, j * P:(j + 1) * P],
                                          basis_sb[:, 4 * half:4 * half + 4, :], start=True, stop=True)\
                                    .then_inc(products, 1)

            each(pe, EG, 1, stage1)

            def general(n):
                b_key, b_attr, b_msg, b_sum, b_count = bank[0:5]

                def tile(t):
                    pe.wait_ge(g_cols_set[n], t + 1)
                    need(pe, g_added[n], t)
                    ins = pe.transpose(b_key[:, 0:P], g_key_wide[:, :], ident[:, :])
                    if n == 1:
                        ins = pe.transpose(b_attr[0:ED + 1, 0:P], g_attr[:, :], ident[:, :])
                    ins.then_inc(g_turned[n], 1)
                    pe.wait_ge(g_marked[n], t + 1)
                    if n == 1:
                        pe.matmul(b_msg[:, 0:D], g_attr_t[:, :], we_sb[:, :], start=True, stop=True)\
                            .then_inc(g_attr_out, 1)
                        pe.wait_ge(g_msg_made, t + 1)
                    else:
                        pe.wait_ge(g_msg_in, 16 * (t + 1))
                    pe.matmul(b_sum[:, 0:D], g_same[:, :], g_msg[:, :], start=True, stop=True)
                    pe.matmul(b_count[:, 0:1], g_earlier[:, :], ones_col[:, :], start=True, stop=True)\
                        .then_inc(g_combined[n], 1)

                g_tiles(pe, tile)
                pe.wait_ge(g_added[n], ET)

            pe.wait_ge(windows_ready, 1)
            ok = pe.value_load(ok_i[0:1, 0:1], min_val=0, max_val=1)
            with pe.If(ok < 1):
                general(0)

            def stage2(k, u):
                i = 4 * k + u
                s = u % 2
                if valid(k, u, NG):
                    pe.wait_ge(in2[u], loaded_count(k, u))
                    need(pe, lhs2, i - 1)
                    for j in range(T):
                        ins = pe.transpose(bank[0 + s][:, j * P:(j + 1) * P], xin[:, u, j, :], ident[:, :])
                    ins.then_inc(turned2, 1)
                pk, pu = back(k, u, 1)
                if valid(pk, pu, NG):
                    i = 4 * pk + pu
                    s = pu % 2
                    pe.wait_ge(lhs2, i + 1)
                    need(pe, act2, i - 1)
                    pe.matmul(bank[2 + s][:, :], loop_sb[:, :], lhs_t[:, s, :], start=True, stop=False,
                              skip_group_check=True)
                    pe.wait_ge(hot2, i + 1)
                    for j in range(T):
                        ins = pe.matmul(bank[2 + s][:, j * P:(j + 1) * P], mwin[:, pu, j, 0:D], hot[:, s, j, :],
                                        start=False, stop=(j == T - 1), skip_group_check=True)
                    ins.then_inc(sum2, 1)
                pk, pu = back(k, u, 2)
                if valid(pk, pu, NG):
                    i = 4 * pk + pu
                    s = pu % 2
                    pe.wait_ge(act2, i + 1)
                    need(pe, y2, i - 1)
                    for j in range(T):
                        ins = pe.transpose(bank[4 + s][:, j * P:(j + 1) * P], act_t[:, s, j * P:(j + 1) * P],
                                           ident[:, :])
                    ins.then_inc(back2, 1)

            each(pe, NG, 2, stage2)

            ok1 = pe.value_load(ok_i[0:1, 1:2], min_val=0, max_val=1)
            with pe.If(ok1 < 1):
                general(1)

            def stage3(k, u):
                i = 4 * k + u
                s = u % 2
                if valid(k, u, NG):
                    pe.wait_ge(hot3, i + 1)
                    need(pe, ea3_copied, i)
                    for j in range(T):
                        ins = pe.matmul(bank[2][0:ED + 1, j * P:(j + 1) * P], ewin[:, u, j, 0:ED + 1],
                                        hot[:, s, j, :], start=True, stop=True)
                    ins.then_inc(ea3, 1)
                pk, pu = back(k, u, 1)
                if valid(pk, pu, NG):
                    pi = 4 * pk + pu
                    ps = pu % 2
                    pe.wait_ge(lhs3, pi + 1)
                    need(pe, act3, pi - 1)
                    pe.matmul(bank[3 + ps][:, :], w1_sb[:, :], lhs_t[:, ps, :], start=True, stop=True)\
                        .then_inc(mid3, 1)
                if valid(k, u, NG):
                    pe.wait_ge(ea3_copied, i + 1)
                    need(pe, lhs3, i - 1)
                    pe.matmul(bank[0 + s][:, :], we_sb[:, :], ea_t[:, s, :], start=True, stop=False,
                              skip_group_check=True)
                    for j in range(T):
                        pe.matmul(bank[0 + s][:, j * P:(j + 1) * P], xin[:, u, j, :], self_diag[:, :],
                                  start=False, stop=False, skip_group_check=True)
                    pe.wait_ge(xg3_loaded[u], 64 * (k + 1))
                    for j in range(T):
                        ins = pe.matmul(bank[0 + s][:, j * P:(j + 1) * P], xg[:, u, j, :], hot[:, s, j, :],
                                        start=False, stop=(j == T - 1), skip_group_check=True)
                    ins.then_inc(sum3, 1)
                if valid(pk, pu, NG):
                    pe.wait_ge(act3, pi + 1)
                    need(pe, o3_copied, pi)
                    pe.matmul(bank[5][:, :], w2_sb[:, :], act_t[:, ps, :], start=True, stop=True).then_inc(o3, 1)
                pk, pu = back(k, u, 2)
                if valid(pk, pu, NG):
                    pi = 4 * pk + pu
                    ps = pu % 2
                    pe.wait_ge(o3_copied, pi + 1)
                    need(pe, z3, pi - 1)
                    for j in range(T):
                        ins = pe.transpose(bank[6 + ps][:, j * P:(j + 1) * P], out_t[:, ps, j * P:(j + 1) * P],
                                           ident[:, :])
                    ins.then_inc(back3, 1)

            each(pe, NG, 2, stage3)

        @block.scalar
        def _(act):
            def stage1(k, u):
                i = 4 * k + u
                s = u % 2
                if valid(k, u, EG):
                    act.wait_ge(xg_turned, i + 1)
                    need(act, products, 8 * (i - 1))
                    act.activation(xg_t[:, s, :], bank[4][:, :], ACT.Copy).then_inc(xg_t_ready, 1)
                    act.wait_ge(taken_done, i + 2)
                    need(act, looked_up, i - 1)
                    act.activation(taken[:, s, :, :],
                                   bank[6][0:A_OF, 256:256 + 32 * (T + 1)].rearrange("a (t b) -> a t b", b=32),
                                   ACT.Copy).then_inc(taken_copied, 1)
                pk, pu = back(k, u, 1)
                if valid(pk, pu, EG):
                    i = 4 * pk + pu
                    s = pu % 2
                    act.wait_ge(coef_ready, i + 1)
                    for j in range(T):
                        pair = 2 * i + j // 2
                        w = j % 2
                        act.wait_ge(products, 4 * pair + w + 1)
                        need(act, seeds_added, i * T + j - 1)
                        for b in range(SEED):
                            ins = act.activation(seeds[:, w, b, :], bank[w][:, b * D:(b + 1) * D], ACT.Copy,
                                                 scale=coef[:, s, j, b:b + 1])
                        ins.then_inc(seeds_ready, 1)

            each(act, EG, 1, stage1)

            act.wait_ge(consts_loaded, 16 * CONSTS)

            def stage2(k, u):
                i = 4 * k + u
                s = u % 2
                if valid(k, u, NG):
                    act.wait_ge(turned2, i + 1)
                    need(act, sum2, i - 1)
                    act.activation(lhs_t[:, s, :], bank[0 + s][:, :], ACT.Copy).then_inc(lhs2, 1)
                pk, pu = back(k, u, 1)
                if valid(pk, pu, NG):
                    i = 4 * pk + pu
                    s = pu % 2
                    act.wait_ge(sum2, i + 1)
                    need(act, back2, i - 1)
                    act.activation(act_t[:, s, :], bank[2 + s][:, :], ACT.Relu, bias=h_bias_sb[:, 0:1])\
                        .then_inc(act2, 1)
                pk, pu = back(k, u, 2)
                if valid(pk, pu, NG):
                    i = 4 * pk + pu
                    s = pu % 2
                    act.wait_ge(mv2_done, i + 1)
                    need(act, rstd2_done, i - 1)
                    act.activation(sd[:, s, :].unsqueeze(2), mv[:, s, :, 1:2], ACT.Sqrt, bias=ln_eps[:, 0:1])\
                        .then_inc(sd2_done, 1)
                pk, pu = back(k, u, 3)
                if valid(pk, pu, NG):
                    i = 4 * pk + pu
                    s = pu % 2
                    act.wait_ge(norm2, i + 1)
                    if valid(*back(pk, pu, 2), NG):
                        act.wait_ge(x1_stored[s], 16 * (2 * pk + pu // 2))
                    for j in range(T):
                        ins = act.activation(res[:, s, j, :], y[:, s, j, :], ACT.Identity,
                                             scale=rstd[:, s, j:j + 1], bias=shift[:, s, j:j + 1])
                    ins.then_inc(x1_done, 1)
                    act.wait_ge(x1_done, i + 1)
                    for rows, tiles in rows_and_tiles(x1_rows, res[:, s, :, :], pk, pu):
                        act.dma_start(rows, tiles).then_inc(x1_stored[s], 16)

            each(act, NG, 3, stage2)
            for s in range(2):
                act.wait_ge(x1_stored[s], 16 * (NG // 2 + s))

            def stage3(k, u):
                i = 4 * k + u
                s = u % 2
                if valid(k, u, NG):
                    act.wait_ge(ea3, i + 1)
                    need(act, sum3, i - 1)
                    act.activation(ea_t[:, s, :], bank[2][0:ED + 1, :], ACT.Copy).then_inc(ea3_copied, 1)
                pk, pu = back(k, u, 1)
                if valid(pk, pu, NG):
                    pi = 4 * pk + pu
                    ps = pu % 2
                    act.wait_ge(mid3, pi + 1)
                    need(act, o3, pi - 1)
                    act.activation(act_t[:, ps, :], bank[3 + ps][:, :], ACT.Relu, bias=b1_sb[:, 0:1])\
                        .then_inc(act3, 1)
                if valid(k, u, NG):
                    act.wait_ge(sum3, i + 1)
                    need(act, mid3, i - 1)
                    act.activation(lhs_t[:, s, :], bank[0 + s][:, :], ACT.Copy).then_inc(lhs3, 1)
                if valid(pk, pu, NG):
                    act.wait_ge(o3, pi + 1)
                    need(act, back3, pi - 1)
                    act.activation(out_t[:, ps, :], bank[5][:, :], ACT.Identity, bias=b2_sb[:, 0:1])\
                        .then_inc(o3_copied, 1)
                for lag, ready, dest, of, done, used in ((3, mv3a, sd, mv, sd3a, rstd3a),
                                                         (4, mv3b, sd2, mv2, sd3b, rstd3b)):
                    pk, pu = back(k, u, lag)
                    if valid(pk, pu, NG):
                        pi = 4 * pk + pu
                        ps = pu % 2
                        act.wait_ge(ready, pi + 1)
                        need(act, used, pi - 1)
                        act.activation(dest[:, ps, :].unsqueeze(2), of[:, ps, :, 1:2], ACT.Sqrt,
                                       bias=ln_eps[:, 0:1]).then_inc(done, 1)
                pk, pu = back(k, u, 5)
                if valid(pk, pu, NG):
                    pi = 4 * pk + pu
                    ps = pu % 2
                    act.wait_ge(norm3, pi + 1)
                    if valid(*back(pk, pu, 2), NG):
                        act.wait_ge(out_stored[ps], 16 * (2 * pk + pu // 2))
                    for j in range(T):
                        ins = act.activation(res[:, ps, j, :], y[:, ps, j, :], ACT.Identity,
                                             scale=rstd[:, ps, j:j + 1], bias=shift[:, ps, j:j + 1])
                    ins.then_inc(out_done, 1)
                    act.wait_ge(out_done, pi + 1)
                    for rows, tiles in rows_and_tiles(out, res[:, ps, :, :], pk, pu):
                        act.dma_start(rows, tiles).then_inc(out_stored[ps], 16)

            each(act, NG, 5, stage3)


_INS = ['x', 'src', 'dst', 'edge_attr_32', 'edge_type_32', 'edge_weight1', 'L0_gnn_weight', 'L0_gnn_w_comp',
        'L0_gnn_loop_weight', 'L0_gnn_h_bias', 'L1_gnn_We', 'L1_gnn_be', 'L1_gnn_W1', 'L1_gnn_b1', 'L1_gnn_W2',
        'L1_gnn_b2', 'L1_gnn_eps', 'L1_gnn_gamma', 'L1_gnn_beta']


def kernel(**inputs):
    import numpy as _np
    import concourse.bacc as _bacc
    from concourse import mybir as _mybir
    from concourse.bass_utils import run_bass_kernel_spmd as _run

    nc = _bacc.Bacc("TRN2", target_bir_lowering=False, num_devices=1)
    arrays, args = {}, []
    for name in _INS:
        a = _np.ascontiguousarray(inputs[name])
        arrays[f"in_{name}"] = a
        args.append(nc.dram_tensor(f"in_{name}", a.shape, _mybir.dt.from_np(a.dtype), kind="ExternalInput").ap())
    out = nc.dram_tensor("out_0", arrays["in_x"].shape, _mybir.dt.float32, kind="ExternalOutput").ap()
    gnn_two_layers(nc, *args, out)
    r = _run(nc, [arrays], core_ids=[0])
    return r.results[0]["out_0"]
```

```python
import concourse.bass as bass
from concourse import mybir
from contextlib import ExitStack


def gnn_two_layers(
    nc: bass.Bass,
    x: bass.AP,
    src: bass.AP,
    dst: bass.AP,
    edge_attr: bass.AP,
    edge_type: bass.AP,
    edge_weight: bass.AP,
    basis: bass.AP,
    w_comp: bass.AP,
    loop_weight: bass.AP,
    h_bias: bass.AP,
    We: bass.AP,
    be: bass.AP,
    W1: bass.AP,
    b1: bass.AP,
    W2: bass.AP,
    b2: bass.AP,
    eps: bass.AP,
    gamma: bass.AP,
    beta: bass.AP,
    out: bass.AP,
):
    f32 = mybir.dt.float32
    i32 = mybir.dt.int32
    bf16 = mybir.dt.bfloat16
    ALU = mybir.AluOpType
    ACT = mybir.ActivationFunctionType
    AX = mybir.AxisListType

    P = 128
    N, D = x.shape
    E = src.shape[0]
    ED = edge_attr.shape[1]
    R, B = w_comp.shape
    T = 4
    GP = T * P
    NG = -(-N // GP)
    NT = NG * T
    LAST = (NG - 1) * GP
    LAST_T = (N - LAST) // P
    LAST_R = N - LAST - LAST_T * P
    EG = -(-E // GP)
    ET = EG * T
    EROWS = (ET + 1) * P
    FULL = E // P
    REST = E - FULL * P
    NONE = 1 << 16
    LN_EPS = 1e-5
    MC = D + 4
    DCOL = D
    ONE, ENODE, EFROM, EC = ED, ED + 1, ED + 2, ED + 4
    QR = ET // 2
    QC = 2 * P
    QREST = E - (QR - 1) * QC
    A_OF = -(-(N // P + 1) // 32)
    CH = 7
    NCH = ET // CH
    SKIP = 1 << 20
    SEED = 2
    U1 = 4
    U = 6

    msg_rows = nc.dram_tensor("msg_rows", [EROWS + NT * P, MC], f32).ap()
    edge_rows = nc.dram_tensor("edge_rows", [EROWS + NT * P, EC], f32).ap()
    sum_rows = nc.dram_tensor("sum_rows", [NT * P, D], f32).ap()
    x1_rows = nc.dram_tensor("x1_rows", [N, D], f32).ap()
    counts_dram = nc.dram_tensor("counts_dram", [2, A_OF, 32], f32).ap()

    ctx = ExitStack()
    with ctx:
        def sb(name, shape, dt=f32):
            return ctx.enter_context(nc.sbuf_tensor(name, shape, dt))

        def sem(name):
            return ctx.enter_context(nc.semaphore(name))

        def sems(name, n):
            return [sem(f"{name}{i}") for i in range(n)]

        basis_sb = sb("basis_sb", [P, B, D])
        w_comp_sb = sb("w_comp_sb", [R, B])
        loop_sb = sb("loop_sb", [P, D])
        we_sb = sb("we_sb", [ED + 1, D])
        w1_sb = sb("w1_sb", [P, D])
        w2_sb = sb("w2_sb", [P, D])
        h_bias_sb = sb("h_bias_sb", [P, 1])
        b1_sb = sb("b1_sb", [P, 1])
        b2_sb = sb("b2_sb", [P, 1])
        gamma_sb = sb("gamma_sb", [P, D])
        beta_sb = sb("beta_sb", [P, D])
        eps_sb = sb("eps_sb", [P, 1])
        eps1_sb = sb("eps1_sb", [P, 1])
        ident = sb("ident", [P, P])
        self_diag = sb("self_diag", [P, P])
        count_up = sb("count_up", [P, GP])
        part_no = sb("part_no", [P, 1])
        group_start = sb("group_start", [P, NG])
        ones_bf = sb("ones_bf", [P, CH * 32], bf16)
        ones_col = sb("ones_col", [P, 1])
        dst_q = sb("dst_q", [QR, QC], i32)
        next_q = sb("next_q", [QR, QC], i32)
        src_q = sb("src_q", [QR, QC], i32)
        norm_q = sb("norm_q", [QR, QC])
        dst_qf = sb("dst_qf", [QR, QC])
        src_qf = sb("src_qf", [QR, QC])
        next_qf = sb("next_qf", [QR, QC])
        falls_q = sb("falls_q", [QR, QC])
        stat_q = sb("stat_q", [QR, 1])
        dst_t = sb("dst_t", [P, ET + 1])
        src_t = sb("src_t", [P, ET + 1])
        src_row = sb("src_row", [P, ET], i32)
        dst_row = sb("dst_row", [P, ET + 1], i32)
        norm_t = sb("norm_t", [P, ET])
        skip_t = sb("skip_t", [P, ET])
        node_i = sb("node_i", [P, 2, ET], i32)
        a_i = sb("a_i", [P, 2, ET], i32)
        b_i = sb("b_i", [P, 2, ET], i32)
        b_m = sb("b_m", [P, 2, ET], i32)
        a_f = sb("a_f", [P, 2, ET])
        b_f = sb("b_f", [P, 2, ET])
        tile_f = sb("tile_f", [P, ET])
        pairs_sb = sb("pairs_sb", [CH * A_OF, 2, CH * 32])
        counts_sb = sb("counts_sb", [A_OF, 2, 32])
        count_row = sb("count_row", [1, 2, A_OF * 32])
        stat_row = sb("stat_row", [1, 1])
        sums_start = sb("sums_start", [1, 2, NT])
        win_d = sb("win_d", [1, 2, NT])
        win_g = sb("win_g", [1, 2, NT])
        most = sb("most", [1, 2])
        fits = sb("fits", [1, 2])
        no_falls = sb("no_falls", [1, 1])
        win_row = sb("win_row", [1, 2, NT], i32)
        ok_i = sb("ok_i", [1, 2], i32)
        edge_out = sb("edge_out", [P, ET + 1, EC])
        pad_msgs = sb("pad_msgs", [P, MC])
        pad_edges = sb("pad_edges", [P, EC])
        steps_a = sb("steps_a", [A_OF, A_OF])
        before = sb("before", [P, P])
        a_from = sb("a_from", [A_OF, 1])
        srcs = sb("srcs", [P, 4, GP], i32)
        tiles_bc = sb("tiles_bc", [P, 2, GP], i32)
        same_tile = sb("same_tile", [P, 2, T, P], bf16)
        a_ge = sb("a_ge", [A_OF, 2, GP])
        a_hot = sb("a_hot", [P, 2, T, A_OF + 1], bf16)
        b_bf = sb("b_bf", [P, 2, T, 32], bf16)
        a_step = sb("a_step", [P, 2, T, A_OF], bf16)
        b_hot = sb("b_hot", [P, 4, T, 32])
        taken = sb("taken", [A_OF, 2, T + 1, 32])
        looked = sb("looked", [P, 2, T, 32])
        place_f = sb("place_f", [P, 2, T])
        place_s = sb("place_s", [P, 2, T])
        place_t = sb("place_t", [P, ET], i32)
        place_now = sb("place_now", [P, 2, T], i32)
        edge_now = sb("edge_now", [P, 2, T, EC])
        types = sb("types", [R, 4, GP], i32)
        type_hot = sb("type_hot", [R, 2, GP])
        src_now = sb("src_now", [P, 4, T], i32)
        xg = sb("xg", [P, 4, T, D])
        xg_t = sb("xg_t", [P, 2, GP])
        coef = sb("coef", [P, 2, T, B])
        seeds = sb("seeds", [P, 2, SEED, D])
        seed_sum = sb("seed_sum", [P, 2, D])
        msgs = sb("msgs", [P, 2, T, MC])
        marks = sb("marks", [P, 2, ET * (2 * A_OF + 32)], bf16)
        a_eq = marks[:, :, 0:ET * A_OF]
        a_lt = marks[:, :, ET * A_OF:2 * ET * A_OF]
        b_lt = marks[:, :, 2 * ET * A_OF:]
        reused = marks[:, :, :].rearrange("p l c -> p (l c)").bitcast(f32)
        parts, at = [], 0
        for slots, cols in ((U, D), (3, P), (2, D), (2, D), (1, MC), (1, EC), (U, MC)):
            size = slots * T * cols
            parts.append(reused[:, at:at + size].rearrange("p (s t c) -> p s t c", s=slots, t=T))
            at += size
        xin, hot, y, res, g_rows, g_edges, mwin = parts
        at -= U * T * MC
        for slots, cols in ((U, EC), (2, D), (3, D)):
            size = slots * T * cols
            parts.append(reused[:, at:at + size].rearrange("p (s t c) -> p s t c", s=slots, t=T))
            at += size
        ewin, z, xb = parts[-3:]
        g_rows, g_edges = g_rows[:, 0], g_edges[:, 0]
        lhs_t = sb("lhs_t", [P, 2, GP])
        act_t = sb("act_t", [P, 2, GP])
        out_t = sb("out_t", [P, 2, GP])
        ea_t = sb("ea_t", [ED + 1, 2, GP])
        st = sb("st", [P, 2, T, 6])
        st2 = sb("st2", [P, 2, T, 6])
        mv = sb("mv", [P, 2, 2, T, 2])
        sd = sb("sd", [P, 2, 2, T])
        rstd = sb("rstd", [P, 2, 2, T])
        shift = sb("shift", [P, 2, T])
        ln_eps = sb("ln_eps", [P, 1])

        g_node0 = sb("g_node0", [P, T])
        g_key = sb("g_key", [P, 1])
        g_key_wide = sb("g_key_wide", [P, P])
        g_same = sb("g_same", [P, P])
        g_earlier = sb("g_earlier", [P, P])
        g_attr = sb("g_attr", [P, ED + 1])
        g_attr_t = sb("g_attr_t", [ED + 1, P])
        g_from = sb("g_from", [P, 1], i32)
        g_x = sb("g_x", [P, D])
        g_msg = sb("g_msg", [P, D])
        g_again = sb("g_again", [P, 1])
        g_at = sb("g_at", [P, 1], i32)
        g_sum = sb("g_sum", [P, MC])

        bank = [ctx.enter_context(nc.psum_tensor(f"bank{i}", [P, GP], f32)) for i in range(8)]

        wait_passed = sem("wait_passed")
        consts_loaded = sem("consts_loaded")
        lists_loaded = sem("lists_loaded")
        attr_loaded = sem("attr_loaded")
        pads_set = sem("pads_set")
        consts_made = sem("consts_made")
        zeroed = sem("zeroed")
        dve0 = sem("dve0")
        lists_f = sem("lists_f")
        lists_turned = sem("lists_turned")
        lists_ready = sem("lists_ready")
        stats_ready = sem("stats_ready")
        place_marks = sem("place_marks")
        taken_done = sem("taken_done")
        taken_copied = sem("taken_copied")
        tiles_shifted = sem("tiles_shifted")
        a_marked = sem("a_marked")
        looked_up = sem("looked_up")
        looked_picked = sem("looked_picked")
        looked_summed = sem("looked_summed")
        hots_marked = sem("hots_marked")
        windows0 = sem("windows0")
        ranks_added = sem("ranks_added")
        placed = sem("placed")
        edges_now = sem("edges_now")
        edges_scattered = sems("edges_scattered", 2)
        stats_summed = sem("stats_summed")
        marks_ready = sem("marks_ready")
        pairs_counted = sem("pairs_counted")
        pairs_copied = sem("pairs_copied")
        counts_added = sem("counts_added")
        counts_copied = sem("counts_copied")
        counts_out = sem("counts_out")
        counts_in = sem("counts_in")
        windows_ready = sem("windows_ready")
        edge_cols = sem("edge_cols")
        pads_stored = sem("pads_stored")
        g_begun = sems("g_begun", 2)
        g_rows_set = sems("g_rows_set", 2)
        g_rows_out = sems("g_rows_out", 2)
        g_msg_in = sem("g_msg_in")
        g_from_set = sem("g_from_set")
        g_x_in = sem("g_x_in")
        g_cols_set = sems("g_cols_set", 2)
        g_turned = sems("g_turned", 2)
        g_compared = sems("g_compared", 2)
        g_marked = sems("g_marked", 2)
        g_attr_out = sem("g_attr_out")
        g_msg_made = sem("g_msg_made")
        g_combined = sems("g_combined", 2)
        g_again_set = sems("g_again_set", 2)
        g_at_set = sems("g_at_set", 2)
        g_fetched = sems("g_fetched", 2)
        g_added = sems("g_added", 2)
        g_stored = sems("g_stored", 2)
        lists1_loaded = sems("lists1_loaded", 4)
        src_placed = sem("src_placed")
        xg_loaded = sems("xg_loaded", 4)
        hot_types = sem("hot_types")
        xg_turned = sem("xg_turned")
        xg_t_ready = sem("xg_t_ready")
        coef_done = sem("coef_done")
        coef_ready = sem("coef_ready")
        products = sem("products")
        seeds_ready = sem("seeds_ready")
        seeds_added = sem("seeds_added")
        chain1 = sem("chain1")
        msgs_ready = sem("msgs_ready")
        msgs_stored = sems("msgs_stored", 2)
        in2 = sems("in2_", U)
        hot2 = sem("hot2")
        turned2 = sem("turned2")
        lhs2 = sem("lhs2")
        sum2 = sem("sum2")
        act2 = sem("act2")
        back2 = sem("back2")
        y2 = sem("y2")
        st2_done = sem("st2_done")
        mv2_done = sem("mv2_done")
        sd2_done = sem("sd2_done")
        rstd2_done = sem("rstd2_done")
        norm2 = sem("norm2")
        x1_done = sem("x1_done")
        x1_stored = sems("x1_stored", 2)
        stats_zeroed = sem("stats_zeroed")
        in3 = sems("in3_", U)
        ewin_loaded = sems("ewin_loaded", U)
        xg3_loaded = sems("xg3_loaded", 3)
        hot3 = sem("hot3")
        ea3 = sem("ea3")
        ea3_copied = sem("ea3_copied")
        sum3 = sem("sum3")
        lhs3 = sem("lhs3")
        mid3 = sem("mid3")
        act3 = sem("act3")
        o3 = sem("o3")
        o3_copied = sem("o3_copied")
        back3 = sem("back3")
        xb3 = sem("xb3")
        st3a = sem("st3a")
        mv3 = sem("mv3")
        sd3 = sem("sd3")
        rstd3 = sem("rstd3")
        z3 = sem("z3")
        y3 = sem("y3")
        st3b = sem("st3b")
        norm3 = sem("norm3")
        out_done = sem("out_done")
        out_stored = sems("out_stored", 2)

        def need(eng, s, value):
            if not (isinstance(value, int) and value <= 0):
                eng.wait_ge(s, value)

        def each(eng, count, more, body, U=U1):
            peeled = 1 if more <= U - 1 - (U == 4) else 2
            end = (count - 1) // U
            for i in range(U * peeled):
                body(i // U, i % U)
            with eng.Fori(peeled, end) as k:
                for u in range(U):
                    body(k, u)
            for i in range(U * end, count + more):
                body(i // U, i % U)

        def back(k, u, d, U=U1):
            return k + (u - d) // U, (u - d) % U

        def valid(k, u, count, U=U1):
            return not isinstance(k, int) or 0 <= U * k + u < count

        def node_group(k, u, lag):
            k, u = back(k, u, lag, U)
            return k, u, U * k + u, valid(k, u, NG, U)

        def node0(k, u):
            return (U * k + u) * GP

        def last(k, u):
            return isinstance(k, int) and U * k + u == NG - 1

        def loaded_count(k, u):
            return 80 * (k + 1) + 16 * last(k, u)

        def rows_count(k, u):
            return 16 * (k + 1) + 16 * last(k, u)

        def stored_before(k, u):
            return 16 * (U // 2 * k + u // 2)

        def rows_and_tiles(dram, tiles, k, u):
            if last(k, u):
                mid = LAST + LAST_T * P
                return [(tiles_of(dram[LAST:mid, :]), tiles[:, 0:LAST_T, :]),
                        (dram[mid:N, :], tiles[0:LAST_R, LAST_T, :])]
            return [(tiles_of(dram[bass.ds(node0(k, u), GP), :]), tiles)]

        def tiles_of(rows):
            return rows.rearrange("(j p) d -> p j d", p=P)

        g_table = (msg_rows, sum_rows)
        g_cols = (MC, D)
        g_base = (EROWS, 0)
        g_keys = (dst_t, src_t)

        def g_tiles(eng, body):
            body(0)
            with eng.Fori(1, ET) as t:
                body(t)

        def g_groups(eng, body):
            body(0)
            with eng.Fori(1, NG) as g:
                body(g)

        block = ctx.enter_context(nc.Block())

        CONSTS = 13

        @block.sync
        def _(sp):
            flat = (QR - 1) * QC
            sp.wait_ge(pads_set, 1)
            for q, a, n in ((dst_q, dst, E), (src_q, src, E), (next_q, dst[1:E], E - 1),
                            (norm_q, edge_weight.rearrange("e o -> (e o)"), E)):
                sp.dma_start(q[0:QR - 1, :], a[0:flat].rearrange("(q c) -> q c", c=QC)).then_inc(lists_loaded, 16)
                sp.dma_start(q[QR - 1:QR, 0:n - flat],
                             a[flat:n].rearrange("(q c) -> q c", q=1)).then_inc(lists_loaded, 16)
            sp.dma_start(basis_sb[:, :, :], basis.rearrange("b d f -> d b f")).then_inc(consts_loaded, 16)
            sp.dma_start(w_comp_sb[:, :], w_comp).then_inc(consts_loaded, 16)
            sp.dma_start(loop_sb[:, :], loop_weight).then_inc(consts_loaded, 16)
            sp.dma_start(we_sb[0:ED, :], We).then_inc(consts_loaded, 16)
            sp.dma_start(we_sb[ED:ED + 1, :], be.rearrange("(o d) -> o d", o=1)).then_inc(consts_loaded, 16)
            sp.dma_start(w1_sb[:, :], W1).then_inc(consts_loaded, 16)
            sp.dma_start(w2_sb[:, :], W2).then_inc(consts_loaded, 16)
            for c, a in ((h_bias_sb, h_bias), (b1_sb, b1), (b2_sb, b2)):
                sp.dma_start(c[:, :], a.rearrange("(d o) -> d o", o=1)).then_inc(consts_loaded, 16)
            for c, a in ((gamma_sb, gamma), (beta_sb, beta), (eps_sb, eps)):
                sp.dma_start(c[:, :], a.partition_broadcast(P)).then_inc(consts_loaded, 16)
            sp.wait_ge(zeroed, 1)
            sp.dma_start(edge_out[:, 0:FULL, 0:ED],
                         edge_attr[0:FULL * P, :].rearrange("(t p) c -> p t c", p=P)).then_inc(attr_loaded, 16)
            sp.dma_start(edge_out[0:REST, FULL, 0:ED], edge_attr[FULL * P:E, :]).then_inc(attr_loaded, 16)

            sp.wait_ge(edge_cols, 1)
            sp.dma_start(edge_rows[E:E + P, :], pad_edges[:, :]).then_inc(pads_stored, 16)
            sp.dma_start(edge_rows[E + P:EROWS, :], pad_edges[0:EROWS - E - P, :]).then_inc(pads_stored, 16)
            sp.wait_ge(counts_copied, 1)
            sp.dma_start(counts_dram.rearrange("l a b -> a l b"), counts_sb[:, :, :]).then_inc(counts_out, 16)
            sp.wait_ge(counts_out, 16)
            sp.dma_start(count_row[:, :, :], counts_dram.rearrange("(o l) a b -> o l (a b)", o=1))\
                .then_inc(counts_in, 16)

            def load_types(k, u):
                i = 4 * k + u
                need(sp, hot_types, i - 3)
                n = E - i * GP if isinstance(i, int) and i == EG - 1 else GP
                e0 = i * GP
                sp.dma_start(types[:, u, 0:n],
                             edge_type[bass.ds(e0, n)].partition_broadcast(R)).then_inc(lists1_loaded[u], 16)
                need(sp, tiles_shifted, i - 3)
                need(sp, a_marked, i - 3)
                sp.dma_start(srcs[:, u, 0:n],
                             src[bass.ds(e0, n)].partition_broadcast(P)).then_inc(lists1_loaded[u], 16)

            def store_msgs(k, u):
                i = 4 * k + u
                sp.wait_ge(msgs_ready, i + 1)
                sp.dma_start(tiles_of(msg_rows[bass.ds(i * GP, GP), :]), msgs[:, u % 2, :, :])\
                    .then_inc(msgs_stored[u % 2], 16)

            def stage1(k, u):
                if valid(k, u, EG):
                    load_types(k, u)
                if valid(*back(k, u, 2), EG):
                    store_msgs(*back(k, u, 2))
            each(sp, EG, 2, stage1)
            sp.dma_start(msg_rows[EROWS - P:EROWS, :], pad_msgs[:, :]).then_inc(pads_stored, 16)

            sp.wait_ge(windows_ready, 1)
            sp.wait_ge(pads_stored, 48)
            for s in range(2):
                sp.wait_ge(msgs_stored[s], 16 * len(range(s, EG, 2)))

            def general(n):
                def set_rows(g):
                    sp.wait_ge(g_rows_set[n], g + 1)
                    if n == 0:
                        sp.dma_start(tiles_of(msg_rows[bass.ds(EROWS + g * GP, GP), :]), g_rows[:, :, :])\
                            .then_inc(g_rows_out[n], 16)
                    else:
                        sp.dma_start(tiles_of(edge_rows[bass.ds(EROWS + g * GP, GP), :]), g_edges[:, :, :])\
                            .then_inc(g_rows_out[n], 16)
                        sp.dma_start(tiles_of(sum_rows[bass.ds(g * GP, GP), :]), g_rows[:, :, 0:D])\
                            .then_inc(g_rows_out[n], 16)

                def load_msgs(t):
                    need(sp, g_stored[n], 16 * t)
                    sp.dma_start(g_msg[:, :], msg_rows[bass.ds(t * P, P), 0:D]).then_inc(g_msg_in, 16)

                g_groups(sp, set_rows)
                if n == 0:
                    g_tiles(sp, load_msgs)
                sp.wait_ge(g_rows_out[n], 16 * (n + 1) * NG)
                sp.wait_ge(g_stored[n], 16 * ET)

            ok = sp.value_load(ok_i[0:1, 0:1], min_val=0, max_val=1)
            with sp.If(ok < 1):
                general(0)

            def load_windows(n, i, win, rows, done):
                _, starts = nc.values_load_multi_w_load_instructions(
                    win_row[0:1, n, bass.ds(i * T, T)], engines=[sp.engine],
                    min_val=0, max_val=EROWS + NT * P - P)
                for j in range(T):
                    sp.dma_start(win[:, j, :], rows[bass.ds(starts[j], P), :]).then_inc(done, 16)

            def load2(k, u):
                i = U * k + u
                need(sp, y2, i - U + 1)
                for rows, tiles in rows_and_tiles(x, xin[:, u, :, :], k, u):
                    sp.dma_start(tiles, rows).then_inc(in2[u], 16)
                load_windows(0, i, mwin[:, u, :, :], msg_rows, in2[u])

            each(sp, NG, 0, load2, U)

            for s in range(2):
                sp.wait_ge(x1_stored[s], 16 * (NG // 2 + s))
                sp.wait_ge(edges_scattered[s], 64 * len(range(s, EG, 2)))

            ok = sp.value_load(ok_i[0:1, 1:2], min_val=0, max_val=1)
            with sp.If(ok < 1):
                general(1)

            def load3(k, u):
                i = U * k + u
                need(sp, sum3, i - U + 1)
                need(sp, xb3, i - U + 1)
                load_windows(1, i, ewin[:, u, :, :], edge_rows, ewin_loaded[u])
                for rows, tiles in rows_and_tiles(x1_rows, xin[:, u, :, :], k, u):
                    sp.dma_start(tiles, rows).then_inc(in3[u], 16)

            each(sp, NG, 0, load3, U)
            for s in range(2):
                sp.wait_ge(out_stored[s], 16 * (NG // 2 + s))

        @block.gpsimd
        def _(pool):
            pool.memset(edge_out[:, FULL:ET + 1, :], 0.0).then_inc(zeroed, 1)
            pool.memset(ident[:, :], 0.0).then_inc(consts_made, 1)
            pool.wait_ge(consts_made, 1)
            pool.affine_select(out=ident[:, :], in_=ident[:, :], compare_op=ALU.not_equal, fill=1.0,
                               base=0, pattern=[[-1, P]], channel_multiplier=1)
            pool.iota(count_up[:, :], pattern=[[1, GP]], base=0, channel_multiplier=0,
                      allow_small_or_imprecise_dtypes=True)
            pool.iota(part_no[:, :], pattern=[[1, 1]], base=0, channel_multiplier=1,
                      allow_small_or_imprecise_dtypes=True)
            pool.iota(group_start[:, :], pattern=[[GP, NG]], base=0, channel_multiplier=0,
                      allow_small_or_imprecise_dtypes=True)
            pool.iota(sums_start[:, :, :], pattern=[[0, 2], [P, NT]], base=EROWS, channel_multiplier=0,
                      allow_small_or_imprecise_dtypes=True)
            pool.iota(g_node0[:, :], pattern=[[P, T]], base=0, channel_multiplier=1,
                      allow_small_or_imprecise_dtypes=True)
            pool.iota(a_from[:, :], pattern=[[1, 1]], base=0, channel_multiplier=32 * P,
                      allow_small_or_imprecise_dtypes=True)
            pool.memset(before[:, :], 0.0)
            pool.memset(pad_edges[:, :], 0.0)
            pool.memset(a_hot[:, :, :, 0:1], 0.0)
            pool.memset(steps_a[:, :], 0.0).then_inc(consts_made, 1)
            pool.wait_ge(consts_made, 2)
            pool.memset(pad_edges[:, ENODE:ENODE + 1], float(NONE))
            pool.affine_select(out=before[:, :], in_=before[:, :], compare_op=ALU.is_ge, fill=1.0,
                               base=0, pattern=[[-1, P]], channel_multiplier=1)
            pool.affine_select(out=steps_a[:, :], in_=steps_a[:, :], compare_op=ALU.not_equal, fill=1.0,
                               base=0, pattern=[[-1, A_OF]], channel_multiplier=1).then_inc(consts_made, 1)
            pool.wait_ge(consts_made, 3)
            pool.affine_select(out=steps_a[:, :], in_=steps_a[:, :], compare_op=ALU.not_equal, fill=-1.0,
                               base=1, pattern=[[-1, A_OF]], channel_multiplier=1)
            pool.memset(ln_eps[:, :], LN_EPS)
            pool.memset(ones_bf[:, :], 1.0)
            pool.memset(ones_col[:, :], 1.0)
            pool.memset(pad_msgs[:, :], 0.0)
            pool.memset(edge_out[:, :, ONE:ONE + 1], 1.0)
            pool.memset(edge_out[:, :, EC - 1:EC], 0.0)
            pool.memset(msgs[:, :, :, DCOL:MC], 0.0).then_inc(consts_made, 1)
            pool.wait_ge(lists_ready, 1)

            def sources1(k, u):
                i = 4 * k + u
                need(pool, xg_turned, i - 3)
                pool.tensor_copy(src_now[:, u, :], src_row[:, bass.ds(i * T, T)]).then_inc(src_placed, 1)
                pool.wait_ge(src_placed, i + 1)
                pool.sem_inc(wait_passed, 1)

            def gather1(u, j):
                pool.indirect_dma_start(
                    out=xg[:, u, j, :], out_offset=None, in_=x,
                    in_offset=bass.IndirectOffsetOnAxis(ap=src_now[:, u, j:j + 1], axis=0),
                ).then_inc(xg_loaded[u], 16)

            def stage1(k, u):
                if valid(k, u, EG):
                    sources1(k, u)
                for j in range(T):
                    if valid(k, u, EG):
                        gather1(u, j)
                    pk, pu = back(k, u, 2)
                    if valid(pk, pu, EG):
                        t = (4 * pk + pu) * T + j
                        pool.wait_ge(seeds_ready, t + 1)
                        if isinstance(t, int) and t < 2:
                            pass
                        elif j % 2 == 0:
                            pool.wait_ge(chain1, (t // 2 if isinstance(t, int) else (4 * pk + pu) * 2 + j // 2) * 12)
                        pool.tensor_tensor(seed_sum[:, j % 2, :], seeds[:, j % 2, 0, :], seeds[:, j % 2, 1, :],
                                           ALU.add).then_inc(seeds_added, 1)

            each(pool, EG, 2, stage1)

            def general(n):
                def tile(t):
                    if n == 1:
                        need(pool, g_stored[n], 16 * t)
                        pool.tensor_copy(g_from[:, :], edge_out[:, bass.ds(t, 1), EFROM].bitcast(i32))\
                            .then_inc(g_from_set, 1)
                        pool.wait_ge(g_from_set, t + 1)
                        pool.sem_inc(wait_passed, 1)
                        pool.indirect_dma_start(
                            out=g_x[:, :], out_offset=None, in_=x1_rows,
                            in_offset=bass.IndirectOffsetOnAxis(ap=g_from[:, :], axis=0)).then_inc(g_x_in, 16)
                    pool.wait_ge(g_at_set[n], t + 1)
                    pool.sem_inc(wait_passed, 1)
                    pool.indirect_dma_start(
                        out=g_sum[:, 0:g_cols[n]], out_offset=None, in_=g_table[n],
                        in_offset=bass.IndirectOffsetOnAxis(ap=g_at[:, :], axis=0),
                        bounds_check=g_base[n] + N - 1, oob_is_err=False).then_inc(g_fetched[n], 16)
                    pool.wait_ge(g_added[n], t + 1)
                    pool.sem_inc(wait_passed, 1)
                    pool.indirect_dma_start(
                        out=g_table[n], out_offset=bass.IndirectOffsetOnAxis(ap=g_at[:, :], axis=0),
                        in_=g_sum[:, 0:g_cols[n]], in_offset=None,
                        bounds_check=g_base[n] + N - 1, oob_is_err=False).then_inc(g_stored[n], 16)
                    pool.wait_ge(g_stored[n], 16 * (t + 1))
                    pool.sem_inc(wait_passed, 1)

                pool.wait_ge(g_rows_out[n], 16 * (n + 1) * NG)
                if n == 0:
                    for s in range(2):
                        pool.wait_ge(msgs_stored[s], 16 * len(range(s, EG, 2)))
                    pool.wait_ge(pads_stored, 48)
                g_tiles(pool, tile)

            pool.wait_ge(windows_ready, 1)
            ok = pool.value_load(ok_i[0:1, 0:1], min_val=0, max_val=1)
            with pool.If(ok < 1):
                general(0)

            pool.wait_ge(edge_cols, 1)

            def scatter2(k, u):
                i = 4 * k + u
                s = u % 2
                if valid(*back(k, u, 2), EG):
                    pool.wait_ge(edges_scattered[s], 64 * (2 * k + u // 2))
                pool.wait_ge(placed, i + 1)
                pool.tensor_copy(edge_now[:, s, :, :], edge_out[:, bass.ds(i * T, T), :])
                pool.tensor_copy(place_now[:, s, :], place_t[:, bass.ds(i * T, T)]).then_inc(edges_now, 1)
                pool.wait_ge(edges_now, i + 1)
                pool.sem_inc(wait_passed, 1)
                for j in range(T):
                    pool.indirect_dma_start(
                        out=edge_rows, out_offset=bass.IndirectOffsetOnAxis(ap=place_now[:, s, j:j + 1], axis=0),
                        in_=edge_now[:, s, j, :], in_offset=None, bounds_check=E - 1, oob_is_err=False,
                    ).then_inc(edges_scattered[s], 16)

            each(pool, EG, 0, scatter2)
            for s in range(2):
                pool.wait_ge(x1_stored[s], 16 * (NG // 2 + s))

            ok1 = pool.value_load(ok_i[0:1, 1:2], min_val=0, max_val=1)
            with pool.If(ok1 < 1):
                general(1)

            def gather3(k, u):
                i = U * k + u
                s = u % 3
                need(pool, sum3, i - 2)
                pool.wait_ge(ewin_loaded[u], 64 * (k + 1))
                pool.sem_inc(wait_passed, 1)
                with pool.If(ok1 < 1):
                    pool.dma_start(xg[:, s, :, :], tiles_of(sum_rows[bass.ds(node0(k, u), GP), :]))\
                        .then_inc(xg3_loaded[s], 64)
                with pool.Else():
                    for j in range(T):
                        pool.indirect_dma_start(
                            out=xg[:, s, j, :], out_offset=None, in_=x1_rows,
                            in_offset=bass.IndirectOffsetOnAxis(ap=ewin[:, u, j, EFROM:EFROM + 1].bitcast(i32),
                                                                axis=0)).then_inc(xg3_loaded[s], 16)

            each(pool, NG, 0, gather3, U)

        @block.vector
        def _(dve):
            steps = [0]

            def link(ins):
                steps[0] += 1
                ins.then_inc(dve0, 1)
                dve.wait_ge(dve0, steps[0])

            dve.memset(dst_q[96:QR, :], NONE)
            dve.memset(next_q[96:QR, :], NONE)
            dve.memset(src_q[96:QR, :], NONE)
            dve.memset(norm_q[96:QR, :], 0.0).then_inc(pads_set, 1)
            dve.wait_ge(lists_loaded, 16 * 8)
            dve.wait_ge(pads_set, 1)
            dve.tensor_copy(dst_qf[:, :], dst_q[:, :])
            dve.tensor_copy(src_qf[:, :], src_q[:, :]).then_inc(lists_f, 1)
            dve.tensor_copy(next_qf[:, :], next_q[:, :])
            dve.wait_ge(lists_turned, 1)
            for b, dest in enumerate((dst_t, src_t, norm_t)):
                dve.tensor_copy(dest[:, 0:ET].rearrange("p (q h) -> p q h", h=2),
                                bank[b][:, 0:ET].rearrange("p (h q) -> p q h", h=2))
            dve.memset(dst_t[:, ET:ET + 1], float(NONE))
            link(dve.memset(src_t[:, ET:ET + 1], float(NONE)))
            dve.tensor_scalar(src_row[:, :], src_t[:, 0:ET], float(N - 1), None, ALU.min)
            link(dve.tensor_scalar(dst_row[:, :], dst_t[:, :], float(N - 1), None, ALU.min))
            dve.tensor_scalar(skip_t[:, :], src_t[:, 0:ET], float(N), float(SKIP), ALU.is_ge, ALU.mult)\
                .then_inc(lists_ready, 1)
            dve.wait_ge(consts_made, 4)
            dve.tensor_copy(edge_out[:, :, ENODE:ENODE + 1], src_t[:, :].unsqueeze(2))
            dve.tensor_copy(edge_out[:, :, EFROM:EFROM + 1].bitcast(i32), dst_row[:, :].unsqueeze(2))
            dve.wait_ge(attr_loaded, 32)
            dve.wait_ge(consts_loaded, 16 * CONSTS)
            link(dve.tensor_scalar(eps1_sb[:, :], eps_sb[:, :], 1.0, None, ALU.add))
            dve.tensor_scalar(self_diag[:, :], ident[:, :], eps1_sb[:, 0:1], None, ALU.mult).then_inc(edge_cols, 1)
            link(dve.tensor_tensor(falls_q[:, :], dst_qf[:, :], next_qf[:, :], ALU.is_gt))
            dve.tensor_reduce(stat_q[:, :], falls_q[:, :], AX.X, ALU.add).then_inc(stats_ready, 1)
            dve.tensor_copy(node_i[:, 0, :], dst_t[:, 0:ET])
            link(dve.tensor_copy(node_i[:, 1, :], src_t[:, 0:ET]))
            dve.tensor_scalar(a_i[:, :, :], node_i[:, :, :], 12, None, ALU.logical_shift_right)
            link(dve.tensor_scalar(b_i[:, :, :], node_i[:, :, :], 7, None, ALU.logical_shift_right))
            link(dve.tensor_scalar(b_m[:, :, :], b_i[:, :, :], 31, None, ALU.bitwise_and))
            dve.tensor_copy(tile_f[:, :], b_i[:, 1, :])
            dve.tensor_copy(a_f[:, :, :], a_i[:, :, :])
            link(dve.tensor_copy(b_f[:, :, :], b_m[:, :, :]))
            ca = count_up[:, 0:A_OF].unsqueeze(1).to_broadcast([P, ET, A_OF])
            cb = count_up[:, 0:32].unsqueeze(1).to_broadcast([P, ET, 32])
            for n in range(2):
                av = a_f[:, n, :].unsqueeze(2).to_broadcast([P, ET, A_OF])
                bv = b_f[:, n, :].unsqueeze(2).to_broadcast([P, ET, 32])
                dve.tensor_tensor(a_eq[:, n, :].rearrange("p (t a) -> p t a", a=A_OF), av, ca, ALU.is_equal)
                dve.tensor_tensor(a_lt[:, n, :].rearrange("p (t a) -> p t a", a=A_OF), av, ca, ALU.is_lt)
                dve.tensor_tensor(b_lt[:, n, :].rearrange("p (t b) -> p t b", b=32), bv, cb, ALU.is_lt)\
                    .then_inc(marks_ready, 1)
            for n in range(2):
                dve.wait_ge(pairs_counted, n + 1)
                dve.tensor_copy(pairs_sb[:, n, :], bank[3 + n][0:CH * A_OF, 0:CH * 32]).then_inc(pairs_copied, 1)
            dve.wait_ge(counts_added, 1)
            dve.tensor_copy(counts_sb[:, :, :], bank[5][0:A_OF, 0:64].rearrange("a (l b) -> a l b", b=32))\
                .then_inc(counts_copied, 1)
            dve.wait_ge(stats_summed, 1)
            dve.tensor_copy(stat_row[:, :], bank[6][0:1, 0:1])
            dve.wait_ge(taken_done, 1)
            dve.tensor_copy(taken[:, 1, T, :], bank[7][0:A_OF, 0:32]).then_inc(taken_copied, 1)

            def stage1(k, u):
                if valid(k, u, EG):
                    i = 4 * k + u
                    s = u % 2
                    dve.wait_ge(lists1_loaded[u], 32 * (k + 1))
                    need(dve, coef_done, i - 1)
                    dve.tensor_scalar(type_hot[:, s, :], types[:, u, :], part_no[0:R, 0:1], None,
                                      ALU.is_equal).then_inc(hot_types, 1)
                    need(dve, looked_up, i - 1)
                    dve.tensor_scalar(tiles_bc[:, s, :], srcs[:, u, :], 7, None, ALU.logical_shift_right)\
                        .then_inc(tiles_shifted, 1)
                    dve.tensor_scalar(a_ge[:, s, :], srcs[0:A_OF, u, :], a_from[:, 0:1], None, ALU.is_ge)\
                        .then_inc(a_marked, 1)
                    dve.tensor_tensor(a_hot[:, s, :, 1:A_OF + 1],
                                      a_f[:, 1, bass.ds(i * T, T)].unsqueeze(2).to_broadcast([P, T, A_OF]),
                                      count_up[:, 0:A_OF].unsqueeze(1).to_broadcast([P, T, A_OF]), ALU.is_equal)
                    dve.tensor_tensor(b_hot[:, u, :, :],
                                      b_f[:, 1, bass.ds(i * T, T)].unsqueeze(2).to_broadcast([P, T, 32]),
                                      count_up[:, 0:32].unsqueeze(1).to_broadcast([P, T, 32]), ALU.is_equal)\
                        .then_inc(hots_marked, 1)
                    dve.tensor_tensor(b_bf[:, s, :, :],
                                      b_f[:, 1, bass.ds(i * T, T)].unsqueeze(2).to_broadcast([P, T, 32]),
                                      count_up[:, 0:32].unsqueeze(1).to_broadcast([P, T, 32]), ALU.is_equal)
                    dve.wait_ge(tiles_shifted, i + 1)
                    for j in range(T):
                        dve.scalar_tensor_tensor(
                            out=same_tile[:, s, j, :], in0=tiles_bc[:, s, j * P:(j + 1) * P],
                            scalar=tile_f[:, bass.ds(i * T + j, 1)], in1=before[:, :],
                            op0=ALU.is_equal, op1=ALU.mult)
                    dve.wait_ge(hots_marked, i + 1)
                    dve.tensor_tensor(a_step[:, s, :, :], a_hot[:, s, :, 1:A_OF + 1], a_hot[:, s, :, 0:A_OF],
                                      ALU.subtract).then_inc(place_marks, 1)
                pk, pu = back(k, u, 2)
                if valid(pk, pu, EG):
                    i = 4 * pk + pu
                    s = pu % 2
                    dve.wait_ge(looked_up, i + 1)
                    dve.tensor_tensor(looked[:, s, :, :], b_hot[:, pu, :, :],
                                      bank[7][:, P:P + 32 * T].rearrange("p (t b) -> p t b", b=32), ALU.mult)\
                        .then_inc(looked_picked, 1)
                    dve.wait_ge(looked_picked, i + 1)
                    dve.tensor_reduce(place_s[:, s, :], looked[:, s, :, :], AX.X, ALU.add).then_inc(looked_summed, 1)
                    dve.wait_ge(looked_summed, i + 1)
                    dve.tensor_tensor(place_f[:, s, :], place_s[:, s, :], skip_t[:, bass.ds(i * T, T)], ALU.add)\
                        .then_inc(ranks_added, 1)
                    dve.wait_ge(ranks_added, i + 1)
                    dve.tensor_tensor(place_t[:, bass.ds(i * T, T)], place_f[:, s, :], bank[7][:, 64:64 + T],
                                      ALU.add).then_inc(placed, 1)
                    dve.wait_ge(coef_ready, i + 1)
                    if valid(*back(pk, pu, 2), EG):
                        dve.wait_ge(msgs_stored[s], 16 * (2 * pk + pu // 2))
                    dve.tensor_copy(msgs[:, s, :, DCOL:DCOL + 1], dst_t[:, bass.ds(i * T, T)].unsqueeze(2))
                    for h in range(2):
                        pair = 2 * i + h
                        for b in range(SEED, B):
                            for w in range(2):
                                j = 2 * h + w
                                n = 2 * (b - SEED) + w
                                if b == SEED:
                                    dve.wait_ge(seeds_added, i * T + j + 1)
                                if b == 4:
                                    dve.wait_ge(products, 4 * pair + 3 + w)
                                if b > SEED:
                                    dve.wait_ge(chain1, 12 * pair + n - 1)
                                ins = dve.scalar_tensor_tensor(
                                    out=msgs[:, s, j, 0:D],
                                    in0=bank[w + 2 * (b // 4)][:, (b % 4) * D:(b % 4 + 1) * D],
                                    scalar=coef[:, s, j, b:b + 1],
                                    in1=seed_sum[:, w, :] if b == SEED else msgs[:, s, j, 0:D],
                                    op0=ALU.mult, op1=ALU.add).then_inc(chain1, 1)
                    dve.wait_ge(chain1, 12 * (2 * i + 2))
                    dve.sem_inc(msgs_ready, 1)
                if valid(k, u, EG):
                    i = 4 * k + u
                    s = u % 2
                    dve.wait_ge(coef_done, i + 1)
                    dve.tensor_tensor(coef[:, s, :, :], bank[5][:, 0:T * B].rearrange("p (t b) -> p t b", b=B),
                                      norm_t[:, bass.ds(i * T, T)].unsqueeze(2).to_broadcast([P, T, B]),
                                      ALU.mult).then_inc(coef_ready, 1)

            each(dve, EG, 2, stage1)

            dve.wait_ge(counts_in, 16)
            wsteps = [0]

            def wlink(ins):
                wsteps[0] += 1
                ins.then_inc(windows0, 1)
                dve.wait_ge(windows0, wsteps[0])

            wlink(dve.tensor_tensor(win_d[:, :, :], count_row[:, :, 1:NT + 1], count_row[:, :, 0:NT], ALU.subtract))
            dve.tensor_scalar(no_falls[:, :], stat_row[:, :], 0.0, None, ALU.is_equal)
            wlink(dve.tensor_reduce(most[:, :], win_d[:, :, :], AX.X, ALU.max))
            wlink(dve.tensor_scalar(fits[:, :], most[:, :], float(P), None, ALU.is_le))
            wlink(dve.tensor_tensor(fits[:, 0:1], fits[:, 0:1], no_falls[:, :], ALU.mult))
            dve.tensor_copy(ok_i[:, :], fits[:, :])
            wlink(dve.tensor_tensor(win_d[:, :, :], count_row[:, :, 0:NT], sums_start[:, :, :], ALU.subtract))
            for n in range(2):
                ins = dve.scalar_tensor_tensor(out=win_g[:, n, :], in0=win_d[:, n, :], scalar=fits[:, n:n + 1],
                                               in1=sums_start[:, n, :], op0=ALU.mult, op1=ALU.add)
            wlink(ins)
            dve.tensor_copy(win_row[:, :, :], win_g[:, :, :]).then_inc(windows_ready, 1)

            def general(n):
                b_key, b_attr, b_msg, b_sum, b_count = bank[0:5]
                if n == 1:
                    for s in range(2):
                        dve.wait_ge(x1_stored[s], 16 * (NG // 2 + s))

                def set_rows(g):
                    need(dve, g_rows_out[n], 16 * (n + 1) * g)
                    of, c = (g_rows, DCOL) if n == 0 else (g_edges, ENODE)
                    dve.tensor_scalar(of[:, :, c:c + 1], g_node0[:, :].unsqueeze(2),
                                      group_start[:, bass.ds(g, 1)], None, ALU.add).then_inc(g_rows_set[n], 1)

                def tile(t):
                    need(dve, g_stored[n], 16 * t)
                    dve.tensor_copy(g_key[:, :], g_keys[n][:, bass.ds(t, 1)])
                    if n == 1:
                        dve.tensor_copy(g_attr[:, :], edge_out[:, bass.ds(t, 1), 0:ED + 1].rearrange("p o c -> p (o c)"))
                    dve.tensor_copy(g_key_wide[:, :], g_keys[n][:, bass.ds(t, 1)].to_broadcast([P, P]))\
                        .then_inc(g_cols_set[n], 1)
                    dve.wait_ge(g_turned[n], t + 1)
                    if n == 1:
                        dve.tensor_copy(g_attr_t[:, :], b_attr[0:ED + 1, 0:P])
                    dve.tensor_scalar(g_same[:, :], b_key[:, 0:P], g_key[:, 0:1], None, ALU.is_equal)\
                        .then_inc(g_compared[n], 1)
                    dve.wait_ge(g_compared[n], t + 1)
                    dve.tensor_tensor(g_earlier[:, :], g_same[:, :], before[:, :], ALU.mult).then_inc(g_marked[n], 1)
                    if n == 1:
                        dve.wait_ge(g_attr_out, t + 1)
                        dve.wait_ge(g_x_in, 16 * (t + 1))
                        dve.tensor_tensor(g_msg[:, :], g_x[:, :], b_msg[:, 0:D], ALU.add).then_inc(g_msg_made, 1)
                    dve.wait_ge(g_combined[n], t + 1)
                    dve.tensor_scalar(g_again[:, :], b_count[:, 0:1], 0.0, float(SKIP), ALU.is_gt, ALU.mult)\
                        .then_inc(g_again_set[n], 1)
                    dve.wait_ge(g_again_set[n], t + 1)
                    dve.scalar_tensor_tensor(out=g_at[:, :], in0=g_again[:, :], scalar=float(g_base[n]),
                                             in1=g_key[:, :], op0=ALU.add, op1=ALU.add).then_inc(g_at_set[n], 1)
                    dve.wait_ge(g_fetched[n], 16 * (t + 1))
                    dve.tensor_tensor(g_sum[:, 0:D], g_sum[:, 0:D], b_sum[:, 0:D], ALU.add).then_inc(g_added[n], 1)

                dve.memset(g_rows[:, :, :], 0.0)
                dve.memset(g_edges[:, :, :], 0.0)
                dve.memset(g_sum[:, :], 0.0).then_inc(g_begun[n], 1)
                dve.wait_ge(g_begun[n], 1)
                g_groups(dve, set_rows)
                g_tiles(dve, tile)
                dve.wait_ge(g_stored[n], 16 * ET)

            dve.wait_ge(windows_ready, 1)
            ok = dve.value_load(ok_i[0:1, 0:1], min_val=0, max_val=1)
            with dve.If(ok < 1):
                general(0)

            def make_hot(i, u, used, dcol, win, done):
                need(dve, used, i - 2)
                dve.scalar_tensor_tensor(
                    out=hot[:, u % 3, :, :], in0=count_up[:, :].rearrange("p (t n) -> p t n", n=P),
                    scalar=group_start[:, bass.ds(i, 1)],
                    in1=win[:, u, :, dcol:dcol + 1].to_broadcast([P, T, P]),
                    op0=ALU.add, op1=ALU.is_equal).then_inc(done, 1)

            def stage2(k, u):
                nk, nu, n, norms = node_group(k, u, 4)
                if norms:
                    dve.wait_ge(sd2_done, n + 1)
                    need(dve, x1_done, n - 1)
                    dve.reciprocal(rstd[:, nu % 2, 0, :], sd[:, nu % 2, 0, :]).then_inc(rstd2_done, 1)
                if valid(k, u, NG, U):
                    dve.wait_ge(in2[u], loaded_count(k, u))
                    make_hot(U * k + u, u, sum2, DCOL, mwin, hot2)
                if norms:
                    s = nu % 2
                    dve.wait_ge(rstd2_done, n + 1)
                    dve.scalar_tensor_tensor(out=shift[:, s, :].unsqueeze(2), in0=mv[:, s, 0, :, 0:1], scalar=-1.0,
                                             in1=rstd[:, s, 0, :].unsqueeze(2), op0=ALU.mult, op1=ALU.mult)\
                        .then_inc(norm2, 1)
                pk, pu, p, ok = node_group(k, u, 3)
                if ok:
                    s = pu % 2
                    dve.wait_ge(back2, p + 1)
                    need(dve, x1_done, p - 1)
                    dve.tensor_tensor(y[:, s, :, :], xin[:, pu, :, :],
                                      bank[4 + s][:, :].rearrange("p (t d) -> p t d", d=D), ALU.add).then_inc(y2, 1)
                    dve.wait_ge(y2, p + 1)
                    for j in range(T):
                        ins = dve.bn_stats(st[:, s, j, :], y[:, s, j, :])
                    ins.then_inc(st2_done, 1)
                    dve.wait_ge(st2_done, p + 1)
                    dve.sem_inc(wait_passed, 1)
                    for j in range(T):
                        ins = dve.bn_aggr(mv[:, s, 0, j, :], st[:, s, j, :])
                    ins.then_inc(mv2_done, 1)

            each(dve, NG, 4, stage2, U)

            ok1 = dve.value_load(ok_i[0:1, 1:2], min_val=0, max_val=1)
            with dve.If(ok1 < 1):
                general(1)

            dve.wait_ge(norm2, NG)
            dve.memset(mv[:, :, :, :, :], 0.0).then_inc(stats_zeroed, 1)
            dve.wait_ge(stats_zeroed, 1)

            def stage3(k, u):
                outer_k, outer_u, outer, outer_ok = node_group(k, u, 6)
                mid_k, mid_u, mid, mid_ok = node_group(k, u, 5)
                inner_k, inner_u, inner, inner_ok = node_group(k, u, 4)
                m = mid_u % 2
                if mid_ok or outer_ok:
                    dve.wait_ge(sd3, mid + 1)
                    need(dve, out_done, outer - 1)
                    dve.reciprocal(rstd[:, m, :, :], sd[:, m, :, :]).then_inc(rstd3, 1)
                if valid(k, u, NG, U):
                    dve.wait_ge(ewin_loaded[u], 64 * (k + 1))
                    make_hot(U * k + u, u, sum3, ENODE, ewin, hot3)
                if mid_ok or outer_ok:
                    dve.wait_ge(rstd3, mid + 1)
                if outer_ok:
                    dve.scalar_tensor_tensor(out=shift[:, m, :].unsqueeze(2), in0=mv[:, m, 0, :, 0:1],
                                             scalar=-1.0, in1=rstd[:, m, 0, :].unsqueeze(2),
                                             op0=ALU.mult, op1=ALU.mult).then_inc(norm3, 1)
                if mid_ok:
                    need(dve, out_done, mid - 1)
                    for j in range(T):
                        ins = dve.scalar_tensor_tensor(out=y[:, m, j, :], in0=z[:, m, j, :],
                                                       scalar=rstd[:, m, 1, j:j + 1], in1=xb[:, mid_u % 3, j, :],
                                                       op0=ALU.mult, op1=ALU.add)
                    ins.then_inc(y3, 1)
                s = inner_u % 2
                b = bank[6 + s]
                if inner_ok:
                    dve.wait_ge(back3, inner + 1)
                    for j in range(T):
                        ins = dve.bn_stats(st[:, s, j, :], b[:, j * D:(j + 1) * D])
                    ins.then_inc(st3a, 1)
                if mid_ok:
                    dve.wait_ge(y3, mid + 1)
                    for j in range(T):
                        ins = dve.bn_stats(st2[:, m, j, :], y[:, m, j, :])
                    ins.then_inc(st3b, 1)
                if inner_ok:
                    dve.wait_ge(st3a, inner + 1)
                    dve.sem_inc(wait_passed, 1)
                    for j in range(T):
                        ins = dve.bn_aggr(mv[:, s, 1, j, :], st[:, s, j, :])
                if mid_ok:
                    dve.wait_ge(st3b, mid + 1)
                    dve.sem_inc(wait_passed, 1)
                    for j in range(T):
                        ins = dve.bn_aggr(mv[:, s, 0, j, :], st2[:, m, j, :])
                if inner_ok or mid_ok:
                    ins.then_inc(mv3, 1)
                    dve.wait_ge(mv3, inner + 1)
                if inner_ok:
                    for j in range(T):
                        ins = dve.scalar_tensor_tensor(out=z[:, s, j, :], in0=b[:, j * D:(j + 1) * D],
                                                       scalar=mv[:, s, 1, j, 0:1], in1=gamma_sb[:, :],
                                                       op0=ALU.subtract, op1=ALU.mult)
                    ins.then_inc(z3, 1)
                pk, pu, p, ok = node_group(k, u, 2)
                if ok:
                    dve.wait_ge(in3[pu], rows_count(pk, pu))
                    dve.tensor_tensor(xb[:, pu % 3, :, :], xin[:, pu, :, :],
                                      beta_sb[:, :].unsqueeze(1).to_broadcast([P, T, D]), ALU.add).then_inc(xb3, 1)

            each(dve, NG, 6, stage3, U)

        @block.tensor
        def _(pe):
            pe.wait_ge(consts_made, 4)
            pe.wait_ge(lists_f, 1)
            for b, q in enumerate((dst_qf, src_qf, norm_q)):
                for h in range(2):
                    ins = pe.transpose(bank[b][:, h * QR:(h + 1) * QR], q[:, h * P:(h + 1) * P],
                                       ident[0:QR, 0:QR])
            ins.then_inc(lists_turned, 1)
            pe.wait_ge(stats_ready, 1)
            pe.matmul(bank[6][0:1, 0:1], ones_col[0:QR, :], stat_q[:, :], start=True, stop=True)\
                .then_inc(stats_summed, 1)
            for n in range(2):
                pe.wait_ge(marks_ready, n + 1)
                for c in range(NCH):
                    ca = slice(c * CH * A_OF, (c + 1) * CH * A_OF)
                    pe.matmul(bank[3 + n][0:CH * A_OF, 0:CH * 32], a_lt[:, n, ca], ones_bf[:, :],
                              start=(c == 0), stop=False)
                    ins = pe.matmul(bank[3 + n][0:CH * A_OF, 0:CH * 32], a_eq[:, n, ca],
                                    b_lt[:, n, c * CH * 32:(c + 1) * CH * 32], start=False, stop=(c == NCH - 1))
                ins.then_inc(pairs_counted, 1)
            for n in range(2):
                pe.wait_ge(pairs_copied, n + 1)
                for c in range(CH):
                    ins = pe.matmul(bank[5][0:A_OF, n * 32:(n + 1) * 32],
                                    ident[0:CH * A_OF, c * A_OF:(c + 1) * A_OF],
                                    pairs_sb[:, n, c * 32:(c + 1) * 32], start=(c == 0), stop=(c == CH - 1))
            ins.then_inc(counts_added, 1)
            pe.wait_ge(counts_copied, 1)
            pe.matmul(bank[7][0:A_OF, 0:32], steps_a[:, :], counts_sb[:, 1, :], start=True, stop=True)\
                .then_inc(taken_done, 1)
            pe.wait_ge(consts_loaded, 16 * CONSTS)

            def stage1(k, u):
                i = 4 * k + u
                s = u % 2
                if valid(k, u, EG):
                    pe.wait_ge(xg_loaded[u], 64 * (k + 1))
                    need(pe, xg_t_ready, i)
                    for j in range(T):
                        ins = pe.transpose(bank[4][:, j * P:(j + 1) * P], xg[:, u, j, :], ident[:, :])
                    ins.then_inc(xg_turned, 1)
                    pe.wait_ge(hot_types, i + 1)
                    pe.wait_ge(place_marks, i + 1)
                    pe.wait_ge(taken_copied, i + 1)
                    need(pe, coef_ready, i)
                    for j in range(T):
                        ins = pe.matmul(bank[5][:, j * B:(j + 1) * B], type_hot[:, s, j * P:(j + 1) * P],
                                        w_comp_sb[:, :], start=True, stop=True)
                    ins.then_inc(coef_done, 1)
                    for j in range(T + 1):
                        part = bank[6][0:A_OF, 256 + 32 * j:256 + 32 * (j + 1)]
                        ins = pe.matmul(part, ident[0:A_OF, 0:A_OF], taken[:, 1 - s, T, :],
                                        start=True, stop=(j == 0))
                        for m in range(j):
                            ins = pe.matmul(part, a_step[:, s, m, :], b_bf[:, s, m, :],
                                            start=False, stop=(m == j - 1))
                    ins.then_inc(taken_done, 1)
                pk, pu = back(k, u, 1)
                if valid(pk, pu, EG):
                    i = 4 * pk + pu
                    s = pu % 2
                    pe.wait_ge(taken_copied, i + 2)
                    need(pe, placed, i)
                    for j in range(T):
                        pe.matmul(bank[7][:, 64 + j:65 + j], same_tile[:, s, j, :], ones_bf[:, 0:1],
                                  start=True, stop=True)
                        ins = pe.matmul(bank[7][:, P + 32 * j:P + 32 * (j + 1)],
                                        a_ge[:, s, j * P:(j + 1) * P], taken[:, s, j, :], start=True, stop=True)
                    ins.then_inc(looked_up, 1)
                    pe.wait_ge(xg_t_ready, i + 1)
                    for h in range(2):
                        pair = 2 * i + h
                        for half in range(2):
                            for w in range(2):
                                j = 2 * h + w
                                need(pe, chain1, 12 * (pair - 1) + (2 * (4 - SEED) if half == 0 else 12)
                                     - (1 - w))
                                pe.matmul(bank[w + 2 * half][:, :], xg_t[:, s, j * P:(j + 1) * P],
                                          basis_sb[:, 4 * half:4 * half + 4, :], start=True, stop=True)\
                                    .then_inc(products, 1)

            each(pe, EG, 1, stage1)

            def general(n):
                b_key, b_attr, b_msg, b_sum, b_count = bank[0:5]

                def tile(t):
                    pe.wait_ge(g_cols_set[n], t + 1)
                    need(pe, g_added[n], t)
                    ins = pe.transpose(b_key[:, 0:P], g_key_wide[:, :], ident[:, :])
                    if n == 1:
                        ins = pe.transpose(b_attr[0:ED + 1, 0:P], g_attr[:, :], ident[:, :])
                    ins.then_inc(g_turned[n], 1)
                    pe.wait_ge(g_marked[n], t + 1)
                    if n == 1:
                        pe.matmul(b_msg[:, 0:D], g_attr_t[:, :], we_sb[:, :], start=True, stop=True)\
                            .then_inc(g_attr_out, 1)
                        pe.wait_ge(g_msg_made, t + 1)
                    else:
                        pe.wait_ge(g_msg_in, 16 * (t + 1))
                    pe.matmul(b_sum[:, 0:D], g_same[:, :], g_msg[:, :], start=True, stop=True)
                    pe.matmul(b_count[:, 0:1], g_earlier[:, :], ones_col[:, :], start=True, stop=True)\
                        .then_inc(g_combined[n], 1)

                g_tiles(pe, tile)
                pe.wait_ge(g_added[n], ET)

            pe.wait_ge(windows_ready, 1)
            ok = pe.value_load(ok_i[0:1, 0:1], min_val=0, max_val=1)
            with pe.If(ok < 1):
                general(0)

            def stage2(k, u):
                if valid(k, u, NG, U):
                    i = U * k + u
                    pe.wait_ge(in2[u], loaded_count(k, u))
                    need(pe, lhs2, i - 1)
                    for j in range(T):
                        ins = pe.transpose(bank[0 + u % 2][:, j * P:(j + 1) * P], xin[:, u, j, :], ident[:, :])
                    ins.then_inc(turned2, 1)
                pk, pu, p, ok = node_group(k, u, 1)
                if ok:
                    s = pu % 2
                    pe.wait_ge(hot2, p + 1)
                    need(pe, act2, p - 1)
                    pe.wait_ge(lhs2, p + 1)
                    pe.matmul(bank[2 + s][:, :], loop_sb[:, :], lhs_t[:, s, :], start=True, stop=False,
                              skip_group_check=True)
                    for j in range(T):
                        ins = pe.matmul(bank[2 + s][:, j * P:(j + 1) * P], mwin[:, pu, j, 0:D],
                                        hot[:, pu % 3, j, :], start=False, stop=(j == T - 1),
                                        skip_group_check=True)
                    ins.then_inc(sum2, 1)
                pk, pu, p, ok = node_group(k, u, 2)
                if ok:
                    s = pu % 2
                    need(pe, y2, p - 1)
                    pe.wait_ge(act2, p + 1)
                    for j in range(T):
                        ins = pe.transpose(bank[4 + s][:, j * P:(j + 1) * P], act_t[:, s, j * P:(j + 1) * P],
                                           ident[:, :])
                    ins.then_inc(back2, 1)

            each(pe, NG, 2, stage2, U)

            ok1 = pe.value_load(ok_i[0:1, 1:2], min_val=0, max_val=1)
            with pe.If(ok1 < 1):
                general(1)

            def stage3(k, u):
                pk, pu, p, ok = node_group(k, u, 1)
                if ok:
                    b = bank[0 + pu % 2]
                    need(pe, lhs3, p - 1)
                    pe.wait_ge(in3[pu], rows_count(pk, pu))
                    pe.wait_ge(ea3_copied, p + 1)
                    pe.matmul(b[:, :], we_sb[:, :], ea_t[:, pu % 2, :], start=True, stop=False,
                              skip_group_check=True)
                    for j in range(T):
                        pe.matmul(b[:, j * P:(j + 1) * P], xin[:, pu, j, :], self_diag[:, :],
                                  start=False, stop=False, skip_group_check=True)
                    pe.wait_ge(xg3_loaded[pu % 3], 64 * (U // 3 * pk + pu // 3 + 1))
                    for j in range(T):
                        ins = pe.matmul(b[:, j * P:(j + 1) * P], xg[:, pu % 3, j, :], hot[:, pu % 3, j, :],
                                        start=False, stop=(j == T - 1), skip_group_check=True)
                    ins.then_inc(sum3, 1)
                pk, pu, p, ok = node_group(k, u, 2)
                ps = pu % 2
                if ok:
                    need(pe, act3, p - 1)
                    pe.wait_ge(lhs3, p + 1)
                    pe.matmul(bank[3 + ps][:, :], w1_sb[:, :], lhs_t[:, ps, :], start=True, stop=True)\
                        .then_inc(mid3, 1)
                if valid(k, u, NG, U):
                    i = U * k + u
                    need(pe, ea3_copied, i)
                    pe.wait_ge(hot3, i + 1)
                    for j in range(T):
                        ins = pe.matmul(bank[2][0:ED + 1, j * P:(j + 1) * P], ewin[:, u, j, 0:ED + 1],
                                        hot[:, u % 3, j, :], start=True, stop=True)
                    ins.then_inc(ea3, 1)
                if ok:
                    need(pe, o3_copied, p)
                    pe.wait_ge(act3, p + 1)
                    pe.matmul(bank[5][:, :], w2_sb[:, :], act_t[:, ps, :], start=True, stop=True).then_inc(o3, 1)
                pk, pu, p, ok = node_group(k, u, 3)
                if ok:
                    ps = pu % 2
                    need(pe, z3, p - 1)
                    pe.wait_ge(o3_copied, p + 1)
                    for j in range(T):
                        ins = pe.transpose(bank[6 + ps][:, j * P:(j + 1) * P], out_t[:, ps, j * P:(j + 1) * P],
                                           ident[:, :])
                    ins.then_inc(back3, 1)

            each(pe, NG, 3, stage3, U)

        @block.scalar
        def _(act):
            def stage1(k, u):
                i = 4 * k + u
                s = u % 2
                if valid(k, u, EG):
                    act.wait_ge(xg_turned, i + 1)
                    need(act, products, 8 * (i - 1))
                    act.activation(xg_t[:, s, :], bank[4][:, :], ACT.Copy).then_inc(xg_t_ready, 1)
                    act.wait_ge(taken_done, i + 2)
                    need(act, looked_up, i - 1)
                    act.activation(taken[:, s, :, :],
                                   bank[6][0:A_OF, 256:256 + 32 * (T + 1)].rearrange("a (t b) -> a t b", b=32),
                                   ACT.Copy).then_inc(taken_copied, 1)
                pk, pu = back(k, u, 1)
                if valid(pk, pu, EG):
                    i = 4 * pk + pu
                    s = pu % 2
                    act.wait_ge(coef_ready, i + 1)
                    for j in range(T):
                        pair = 2 * i + j // 2
                        w = j % 2
                        act.wait_ge(products, 4 * pair + w + 1)
                        need(act, seeds_added, i * T + j - 1)
                        for b in range(SEED):
                            ins = act.activation(seeds[:, w, b, :], bank[w][:, b * D:(b + 1) * D], ACT.Copy,
                                                 scale=coef[:, s, j, b:b + 1])
                        ins.then_inc(seeds_ready, 1)

            each(act, EG, 1, stage1)

            act.wait_ge(consts_loaded, 16 * CONSTS)

            def normalise(u, m, done):
                for j in range(T):
                    ins = act.activation(res[:, u % 2, j, :], y[:, u % 2, j, :], ACT.Identity,
                                         scale=rstd[:, m, 0, j:j + 1], bias=shift[:, m, j:j + 1])
                ins.then_inc(done, 1)

            def stage2(k, u):
                if valid(k, u, NG, U):
                    i = U * k + u
                    need(act, sum2, i - 1)
                    act.wait_ge(turned2, i + 1)
                    act.activation(lhs_t[:, u % 2, :], bank[0 + u % 2][:, :], ACT.Copy).then_inc(lhs2, 1)
                pk, pu, p, ok = node_group(k, u, 5)
                if ok:
                    act.wait_ge(x1_done, p + 1)
                    for rows, tiles in rows_and_tiles(x1_rows, res[:, pu % 2, :, :], pk, pu):
                        act.dma_start(rows, tiles).then_inc(x1_stored[pu % 2], 16)
                pk, pu, p, ok = node_group(k, u, 4)
                if ok:
                    need(act, x1_stored[pu % 2], stored_before(pk, pu))
                    act.wait_ge(norm2, p + 1)
                    normalise(pu, pu % 2, x1_done)
                pk, pu, p, ok = node_group(k, u, 1)
                if ok:
                    s = pu % 2
                    need(act, back2, p - 1)
                    act.wait_ge(sum2, p + 1)
                    act.activation(act_t[:, s, :], bank[2 + s][:, :], ACT.Relu, bias=h_bias_sb[:, 0:1])\
                        .then_inc(act2, 1)
                pk, pu, p, ok = node_group(k, u, 3)
                if ok:
                    s = pu % 2
                    need(act, rstd2_done, p - 1)
                    act.wait_ge(mv2_done, p + 1)
                    act.activation(sd[:, s, 0, :].unsqueeze(2), mv[:, s, 0, :, 1:2], ACT.Sqrt, bias=ln_eps[:, 0:1])\
                        .then_inc(sd2_done, 1)

            each(act, NG, 5, stage2, U)
            for s in range(2):
                act.wait_ge(x1_stored[s], 16 * (NG // 2 + s))

            def stage3(k, u):
                pk, pu, p, ok = node_group(k, u, 7)
                if ok:
                    act.wait_ge(out_done, p + 1)
                    for rows, tiles in rows_and_tiles(out, res[:, pu % 2, :, :], pk, pu):
                        act.dma_start(rows, tiles).then_inc(out_stored[pu % 2], 16)
                pk, pu, p, ok = node_group(k, u, 1)
                if ok:
                    s = pu % 2
                    need(act, mid3, p - 1)
                    act.wait_ge(sum3, p + 1)
                    act.activation(lhs_t[:, s, :], bank[0 + s][:, :], ACT.Copy).then_inc(lhs3, 1)
                pk, pu, p, ok = node_group(k, u, 2)
                s = pu % 2
                if ok:
                    need(act, o3, p - 1)
                    act.wait_ge(mid3, p + 1)
                    act.activation(act_t[:, s, :], bank[3 + s][:, :], ACT.Relu, bias=b1_sb[:, 0:1])\
                        .then_inc(act3, 1)
                if valid(k, u, NG, U):
                    i = U * k + u
                    need(act, sum3, i - 1)
                    act.wait_ge(ea3, i + 1)
                    act.activation(ea_t[:, u % 2, :], bank[2][0:ED + 1, :], ACT.Copy).then_inc(ea3_copied, 1)
                if ok:
                    need(act, back3, p - 1)
                    act.wait_ge(o3, p + 1)
                    act.activation(out_t[:, s, :], bank[5][:, :], ACT.Identity, bias=b2_sb[:, 0:1])\
                        .then_inc(o3_copied, 1)
                pk, pu, p, inner_ok = node_group(k, u, 4)
                s = pu % 2
                if inner_ok or node_group(k, u, 5)[3]:
                    need(act, rstd3, p - 1)
                    act.wait_ge(mv3, p + 1)
                    act.activation(sd[:, s, :, :].unsqueeze(3), mv[:, s, :, :, 1:2], ACT.Sqrt, bias=ln_eps[:, 0:1])\
                        .then_inc(sd3, 1)
                pk, pu, p, ok = node_group(k, u, 6)
                if ok:
                    need(act, out_stored[pu % 2], stored_before(pk, pu))
                    act.wait_ge(norm3, p + 1)
                    normalise(pu, (pu + 1) % 2, out_done)

            each(act, NG, 7, stage3, U)


_INS = ['x', 'src', 'dst', 'edge_attr_32', 'edge_type_32', 'edge_weight1', 'L0_gnn_weight', 'L0_gnn_w_comp',
        'L0_gnn_loop_weight', 'L0_gnn_h_bias', 'L1_gnn_We', 'L1_gnn_be', 'L1_gnn_W1', 'L1_gnn_b1', 'L1_gnn_W2',
        'L1_gnn_b2', 'L1_gnn_eps', 'L1_gnn_gamma', 'L1_gnn_beta']


def kernel(**inputs):
    import numpy as _np
    import concourse.bacc as _bacc
    from concourse import mybir as _mybir
    from concourse.bass_utils import run_bass_kernel_spmd as _run

    nc = _bacc.Bacc("TRN2", target_bir_lowering=False, num_devices=1)
    arrays, args = {}, []
    for name in _INS:
        a = _np.ascontiguousarray(inputs[name])
        arrays[f"in_{name}"] = a
        args.append(nc.dram_tensor(f"in_{name}", a.shape, _mybir.dt.from_np(a.dtype), kind="ExternalInput").ap())
    out = nc.dram_tensor("out_0", arrays["in_x"].shape, _mybir.dt.float32, kind="ExternalOutput").ap()
    gnn_two_layers(nc, *args, out)
    r = _run(nc, [arrays], core_ids=[0])
    return r.results[0]["out_0"]
```

```python
import concourse.bass as bass
from concourse import mybir
from contextlib import ExitStack


def gnn_two_layers(
    nc: bass.Bass,
    x: bass.AP,
    src: bass.AP,
    dst: bass.AP,
    edge_attr: bass.AP,
    edge_type: bass.AP,
    edge_weight: bass.AP,
    basis: bass.AP,
    w_comp: bass.AP,
    loop_weight: bass.AP,
    h_bias: bass.AP,
    We: bass.AP,
    be: bass.AP,
    W1: bass.AP,
    b1: bass.AP,
    W2: bass.AP,
    b2: bass.AP,
    eps: bass.AP,
    gamma: bass.AP,
    beta: bass.AP,
    out: bass.AP,
):
    f32 = mybir.dt.float32
    i32 = mybir.dt.int32
    bf16 = mybir.dt.bfloat16
    ALU = mybir.AluOpType
    ACT = mybir.ActivationFunctionType
    AX = mybir.AxisListType

    P = 128
    N, D = x.shape
    E = src.shape[0]
    ED = edge_attr.shape[1]
    R, B = w_comp.shape
    T = 4
    GP = T * P
    NG = -(-N // GP)
    NT = NG * T
    LAST = (NG - 1) * GP
    LAST_T = (N - LAST) // P
    LAST_R = N - LAST - LAST_T * P
    EG = -(-E // GP)
    ET = EG * T
    EROWS = (ET + 1) * P
    FULL = E // P
    REST = E - FULL * P
    NONE = 1 << 16
    AHEAD = 3
    ACT_TILES = 2
    LN_EPS = 1e-5
    MC = D + 4
    DCOL = D
    ONE, ENODE, EFROM, EC = ED, ED + 1, ED + 2, ED + 4
    QR = ET // 2
    QC = 2 * P
    QREST = E - (QR - 1) * QC
    A_OF = -(-(N // P + 1) // 32)
    CH = 7
    NCH = ET // CH
    SKIP = 1 << 20
    SEED = 3
    CHAIN = 2 * (B - SEED)
    HALF = T // 2
    U1 = 4
    U = 6

    msg_rows = nc.dram_tensor("msg_rows", [EROWS + NT * P, MC], f32).ap()
    edge_rows = nc.dram_tensor("edge_rows", [EROWS + NT * P, EC], f32).ap()
    sum_rows = nc.dram_tensor("sum_rows", [NT * P, D], f32).ap()
    x1_rows = nc.dram_tensor("x1_rows", [N, D], f32).ap()
    counts_dram = nc.dram_tensor("counts_dram", [2, A_OF, 32], f32).ap()

    ctx = ExitStack()
    with ctx:
        def sb(name, shape, dt=f32):
            return ctx.enter_context(nc.sbuf_tensor(name, shape, dt))

        def sem(name):
            return ctx.enter_context(nc.semaphore(name))

        def sems(name, n):
            return [sem(f"{name}{i}") for i in range(n)]

        basis_sb = sb("basis_sb", [P, B, D])
        w_comp_sb = sb("w_comp_sb", [R, B])
        loop_sb = sb("loop_sb", [P, D])
        we_sb = sb("we_sb", [ED + 1, D])
        w1_sb = sb("w1_sb", [P, D])
        w2_sb = sb("w2_sb", [P, D])
        h_bias_sb = sb("h_bias_sb", [P, 1])
        b1_sb = sb("b1_sb", [P, 1])
        b2_sb = sb("b2_sb", [P, 1])
        gamma_sb = sb("gamma_sb", [P, D])
        beta_sb = sb("beta_sb", [P, D])
        eps_sb = sb("eps_sb", [P, 1])
        eps1_sb = sb("eps1_sb", [P, 1])
        ident = sb("ident", [P, P])
        self_diag = sb("self_diag", [P, P])
        count_up = sb("count_up", [P, GP])
        part_no = sb("part_no", [P, 1])
        group_start = sb("group_start", [P, NG])
        ones_bf = sb("ones_bf", [P, CH * 32], bf16)
        ones_col = sb("ones_col", [P, 1])
        dst_q = sb("dst_q", [QR, QC], i32)
        next_q = sb("next_q", [QR, QC], i32)
        src_q = sb("src_q", [QR, QC], i32)
        norm_q = sb("norm_q", [QR, QC])
        dst_qf = sb("dst_qf", [QR, QC])
        src_qf = sb("src_qf", [QR, QC])
        next_qf = sb("next_qf", [QR, QC])
        falls_q = sb("falls_q", [QR, QC])
        stat_q = sb("stat_q", [QR, 1])
        dst_t = sb("dst_t", [P, ET + 1])
        src_t = sb("src_t", [P, ET + 1])
        src_row = sb("src_row", [P, ET], i32)
        dst_row = sb("dst_row", [P, ET + 1], i32)
        norm_t = sb("norm_t", [P, ET])
        skip_t = sb("skip_t", [P, ET])
        node_i = sb("node_i", [P, 2, ET], i32)
        a_i = sb("a_i", [P, 2, ET], i32)
        b_i = sb("b_i", [P, 2, ET], i32)
        b_m = sb("b_m", [P, 2, ET], i32)
        a_f = sb("a_f", [P, 2, ET])
        b_f = sb("b_f", [P, 2, ET])
        tile_f = sb("tile_f", [P, ET])
        pairs_sb = sb("pairs_sb", [CH * A_OF, 2, CH * 32])
        counts_sb = sb("counts_sb", [A_OF, 2, 32])
        count_row = sb("count_row", [1, 2, A_OF * 32])
        stat_row = sb("stat_row", [1, 1])
        sums_start = sb("sums_start", [1, 2, NT])
        win_d = sb("win_d", [1, 2, NT])
        win_g = sb("win_g", [1, 2, NT])
        most = sb("most", [1, 2])
        fits = sb("fits", [1, 2])
        no_falls = sb("no_falls", [1, 1])
        win_row = sb("win_row", [1, 2, NT], i32)
        ok_i = sb("ok_i", [1, 2], i32)
        edge_out = sb("edge_out", [P, ET + 1, EC])
        pad_msgs = sb("pad_msgs", [P, MC])
        pad_edges = sb("pad_edges", [P, EC])
        steps_a = sb("steps_a", [A_OF, A_OF])
        before = sb("before", [P, P])
        a_from = sb("a_from", [A_OF, 1])
        srcs = sb("srcs", [P, 4, GP], i32)
        tiles_bc = sb("tiles_bc", [P, 2, GP], i32)
        same_tile = sb("same_tile", [P, 2, T, P], bf16)
        a_ge = sb("a_ge", [A_OF, 2, GP])
        a_hot = sb("a_hot", [P, 2, T, A_OF + 1], bf16)
        b_bf = sb("b_bf", [P, 2, T, 32], bf16)
        a_step = sb("a_step", [P, 2, T, A_OF], bf16)
        b_hot = sb("b_hot", [P, 4, T, 32])
        taken = sb("taken", [A_OF, 2, T + 1, 32])
        looked = sb("looked", [P, 2, T, 32])
        place_f = sb("place_f", [P, 2, T])
        place_s = sb("place_s", [P, 2, T])
        place_t = sb("place_t", [P, ET], i32)
        place_now = sb("place_now", [P, 2, T], i32)
        edge_now = sb("edge_now", [P, 2, T, EC])
        types = sb("types", [R, 4, GP], i32)
        type_hot = sb("type_hot", [R, 2, GP])
        src_now = sb("src_now", [P, 4, T], i32)
        xg = sb("xg", [P, 4, T, D])
        xg_t = sb("xg_t", [P, 2, GP])
        coef = sb("coef", [P, 2, T, B])
        seeds = sb("seeds", [P, T, SEED, D])
        seed_sum = sb("seed_sum", [P, T, D])
        msgs = sb("msgs", [P, 2, T, MC])
        marks = sb("marks", [P, 2, ET * (2 * A_OF + 32)], bf16)
        a_eq = marks[:, :, 0:ET * A_OF]
        a_lt = marks[:, :, ET * A_OF:2 * ET * A_OF]
        b_lt = marks[:, :, 2 * ET * A_OF:]
        reused = marks[:, :, :].rearrange("p l c -> p (l c)").bitcast(f32)
        parts, at = [], 0
        for slots, cols in ((U, D), (3, P), (3, D), (2, D), (1, MC), (1, EC), (U, MC)):
            size = slots * T * cols
            parts.append(reused[:, at:at + size].rearrange("p (s t c) -> p s t c", s=slots, t=T))
            at += size
        xin, hot, y, res, g_rows, g_edges, mwin = parts
        at -= U * T * MC
        for slots, cols in ((U, EC), (2, D), (3, D)):
            size = slots * T * cols
            parts.append(reused[:, at:at + size].rearrange("p (s t c) -> p s t c", s=slots, t=T))
            at += size
        ewin, z, xb = parts[-3:]
        g_rows, g_edges = g_rows[:, 0], g_edges[:, 0]
        lhs_t = sb("lhs_t", [P, 2, GP])
        act_t = sb("act_t", [P, 2, GP])
        out_t = sb("out_t", [P, 2, GP])
        ea_t = sb("ea_t", [ED + 1, 2, GP])
        st = sb("st", [P, 2, T, 6])
        st2 = sb("st2", [P, 2, T, 6])
        mv = sb("mv", [P, 2, 2, T, 2])
        sd = sb("sd", [P, 2, 2, T])
        rstd = sb("rstd", [P, 2, 2, T])
        shift = sb("shift", [P, 2, T])
        ln_eps = sb("ln_eps", [P, 1])

        g_node0 = sb("g_node0", [P, T])
        g_key = sb("g_key", [P, 1])
        g_key_wide = sb("g_key_wide", [P, P])
        g_same = sb("g_same", [P, P])
        g_earlier = sb("g_earlier", [P, P])
        g_attr = sb("g_attr", [P, ED + 1])
        g_attr_t = sb("g_attr_t", [ED + 1, P])
        g_from = sb("g_from", [P, 1], i32)
        g_x = sb("g_x", [P, D])
        g_msg = sb("g_msg", [P, D])
        g_again = sb("g_again", [P, 1])
        g_at = sb("g_at", [P, 1], i32)
        g_sum = sb("g_sum", [P, MC])

        bank = [ctx.enter_context(nc.psum_tensor(f"bank{i}", [P, GP], f32)) for i in range(8)]

        first_half, second_half, turned_bank = bank[0:4], bank[4:6], bank[6]
        at_coef, at_taken, at_ranks, at_looked = 0, T * B, T * B + 32 * (T + 1), 2 * P
        coef_bank = bank[7][:, at_coef:at_coef + T * B]
        taken_bank = bank[7][0:A_OF, at_taken:at_ranks]
        ranks_bank = bank[7][:, at_ranks:at_ranks + T]
        looked_bank = bank[7][:, at_looked:at_looked + 32 * T]

        wait_passed = sem("wait_passed")
        consts_loaded = sem("consts_loaded")
        lists_loaded = sem("lists_loaded")
        attr_loaded = sem("attr_loaded")
        pads_set = sem("pads_set")
        consts_made = sem("consts_made")
        zeroed = sem("zeroed")
        dve0 = sem("dve0")
        lists_f = sem("lists_f")
        lists_turned = sem("lists_turned")
        lists_ready = sem("lists_ready")
        stats_ready = sem("stats_ready")
        place_marks = sem("place_marks")
        taken_done = sem("taken_done")
        taken_copied = sem("taken_copied")
        tiles_shifted = sem("tiles_shifted")
        a_marked = sem("a_marked")
        looked_up = sem("looked_up")
        looked_picked = sem("looked_picked")
        looked_summed = sem("looked_summed")
        hots_marked = sem("hots_marked")
        windows0 = sem("windows0")
        ranks_added = sem("ranks_added")
        placed = sem("placed")
        edges_now = sem("edges_now")
        edges_scattered = sems("edges_scattered", 2)
        stats_summed = sem("stats_summed")
        marks_ready = sem("marks_ready")
        pairs_counted = sem("pairs_counted")
        pairs_copied = sem("pairs_copied")
        counts_added = sem("counts_added")
        counts_copied = sem("counts_copied")
        counts_out = sem("counts_out")
        counts_in = sem("counts_in")
        windows_ready = sem("windows_ready")
        edge_cols = sem("edge_cols")
        pads_stored = sem("pads_stored")
        g_begun = sems("g_begun", 2)
        g_rows_set = sems("g_rows_set", 2)
        g_rows_out = sems("g_rows_out", 2)
        g_msg_in = sem("g_msg_in")
        g_from_set = sem("g_from_set")
        g_x_in = sem("g_x_in")
        g_cols_set = sems("g_cols_set", 2)
        g_turned = sems("g_turned", 2)
        g_compared = sems("g_compared", 2)
        g_marked = sems("g_marked", 2)
        g_attr_out = sem("g_attr_out")
        g_msg_made = sem("g_msg_made")
        g_combined = sems("g_combined", 2)
        g_again_set = sems("g_again_set", 2)
        g_at_set = sems("g_at_set", 2)
        g_fetched = sems("g_fetched", 2)
        g_added = sems("g_added", 2)
        g_stored = sems("g_stored", 2)
        lists1_loaded = sems("lists1_loaded", 4)
        src_placed = sem("src_placed")
        xg_loaded = sems("xg_loaded", 4)
        hot_types = sem("hot_types")
        xg_turned = sem("xg_turned")
        xg_t_ready = sem("xg_t_ready")
        coef_done = sem("coef_done")
        coef_ready = sem("coef_ready")
        products = sem("products")
        seeds_ready = sem("seeds_ready")
        seeds_half = sem("seeds_half")
        seeds_added = sem("seeds_added")
        chain1 = sem("chain1")
        msgs_stored = sems("msgs_stored", 2)
        in2 = sems("in2_", U)
        mwin_loaded = sems("mwin_loaded", U)
        hot2 = sem("hot2")
        turned2 = sem("turned2")
        lhs2 = sem("lhs2")
        sum2 = sem("sum2")
        act2 = sem("act2")
        back2 = sem("back2")
        y2 = sem("y2")
        st2_done = sem("st2_done")
        mv2_done = sem("mv2_done")
        sd2_done = sem("sd2_done")
        rstd2_done = sem("rstd2_done")
        norm2 = sem("norm2")
        x1_halved = sem("x1_halved")
        x1_done = sem("x1_done")
        x1_stored = sems("x1_stored", 2)
        stats_zeroed = sem("stats_zeroed")
        in3 = sems("in3_", U)
        ewin_loaded = sems("ewin_loaded", U)
        xg3_loaded = sems("xg3_loaded", 3)
        hot3 = sem("hot3")
        ea3 = sem("ea3")
        ea3_copied = sem("ea3_copied")
        sum3 = sem("sum3")
        lhs3 = sem("lhs3")
        mid3 = sem("mid3")
        act3 = sem("act3")
        o3 = sem("o3")
        o3_copied = sem("o3_copied")
        back3 = sem("back3")
        xb3 = sem("xb3")
        xb3_rest = sem("xb3_rest")
        st3a = sem("st3a")
        mv3 = sem("mv3")
        sd3 = sem("sd3")
        rstd3 = sem("rstd3")
        z3 = sem("z3")
        y3 = sem("y3")
        st3b = sem("st3b")
        norm3 = sem("norm3")
        out_done = sem("out_done")
        out_stored = sems("out_stored", 2)

        def need(eng, s, value):
            if not (isinstance(value, int) and value <= 0):
                eng.wait_ge(s, value)

        def each(eng, count, more, body, U=U1, ahead=0):
            peeled = 1 if more <= U - 1 - (U == 4) else 2
            end = (count - 1 - ahead) // U
            for i in range(U * peeled):
                body(i // U, i % U)
            with eng.Fori(peeled, end) as k:
                for u in range(U):
                    body(k, u)
            for i in range(U * end, count + more):
                body(i // U, i % U)

        def back(k, u, d, U=U1):
            return k + (u - d) // U, (u - d) % U

        def valid(k, u, count, U=U1):
            return not isinstance(k, int) or 0 <= U * k + u < count

        def node_group(k, u, lag):
            k, u = back(k, u, lag, U)
            return k, u, U * k + u, valid(k, u, NG, U)

        def node0(k, u):
            return (U * k + u) * GP

        def last(k, u):
            return isinstance(k, int) and U * k + u == NG - 1

        def rows_count(k, u):
            return 16 * (k + 1) + 16 * last(k, u)

        def stored_before(k, u):
            return 16 * (U // 2 * k + u // 2)

        def rows_and_tiles(dram, tiles, k, u):
            if last(k, u):
                mid = LAST + LAST_T * P
                return [(tiles_of(dram[LAST:mid, :]), tiles[:, 0:LAST_T, :]),
                        (dram[mid:N, :], tiles[0:LAST_R, LAST_T, :])]
            return [(tiles_of(dram[bass.ds(node0(k, u), GP), :]), tiles)]

        def tiles_of(rows):
            return rows.rearrange("(j p) d -> p j d", p=P)

        def load_nodes(eng, k, u, dram, done):
            for rows, tiles in rows_and_tiles(dram, xin[:, u, :, :], k, u):
                eng.dma_start(tiles, rows).then_inc(done, 16)

        g_table = (msg_rows, sum_rows)
        g_cols = (MC, D)
        g_base = (EROWS, 0)
        g_keys = (dst_t, src_t)

        def g_tiles(eng, body):
            body(0)
            with eng.Fori(1, ET) as t:
                body(t)

        def g_groups(eng, body):
            body(0)
            with eng.Fori(1, NG) as g:
                body(g)

        block = ctx.enter_context(nc.Block())

        CONSTS = 13

        @block.sync
        def _(sp):
            flat = (QR - 1) * QC
            sp.wait_ge(pads_set, 1)
            for q, a, n in ((dst_q, dst, E), (src_q, src, E), (next_q, dst[1:E], E - 1),
                            (norm_q, edge_weight.rearrange("e o -> (e o)"), E)):
                sp.dma_start(q[0:QR - 1, :], a[0:flat].rearrange("(q c) -> q c", c=QC)).then_inc(lists_loaded, 16)
                sp.dma_start(q[QR - 1:QR, 0:n - flat],
                             a[flat:n].rearrange("(q c) -> q c", q=1)).then_inc(lists_loaded, 16)
            sp.dma_start(basis_sb[:, :, :], basis.rearrange("b d f -> d b f")).then_inc(consts_loaded, 16)
            sp.dma_start(w_comp_sb[:, :], w_comp).then_inc(consts_loaded, 16)
            sp.dma_start(loop_sb[:, :], loop_weight).then_inc(consts_loaded, 16)
            sp.dma_start(we_sb[0:ED, :], We).then_inc(consts_loaded, 16)
            sp.dma_start(we_sb[ED:ED + 1, :], be.rearrange("(o d) -> o d", o=1)).then_inc(consts_loaded, 16)
            sp.dma_start(w1_sb[:, :], W1).then_inc(consts_loaded, 16)
            sp.dma_start(w2_sb[:, :], W2).then_inc(consts_loaded, 16)
            for c, a in ((h_bias_sb, h_bias), (b1_sb, b1), (b2_sb, b2)):
                sp.dma_start(c[:, :], a.rearrange("(d o) -> d o", o=1)).then_inc(consts_loaded, 16)
            for c, a in ((gamma_sb, gamma), (beta_sb, beta), (eps_sb, eps)):
                sp.dma_start(c[:, :], a.partition_broadcast(P)).then_inc(consts_loaded, 16)
            sp.wait_ge(zeroed, 1)
            sp.dma_start(edge_out[:, 0:FULL, 0:ED],
                         edge_attr[0:FULL * P, :].rearrange("(t p) c -> p t c", p=P)).then_inc(attr_loaded, 16)
            sp.dma_start(edge_out[0:REST, FULL, 0:ED], edge_attr[FULL * P:E, :]).then_inc(attr_loaded, 16)

            sp.wait_ge(edge_cols, 1)
            sp.dma_start(edge_rows[E:E + P, :], pad_edges[:, :]).then_inc(pads_stored, 16)
            sp.dma_start(edge_rows[E + P:EROWS, :], pad_edges[0:EROWS - E - P, :]).then_inc(pads_stored, 16)
            sp.wait_ge(counts_copied, 1)
            sp.dma_start(counts_dram.rearrange("l a b -> a l b"), counts_sb[:, :, :]).then_inc(counts_out, 16)
            sp.wait_ge(counts_out, 16)
            sp.dma_start(count_row[:, :, :], counts_dram.rearrange("(o l) a b -> o l (a b)", o=1))\
                .then_inc(counts_in, 16)

            def load_types(k, u):
                i = 4 * k + u
                need(sp, hot_types, i - 3)
                n = E - i * GP if isinstance(i, int) and i == EG - 1 else GP
                e0 = i * GP
                sp.dma_start(types[:, u, 0:n],
                             edge_type[bass.ds(e0, n)].partition_broadcast(R)).then_inc(lists1_loaded[u], 16)
                need(sp, tiles_shifted, i - 3)
                need(sp, a_marked, i - 3)
                sp.dma_start(srcs[:, u, 0:n],
                             src[bass.ds(e0, n)].partition_broadcast(P)).then_inc(lists1_loaded[u], 16)

            def store_msgs(k, u):
                i = 4 * k + u
                sp.wait_ge(chain1, 2 * CHAIN * (i + 1))
                sp.dma_start(tiles_of(msg_rows[bass.ds(i * GP, GP), :]), msgs[:, u % 2, :, :])\
                    .then_inc(msgs_stored[u % 2], 16)

            def stage1(k, u):
                if valid(k, u, EG):
                    load_types(k, u)
                if valid(*back(k, u, 4), EG):
                    store_msgs(*back(k, u, 4))
            each(sp, EG, 4, stage1)
            sp.dma_start(msg_rows[EROWS - P:EROWS, :], pad_msgs[:, :]).then_inc(pads_stored, 16)

            sp.wait_ge(windows_ready, 1)
            sp.wait_ge(pads_stored, 48)
            for s in range(2):
                sp.wait_ge(msgs_stored[s], 16 * len(range(s, EG, 2)))

            def general(n):
                def set_rows(g):
                    sp.wait_ge(g_rows_set[n], g + 1)
                    if n == 0:
                        sp.dma_start(tiles_of(msg_rows[bass.ds(EROWS + g * GP, GP), :]), g_rows[:, :, :])\
                            .then_inc(g_rows_out[n], 16)
                    else:
                        sp.dma_start(tiles_of(edge_rows[bass.ds(EROWS + g * GP, GP), :]), g_edges[:, :, :])\
                            .then_inc(g_rows_out[n], 16)
                        sp.dma_start(tiles_of(sum_rows[bass.ds(g * GP, GP), :]), g_rows[:, :, 0:D])\
                            .then_inc(g_rows_out[n], 16)

                def load_msgs(t):
                    need(sp, g_stored[n], 16 * t)
                    sp.dma_start(g_msg[:, :], msg_rows[bass.ds(t * P, P), 0:D]).then_inc(g_msg_in, 16)

                g_groups(sp, set_rows)
                if n == 0:
                    g_tiles(sp, load_msgs)
                sp.wait_ge(g_rows_out[n], 16 * (n + 1) * NG)
                sp.wait_ge(g_stored[n], 16 * ET)

            ok = sp.value_load(ok_i[0:1, 0:1], min_val=0, max_val=1)
            with sp.If(ok < 1):
                general(0)

            def load_windows(n, i, win, rows, done):
                _, starts = nc.values_load_multi_w_load_instructions(
                    win_row[0:1, n, bass.ds(i * T, T)], engines=[sp.engine],
                    min_val=0, max_val=EROWS + NT * P - P,
                    skip_runtime_bounds_check_because="prefix counts of at most E edges, or a node tile's row")
                for j in range(T):
                    sp.dma_start(win[:, j, :], rows[bass.ds(starts[j], P), :]).then_inc(done, 16)

            def load2(k, u):
                i = U * k + u
                need(sp, sum2, i - U + 1)
                load_windows(0, i, mwin[:, u, :, :], msg_rows, mwin_loaded[u])

            each(sp, NG, 0, load2, U)

            for s in range(2):
                sp.wait_ge(x1_stored[s], 16 * (NG // 2 + s))
                sp.wait_ge(edges_scattered[s], 64 * len(range(s, EG, 2)))

            ok = sp.value_load(ok_i[0:1, 1:2], min_val=0, max_val=1)
            with sp.If(ok < 1):
                general(1)

            def load3(k, u):
                i = U * k + u
                need(sp, sum3, i - U + 1)
                need(sp, xb3, i - U + 1)
                need(sp, xb3_rest, i - U + 1)
                load_windows(1, i, ewin[:, u, :, :], edge_rows, ewin_loaded[u])
                load_nodes(sp, k, u, x1_rows, in3[u])

            each(sp, NG, 0, load3, U)
            for s in range(2):
                sp.wait_ge(out_stored[s], 16 * (NG // 2 + s))

        @block.gpsimd
        def _(pool):
            pool.memset(edge_out[:, FULL:ET + 1, :], 0.0).then_inc(zeroed, 1)
            pool.memset(ident[:, :], 0.0).then_inc(consts_made, 1)
            pool.wait_ge(consts_made, 1)
            pool.affine_select(out=ident[:, :], in_=ident[:, :], compare_op=ALU.not_equal, fill=1.0,
                               base=0, pattern=[[-1, P]], channel_multiplier=1)
            pool.iota(count_up[:, :], pattern=[[1, GP]], base=0, channel_multiplier=0,
                      allow_small_or_imprecise_dtypes=True)
            pool.iota(part_no[:, :], pattern=[[1, 1]], base=0, channel_multiplier=1,
                      allow_small_or_imprecise_dtypes=True)
            pool.iota(group_start[:, :], pattern=[[GP, NG]], base=0, channel_multiplier=0,
                      allow_small_or_imprecise_dtypes=True)
            pool.iota(sums_start[:, :, :], pattern=[[0, 2], [P, NT]], base=EROWS, channel_multiplier=0,
                      allow_small_or_imprecise_dtypes=True)
            pool.iota(g_node0[:, :], pattern=[[P, T]], base=0, channel_multiplier=1,
                      allow_small_or_imprecise_dtypes=True)
            pool.iota(a_from[:, :], pattern=[[1, 1]], base=0, channel_multiplier=32 * P,
                      allow_small_or_imprecise_dtypes=True)
            pool.memset(before[:, :], 0.0)
            pool.memset(pad_edges[:, :], 0.0)
            pool.memset(a_hot[:, :, :, 0:1], 0.0)
            pool.memset(steps_a[:, :], 0.0).then_inc(consts_made, 1)
            pool.wait_ge(consts_made, 2)
            pool.memset(pad_edges[:, ENODE:ENODE + 1], float(NONE))
            pool.affine_select(out=before[:, :], in_=before[:, :], compare_op=ALU.is_ge, fill=1.0,
                               base=0, pattern=[[-1, P]], channel_multiplier=1)
            pool.affine_select(out=steps_a[:, :], in_=steps_a[:, :], compare_op=ALU.not_equal, fill=1.0,
                               base=0, pattern=[[-1, A_OF]], channel_multiplier=1).then_inc(consts_made, 1)
            pool.wait_ge(consts_made, 3)
            pool.affine_select(out=steps_a[:, :], in_=steps_a[:, :], compare_op=ALU.not_equal, fill=-1.0,
                               base=1, pattern=[[-1, A_OF]], channel_multiplier=1)
            pool.memset(ln_eps[:, :], LN_EPS)
            pool.memset(ones_bf[:, :], 1.0)
            pool.memset(ones_col[:, :], 1.0)
            pool.memset(pad_msgs[:, :], 0.0)
            pool.memset(edge_out[:, :, ONE:ONE + 1], 1.0)
            pool.memset(edge_out[:, :, EC - 1:EC], 0.0)
            pool.memset(msgs[:, :, :, DCOL:MC], 0.0).then_inc(consts_made, 1)
            pool.wait_ge(lists_ready, 1)

            def sources1(k, u):
                i = 4 * k + u
                need(pool, xg_turned, i - 3)
                pool.tensor_copy(src_now[:, u, :], src_row[:, bass.ds(i * T, T)]).then_inc(src_placed, 1)
                pool.wait_ge(src_placed, i + 1)
                pool.sem_inc(wait_passed, 1)

            def gather1(u, j):
                pool.indirect_dma_start(
                    out=xg[:, u, j, :], out_offset=None, in_=x,
                    in_offset=bass.IndirectOffsetOnAxis(ap=src_now[:, u, j:j + 1], axis=0),
                ).then_inc(xg_loaded[u], 16)

            def stage1(k, u):
                pk, pu = back(k, u, 3)
                if valid(pk, pu, EG):
                    g = 4 * pk + pu
                    for h in range(2):
                        for j in (2 * h, 2 * h + 1):
                            pool.wait_ge(seeds_ready, g * T + j + 1)
                            if j % 2 == 0:
                                need(pool, chain1, CHAIN * (2 * g + h - 1))
                            pool.tensor_tensor(seed_sum[:, j, :], seeds[:, j, 0, :], seeds[:, j, 1, :],
                                               ALU.add).then_inc(seeds_half, 1)
                        for j in (2 * h, 2 * h + 1):
                            pool.wait_ge(seeds_half, g * T + j + 1)
                            pool.tensor_tensor(seed_sum[:, j, :], seed_sum[:, j, :], seeds[:, j, 2, :],
                                               ALU.add).then_inc(seeds_added, 1)
                if valid(k, u, EG):
                    sources1(k, u)
                    for j in range(T):
                        gather1(u, j)

            each(pool, EG, 3, stage1)

            def general(n):
                def tile(t):
                    if n == 1:
                        need(pool, g_stored[n], 16 * t)
                        pool.tensor_copy(g_from[:, :], edge_out[:, bass.ds(t, 1), EFROM].bitcast(i32))\
                            .then_inc(g_from_set, 1)
                        pool.wait_ge(g_from_set, t + 1)
                        pool.sem_inc(wait_passed, 1)
                        pool.indirect_dma_start(
                            out=g_x[:, :], out_offset=None, in_=x1_rows,
                            in_offset=bass.IndirectOffsetOnAxis(ap=g_from[:, :], axis=0)).then_inc(g_x_in, 16)
                    pool.wait_ge(g_at_set[n], t + 1)
                    pool.sem_inc(wait_passed, 1)
                    pool.indirect_dma_start(
                        out=g_sum[:, 0:g_cols[n]], out_offset=None, in_=g_table[n],
                        in_offset=bass.IndirectOffsetOnAxis(ap=g_at[:, :], axis=0),
                        bounds_check=g_base[n] + N - 1, oob_is_err=False).then_inc(g_fetched[n], 16)
                    pool.wait_ge(g_added[n], t + 1)
                    pool.sem_inc(wait_passed, 1)
                    pool.indirect_dma_start(
                        out=g_table[n], out_offset=bass.IndirectOffsetOnAxis(ap=g_at[:, :], axis=0),
                        in_=g_sum[:, 0:g_cols[n]], in_offset=None,
                        bounds_check=g_base[n] + N - 1, oob_is_err=False).then_inc(g_stored[n], 16)
                    pool.wait_ge(g_stored[n], 16 * (t + 1))
                    pool.sem_inc(wait_passed, 1)

                pool.wait_ge(g_rows_out[n], 16 * (n + 1) * NG)
                if n == 0:
                    for s in range(2):
                        pool.wait_ge(msgs_stored[s], 16 * len(range(s, EG, 2)))
                    pool.wait_ge(pads_stored, 48)
                g_tiles(pool, tile)

            pool.wait_ge(windows_ready, 1)
            ok = pool.value_load(ok_i[0:1, 0:1], min_val=0, max_val=1)
            with pool.If(ok < 1):
                general(0)

            pool.wait_ge(edge_cols, 1)

            def scatter2(k, u):
                i = 4 * k + u
                s = u % 2
                if valid(*back(k, u, 2), EG):
                    pool.wait_ge(edges_scattered[s], 64 * (2 * k + u // 2))
                pool.wait_ge(placed, i + 1)
                pool.tensor_copy(edge_now[:, s, :, :], edge_out[:, bass.ds(i * T, T), :])
                pool.tensor_copy(place_now[:, s, :], place_t[:, bass.ds(i * T, T)]).then_inc(edges_now, 1)
                pool.wait_ge(edges_now, i + 1)
                pool.sem_inc(wait_passed, 1)
                for j in range(T):
                    pool.indirect_dma_start(
                        out=edge_rows, out_offset=bass.IndirectOffsetOnAxis(ap=place_now[:, s, j:j + 1], axis=0),
                        in_=edge_now[:, s, j, :], in_offset=None, bounds_check=E - 1, oob_is_err=False,
                    ).then_inc(edges_scattered[s], 16)

            each(pool, EG, 0, scatter2)
            for s in range(2):
                pool.wait_ge(x1_stored[s], 16 * (NG // 2 + s))

            ok1 = pool.value_load(ok_i[0:1, 1:2], min_val=0, max_val=1)
            with pool.If(ok1 < 1):
                general(1)

            def stage3(k, u):
                pk, pu, p, ok = node_group(k, u, 4)
                if ok:
                    need(pool, y3, p - 2)
                    pool.wait_ge(in3[pu], rows_count(pk, pu))
                    pool.tensor_tensor(xb[:, pu % 3, HALF:T, :], xin[:, pu, HALF:T, :],
                                       beta_sb[:, :].unsqueeze(1).to_broadcast([P, T - HALF, D]), ALU.add)\
                        .then_inc(xb3_rest, 1)
                if valid(k, u, NG, U):
                    gather3(k, u)

            def gather3(k, u):
                i = U * k + u
                s = u % 3
                need(pool, sum3, i - 2)
                pool.wait_ge(ewin_loaded[u], 64 * (k + 1))
                pool.sem_inc(wait_passed, 1)
                with pool.If(ok1 < 1):
                    pool.dma_start(xg[:, s, :, :], tiles_of(sum_rows[bass.ds(node0(k, u), GP), :]))\
                        .then_inc(xg3_loaded[s], 64)
                with pool.Else():
                    for j in range(T):
                        pool.indirect_dma_start(
                            out=xg[:, s, j, :], out_offset=None, in_=x1_rows,
                            in_offset=bass.IndirectOffsetOnAxis(ap=ewin[:, u, j, EFROM:EFROM + 1].bitcast(i32),
                                                                axis=0)).then_inc(xg3_loaded[s], 16)

            each(pool, NG, 4, stage3, U)

        @block.vector
        def _(dve):
            steps = [0]

            def link(ins):
                steps[0] += 1
                ins.then_inc(dve0, 1)
                dve.wait_ge(dve0, steps[0])

            dve.memset(dst_q[96:QR, :], NONE)
            dve.memset(next_q[96:QR, :], NONE)
            dve.memset(src_q[96:QR, :], NONE)
            dve.memset(norm_q[96:QR, :], 0.0).then_inc(pads_set, 1)
            dve.wait_ge(lists_loaded, 16 * 8)
            dve.wait_ge(pads_set, 1)
            dve.tensor_copy(dst_qf[:, :], dst_q[:, :])
            dve.tensor_copy(src_qf[:, :], src_q[:, :]).then_inc(lists_f, 1)
            dve.tensor_copy(next_qf[:, :], next_q[:, :])
            dve.wait_ge(lists_turned, 1)
            for b, dest in enumerate((dst_t, src_t, norm_t)):
                dve.tensor_copy(dest[:, 0:ET].rearrange("p (q h) -> p q h", h=2),
                                bank[b][:, 0:ET].rearrange("p (h q) -> p q h", h=2))
            dve.memset(dst_t[:, ET:ET + 1], float(NONE))
            link(dve.memset(src_t[:, ET:ET + 1], float(NONE)))
            dve.tensor_scalar(src_row[:, :], src_t[:, 0:ET], float(N - 1), None, ALU.min)
            link(dve.tensor_scalar(dst_row[:, :], dst_t[:, :], float(N - 1), None, ALU.min))
            dve.tensor_scalar(skip_t[:, :], src_t[:, 0:ET], float(N), float(SKIP), ALU.is_ge, ALU.mult)\
                .then_inc(lists_ready, 1)
            dve.wait_ge(consts_made, 4)
            dve.tensor_copy(edge_out[:, :, ENODE:ENODE + 1], src_t[:, :].unsqueeze(2))
            dve.tensor_copy(edge_out[:, :, EFROM:EFROM + 1].bitcast(i32), dst_row[:, :].unsqueeze(2))
            dve.wait_ge(attr_loaded, 32)
            dve.wait_ge(consts_loaded, 16 * CONSTS)
            link(dve.tensor_scalar(eps1_sb[:, :], eps_sb[:, :], 1.0, None, ALU.add))
            dve.tensor_scalar(self_diag[:, :], ident[:, :], eps1_sb[:, 0:1], None, ALU.mult).then_inc(edge_cols, 1)
            link(dve.tensor_tensor(falls_q[:, :], dst_qf[:, :], next_qf[:, :], ALU.is_gt))
            dve.tensor_reduce(stat_q[:, :], falls_q[:, :], AX.X, ALU.add).then_inc(stats_ready, 1)
            dve.tensor_copy(node_i[:, 0, :], dst_t[:, 0:ET])
            link(dve.tensor_copy(node_i[:, 1, :], src_t[:, 0:ET]))
            dve.tensor_scalar(a_i[:, :, :], node_i[:, :, :], 12, None, ALU.logical_shift_right)
            link(dve.tensor_scalar(b_i[:, :, :], node_i[:, :, :], 7, None, ALU.logical_shift_right))
            link(dve.tensor_scalar(b_m[:, :, :], b_i[:, :, :], 31, None, ALU.bitwise_and))
            dve.tensor_copy(tile_f[:, :], b_i[:, 1, :])
            dve.tensor_copy(a_f[:, :, :], a_i[:, :, :])
            link(dve.tensor_copy(b_f[:, :, :], b_m[:, :, :]))
            ca = count_up[:, 0:A_OF].unsqueeze(1).to_broadcast([P, ET, A_OF])
            cb = count_up[:, 0:32].unsqueeze(1).to_broadcast([P, ET, 32])
            for n in range(2):
                av = a_f[:, n, :].unsqueeze(2).to_broadcast([P, ET, A_OF])
                bv = b_f[:, n, :].unsqueeze(2).to_broadcast([P, ET, 32])
                dve.tensor_tensor(a_eq[:, n, :].rearrange("p (t a) -> p t a", a=A_OF), av, ca, ALU.is_equal)
                dve.tensor_tensor(a_lt[:, n, :].rearrange("p (t a) -> p t a", a=A_OF), av, ca, ALU.is_lt)
                dve.tensor_tensor(b_lt[:, n, :].rearrange("p (t b) -> p t b", b=32), bv, cb, ALU.is_lt)\
                    .then_inc(marks_ready, 1)
            for n in range(2):
                dve.wait_ge(pairs_counted, n + 1)
                dve.tensor_copy(pairs_sb[:, n, :], bank[3 + n][0:CH * A_OF, 0:CH * 32]).then_inc(pairs_copied, 1)
            dve.wait_ge(counts_added, 1)
            dve.tensor_copy(counts_sb[:, :, :], bank[5][0:A_OF, 0:64].rearrange("a (l b) -> a l b", b=32))\
                .then_inc(counts_copied, 1)
            dve.wait_ge(stats_summed, 1)
            dve.tensor_copy(stat_row[:, :], bank[6][0:1, 0:1])
            dve.wait_ge(taken_done, 1)
            dve.tensor_copy(taken[:, 1, T, :], taken_bank[:, 0:32]).then_inc(taken_copied, 1)

            def place_step(k, u, n):
                i = 4 * k + u
                s = u % 2
                if n == 0:
                    dve.wait_ge(looked_up, i + 1)
                    dve.tensor_tensor(looked[:, s, :, :], b_hot[:, u, :, :],
                                      looked_bank.rearrange("p (t b) -> p t b", b=32), ALU.mult)\
                        .then_inc(looked_picked, 1)
                elif n == 1:
                    dve.wait_ge(looked_picked, i + 1)
                    dve.tensor_reduce(place_s[:, s, :], looked[:, s, :, :], AX.X, ALU.add)\
                        .then_inc(looked_summed, 1)
                elif n == 2:
                    dve.wait_ge(looked_summed, i + 1)
                    dve.tensor_tensor(place_f[:, s, :], place_s[:, s, :], skip_t[:, bass.ds(i * T, T)], ALU.add)\
                        .then_inc(ranks_added, 1)
                elif n == 3:
                    dve.wait_ge(ranks_added, i + 1)
                    dve.tensor_tensor(place_t[:, bass.ds(i * T, T)], place_f[:, s, :], ranks_bank, ALU.add)\
                        .then_inc(placed, 1)

            def chains(i, s, h):
                pair = 2 * i + h
                for b in range(SEED, B):
                    for w in range(2):
                        j = 2 * h + w
                        if b == SEED:
                            dve.wait_ge(seeds_added, i * T + j + 1)
                        if b == 4:
                            dve.wait_ge(products, 4 * pair + 3 + w)
                        if b > SEED:
                            dve.wait_ge(chain1, CHAIN * pair + 2 * (b - SEED) + w - 1)
                        of = first_half[j] if b < 4 else second_half[w]
                        dve.scalar_tensor_tensor(
                            out=msgs[:, s, j, 0:D], in0=of[:, (b % 4) * D:(b % 4 + 1) * D],
                            scalar=coef[:, s, j, b:b + 1],
                            in1=seed_sum[:, j, :] if b == SEED else msgs[:, s, j, 0:D],
                            op0=ALU.mult, op1=ALU.add).then_inc(chain1, 1)

            def stage1(k, u):
                i = 4 * k + u
                s = u % 2
                pk, pu = back(k, u, 2)
                if valid(k, u, EG):
                    dve.wait_ge(lists1_loaded[u], 32 * (k + 1))
                    need(dve, coef_done, i - 1)
                    dve.tensor_scalar(type_hot[:, s, :], types[:, u, :], part_no[0:R, 0:1], None,
                                      ALU.is_equal).then_inc(hot_types, 1)
                if valid(pk, pu, EG):
                    place_step(pk, pu, 0)
                if valid(k, u, EG):
                    need(dve, looked_up, i - 1)
                    dve.tensor_scalar(tiles_bc[:, s, :], srcs[:, u, :], 7, None, ALU.logical_shift_right)\
                        .then_inc(tiles_shifted, 1)
                if valid(pk, pu, EG):
                    place_step(pk, pu, 1)
                if valid(k, u, EG):
                    dve.tensor_scalar(a_ge[:, s, :], srcs[0:A_OF, u, :], a_from[:, 0:1], None, ALU.is_ge)\
                        .then_inc(a_marked, 1)
                if valid(pk, pu, EG):
                    place_step(pk, pu, 2)
                if valid(k, u, EG):
                    dve.tensor_tensor(a_hot[:, s, :, 1:A_OF + 1],
                                      a_f[:, 1, bass.ds(i * T, T)].unsqueeze(2).to_broadcast([P, T, A_OF]),
                                      count_up[:, 0:A_OF].unsqueeze(1).to_broadcast([P, T, A_OF]), ALU.is_equal)
                    dve.tensor_tensor(b_hot[:, u, :, :],
                                      b_f[:, 1, bass.ds(i * T, T)].unsqueeze(2).to_broadcast([P, T, 32]),
                                      count_up[:, 0:32].unsqueeze(1).to_broadcast([P, T, 32]), ALU.is_equal)\
                        .then_inc(hots_marked, 1)
                if valid(pk, pu, EG):
                    place_step(pk, pu, 3)
                if valid(k, u, EG):
                    dve.tensor_tensor(b_bf[:, s, :, :],
                                      b_f[:, 1, bass.ds(i * T, T)].unsqueeze(2).to_broadcast([P, T, 32]),
                                      count_up[:, 0:32].unsqueeze(1).to_broadcast([P, T, 32]), ALU.is_equal)
                    dve.wait_ge(tiles_shifted, i + 1)
                    for j in range(T):
                        dve.scalar_tensor_tensor(
                            out=same_tile[:, s, j, :], in0=tiles_bc[:, s, j * P:(j + 1) * P],
                            scalar=tile_f[:, bass.ds(i * T + j, 1)], in1=before[:, :],
                            op0=ALU.is_equal, op1=ALU.mult)
                    dve.wait_ge(hots_marked, i + 1)
                    dve.tensor_tensor(a_step[:, s, :, :], a_hot[:, s, :, 1:A_OF + 1], a_hot[:, s, :, 0:A_OF],
                                      ALU.subtract).then_inc(place_marks, 1)
                if valid(pk, pu, EG):
                    if valid(*back(pk, pu, 2), EG):
                        dve.wait_ge(msgs_stored[s], 16 * (2 * pk + pu // 2))
                    dve.tensor_copy(msgs[:, s, :, DCOL:DCOL + 1],
                                    dst_t[:, bass.ds((4 * pk + pu) * T, T)].unsqueeze(2))
                    chains(4 * pk + pu, s, 0)
                ck, cu = back(k, u, 1)
                if valid(ck, cu, EG):
                    c = 4 * ck + cu
                    dve.wait_ge(coef_done, c + 1)
                    dve.tensor_tensor(coef[:, cu % 2, :, :], coef_bank.rearrange("p (t b) -> p t b", b=B),
                                      norm_t[:, bass.ds(c * T, T)].unsqueeze(2).to_broadcast([P, T, B]),
                                      ALU.mult).then_inc(coef_ready, 1)
                if valid(pk, pu, EG):
                    chains(4 * pk + pu, s, 1)

            each(dve, EG, 2, stage1)

            dve.wait_ge(counts_in, 16)
            wsteps = [0]

            def wlink(ins):
                wsteps[0] += 1
                ins.then_inc(windows0, 1)
                dve.wait_ge(windows0, wsteps[0])

            wlink(dve.tensor_tensor(win_d[:, :, :], count_row[:, :, 1:NT + 1], count_row[:, :, 0:NT], ALU.subtract))
            dve.tensor_scalar(no_falls[:, :], stat_row[:, :], 0.0, None, ALU.is_equal)
            wlink(dve.tensor_reduce(most[:, :], win_d[:, :, :], AX.X, ALU.max))
            wlink(dve.tensor_scalar(fits[:, :], most[:, :], float(P), None, ALU.is_le))
            wlink(dve.tensor_tensor(fits[:, 0:1], fits[:, 0:1], no_falls[:, :], ALU.mult))
            dve.tensor_copy(ok_i[:, :], fits[:, :])
            wlink(dve.tensor_tensor(win_d[:, :, :], count_row[:, :, 0:NT], sums_start[:, :, :], ALU.subtract))
            for n in range(2):
                ins = dve.scalar_tensor_tensor(out=win_g[:, n, :], in0=win_d[:, n, :], scalar=fits[:, n:n + 1],
                                               in1=sums_start[:, n, :], op0=ALU.mult, op1=ALU.add)
            wlink(ins)
            dve.tensor_copy(win_row[:, :, :], win_g[:, :, :]).then_inc(windows_ready, 1)

            def general(n):
                b_key, b_attr, b_msg, b_sum, b_count = bank[0:5]
                if n == 1:
                    for s in range(2):
                        dve.wait_ge(x1_stored[s], 16 * (NG // 2 + s))

                def set_rows(g):
                    need(dve, g_rows_out[n], 16 * (n + 1) * g)
                    of, c = (g_rows, DCOL) if n == 0 else (g_edges, ENODE)
                    dve.tensor_scalar(of[:, :, c:c + 1], g_node0[:, :].unsqueeze(2),
                                      group_start[:, bass.ds(g, 1)], None, ALU.add).then_inc(g_rows_set[n], 1)

                def tile(t):
                    need(dve, g_stored[n], 16 * t)
                    dve.tensor_copy(g_key[:, :], g_keys[n][:, bass.ds(t, 1)])
                    if n == 1:
                        dve.tensor_copy(g_attr[:, :], edge_out[:, bass.ds(t, 1), 0:ED + 1].rearrange("p o c -> p (o c)"))
                    dve.tensor_copy(g_key_wide[:, :], g_keys[n][:, bass.ds(t, 1)].to_broadcast([P, P]))\
                        .then_inc(g_cols_set[n], 1)
                    dve.wait_ge(g_turned[n], t + 1)
                    if n == 1:
                        dve.tensor_copy(g_attr_t[:, :], b_attr[0:ED + 1, 0:P])
                    dve.tensor_scalar(g_same[:, :], b_key[:, 0:P], g_key[:, 0:1], None, ALU.is_equal)\
                        .then_inc(g_compared[n], 1)
                    dve.wait_ge(g_compared[n], t + 1)
                    dve.tensor_tensor(g_earlier[:, :], g_same[:, :], before[:, :], ALU.mult).then_inc(g_marked[n], 1)
                    if n == 1:
                        dve.wait_ge(g_attr_out, t + 1)
                        dve.wait_ge(g_x_in, 16 * (t + 1))
                        dve.tensor_tensor(g_msg[:, :], g_x[:, :], b_msg[:, 0:D], ALU.add).then_inc(g_msg_made, 1)
                    dve.wait_ge(g_combined[n], t + 1)
                    dve.tensor_scalar(g_again[:, :], b_count[:, 0:1], 0.0, float(SKIP), ALU.is_gt, ALU.mult)\
                        .then_inc(g_again_set[n], 1)
                    dve.wait_ge(g_again_set[n], t + 1)
                    dve.scalar_tensor_tensor(out=g_at[:, :], in0=g_again[:, :], scalar=float(g_base[n]),
                                             in1=g_key[:, :], op0=ALU.add, op1=ALU.add).then_inc(g_at_set[n], 1)
                    dve.wait_ge(g_fetched[n], 16 * (t + 1))
                    dve.tensor_tensor(g_sum[:, 0:D], g_sum[:, 0:D], b_sum[:, 0:D], ALU.add).then_inc(g_added[n], 1)

                dve.memset(g_rows[:, :, :], 0.0)
                dve.memset(g_edges[:, :, :], 0.0)
                dve.memset(g_sum[:, :], 0.0).then_inc(g_begun[n], 1)
                dve.wait_ge(g_begun[n], 1)
                g_groups(dve, set_rows)
                g_tiles(dve, tile)
                dve.wait_ge(g_stored[n], 16 * ET)

            dve.wait_ge(windows_ready, 1)
            ok = dve.value_load(ok_i[0:1, 0:1], min_val=0, max_val=1)
            with dve.If(ok < 1):
                general(0)

            def make_hot(i, u, used, dcol, win, done):
                need(dve, used, i - 2)
                dve.scalar_tensor_tensor(
                    out=hot[:, u % 3, :, :], in0=count_up[:, :].rearrange("p (t n) -> p t n", n=P),
                    scalar=group_start[:, bass.ds(i, 1)],
                    in1=win[:, u, :, dcol:dcol + 1].to_broadcast([P, T, P]),
                    op0=ALU.add, op1=ALU.is_equal).then_inc(done, 1)

            def stage2(k, u):
                if valid(k, u, NG, U):
                    dve.wait_ge(mwin_loaded[u], 64 * (k + 1))
                    make_hot(U * k + u, u, sum2, DCOL, mwin, hot2)
                nk, nu, n, norms = node_group(k, u, 4)
                ns = nu % 2
                if norms:
                    dve.wait_ge(sd2_done, n + 1)
                    need(dve, x1_halved, n - 1)
                    dve.reciprocal(rstd[:, ns, 0, :], sd[:, ns, 0, :]).then_inc(rstd2_done, 1)
                pk, pu, p, ok = node_group(k, u, 3)
                s = pu % 2
                if ok:
                    dve.wait_ge(back2, p + 1)
                    need(dve, x1_halved, p - 2)
                    need(dve, x1_done, p - 2)
                    dve.tensor_tensor(y[:, pu % 3, :, :], xin[:, pu, :, :],
                                      bank[4 + s][:, :].rearrange("p (t d) -> p t d", d=D), ALU.add).then_inc(y2, 1)
                if norms:
                    dve.wait_ge(rstd2_done, n + 1)
                    dve.scalar_tensor_tensor(out=shift[:, ns, :].unsqueeze(2), in0=mv[:, ns, 0, :, 0:1], scalar=-1.0,
                                             in1=rstd[:, ns, 0, :].unsqueeze(2), op0=ALU.mult, op1=ALU.mult)\
                        .then_inc(norm2, 1)
                if ok:
                    dve.wait_ge(y2, p + 1)
                    for j in range(T):
                        ins = dve.bn_stats(st[:, s, j, :], y[:, pu % 3, j, :])
                    ins.then_inc(st2_done, 1)
                if norms:
                    dve.wait_ge(norm2, n + 1)
                    need(dve, x1_stored[ns], stored_before(nk, nu))
                    for j in range(ACT_TILES, T):
                        ins = dve.tensor_scalar(res[:, ns, j, :], y[:, nu % 3, j, :], rstd[:, ns, 0, j:j + 1],
                                                shift[:, ns, j:j + 1], ALU.mult, ALU.add)
                    ins.then_inc(x1_done, 1)
                if ok:
                    dve.wait_ge(st2_done, p + 1)
                    dve.sem_inc(wait_passed, 1)
                    for j in range(T):
                        ins = dve.bn_aggr(mv[:, s, 0, j, :], st[:, s, j, :])
                    ins.then_inc(mv2_done, 1)

            each(dve, NG, 4, stage2, U)

            ok1 = dve.value_load(ok_i[0:1, 1:2], min_val=0, max_val=1)
            with dve.If(ok1 < 1):
                general(1)

            dve.wait_ge(norm2, NG)
            dve.memset(mv[:, :, :, :, :], 0.0).then_inc(stats_zeroed, 1)
            dve.wait_ge(stats_zeroed, 1)

            def stage3(k, u):
                outer_k, outer_u, outer, outer_ok = node_group(k, u, 6)
                mid_k, mid_u, mid, mid_ok = node_group(k, u, 5)
                inner_k, inner_u, inner, inner_ok = node_group(k, u, 4)
                m = mid_u % 2
                if mid_ok or outer_ok:
                    dve.wait_ge(sd3, mid + 1)
                    need(dve, out_done, outer - 1)
                    dve.reciprocal(rstd[:, m, :, :], sd[:, m, :, :]).then_inc(rstd3, 1)
                if valid(k, u, NG, U):
                    dve.wait_ge(ewin_loaded[u], 64 * (k + 1))
                    make_hot(U * k + u, u, sum3, ENODE, ewin, hot3)
                if mid_ok or outer_ok:
                    dve.wait_ge(rstd3, mid + 1)
                if outer_ok:
                    dve.scalar_tensor_tensor(out=shift[:, m, :].unsqueeze(2), in0=mv[:, m, 0, :, 0:1],
                                             scalar=-1.0, in1=rstd[:, m, 0, :].unsqueeze(2),
                                             op0=ALU.mult, op1=ALU.mult).then_inc(norm3, 1)
                if mid_ok:
                    need(dve, out_done, mid - 1)
                    dve.wait_ge(xb3_rest, mid + 1)
                    for j in range(T):
                        ins = dve.scalar_tensor_tensor(out=y[:, m, j, :], in0=z[:, m, j, :],
                                                       scalar=rstd[:, m, 1, j:j + 1], in1=xb[:, mid_u % 3, j, :],
                                                       op0=ALU.mult, op1=ALU.add)
                    ins.then_inc(y3, 1)
                s = inner_u % 2
                b = bank[6 + s]
                if inner_ok:
                    dve.wait_ge(back3, inner + 1)
                    for j in range(T):
                        ins = dve.bn_stats(st[:, s, j, :], b[:, j * D:(j + 1) * D])
                    ins.then_inc(st3a, 1)
                if mid_ok:
                    dve.wait_ge(y3, mid + 1)
                    for j in range(T):
                        ins = dve.bn_stats(st2[:, m, j, :], y[:, m, j, :])
                    ins.then_inc(st3b, 1)
                if inner_ok:
                    dve.wait_ge(st3a, inner + 1)
                    dve.sem_inc(wait_passed, 1)
                    for j in range(T):
                        ins = dve.bn_aggr(mv[:, s, 1, j, :], st[:, s, j, :])
                if mid_ok:
                    dve.wait_ge(st3b, mid + 1)
                    dve.sem_inc(wait_passed, 1)
                    for j in range(T):
                        ins = dve.bn_aggr(mv[:, s, 0, j, :], st2[:, m, j, :])
                if inner_ok or mid_ok:
                    ins.then_inc(mv3, 1)
                    dve.wait_ge(mv3, inner + 1)
                if inner_ok:
                    for j in range(T):
                        ins = dve.scalar_tensor_tensor(out=z[:, s, j, :], in0=b[:, j * D:(j + 1) * D],
                                                       scalar=mv[:, s, 1, j, 0:1], in1=gamma_sb[:, :],
                                                       op0=ALU.subtract, op1=ALU.mult)
                    ins.then_inc(z3, 1)
                pk, pu, p, ok = node_group(k, u, 2)
                if ok:
                    dve.wait_ge(in3[pu], rows_count(pk, pu))
                    dve.tensor_tensor(xb[:, pu % 3, 0:HALF, :], xin[:, pu, 0:HALF, :],
                                      beta_sb[:, :].unsqueeze(1).to_broadcast([P, HALF, D]), ALU.add)\
                        .then_inc(xb3, 1)

            each(dve, NG, 6, stage3, U)

        @block.tensor
        def _(pe):
            pe.wait_ge(consts_made, 4)
            pe.wait_ge(lists_f, 1)
            for b, q in enumerate((dst_qf, src_qf, norm_q)):
                for h in range(2):
                    ins = pe.transpose(bank[b][:, h * QR:(h + 1) * QR], q[:, h * P:(h + 1) * P],
                                       ident[0:QR, 0:QR])
            ins.then_inc(lists_turned, 1)
            pe.wait_ge(stats_ready, 1)
            pe.matmul(bank[6][0:1, 0:1], ones_col[0:QR, :], stat_q[:, :], start=True, stop=True)\
                .then_inc(stats_summed, 1)
            for n in range(2):
                pe.wait_ge(marks_ready, n + 1)
                for c in range(NCH):
                    ca = slice(c * CH * A_OF, (c + 1) * CH * A_OF)
                    pe.matmul(bank[3 + n][0:CH * A_OF, 0:CH * 32], a_lt[:, n, ca], ones_bf[:, :],
                              start=(c == 0), stop=False)
                    ins = pe.matmul(bank[3 + n][0:CH * A_OF, 0:CH * 32], a_eq[:, n, ca],
                                    b_lt[:, n, c * CH * 32:(c + 1) * CH * 32], start=False, stop=(c == NCH - 1))
                ins.then_inc(pairs_counted, 1)
            for n in range(2):
                pe.wait_ge(pairs_copied, n + 1)
                for c in range(CH):
                    ins = pe.matmul(bank[5][0:A_OF, n * 32:(n + 1) * 32],
                                    ident[0:CH * A_OF, c * A_OF:(c + 1) * A_OF],
                                    pairs_sb[:, n, c * 32:(c + 1) * 32], start=(c == 0), stop=(c == CH - 1))
            ins.then_inc(counts_added, 1)
            pe.wait_ge(counts_copied, 1)
            pe.matmul(taken_bank[:, 0:32], steps_a[:, :], counts_sb[:, 1, :], start=True, stop=True)\
                .then_inc(taken_done, 1)
            pe.wait_ge(consts_loaded, 16 * CONSTS)
            pe.wait_ge(taken_copied, 1)

            def pair_products(k, u, h, half):
                i = 4 * k + u
                pair = 2 * i + h
                for w in range(2):
                    j = 2 * h + w
                    if half == 0:
                        need(pe, chain1, CHAIN * (pair - 2) + 2 * (4 - SEED) - (1 - w))
                    else:
                        need(pe, chain1, CHAIN * (pair - 1) + CHAIN - (1 - w))
                    pe.matmul((second_half[w] if half else first_half[j])[:, :],
                              xg_t[:, u % 2, j * P:(j + 1) * P],
                              basis_sb[:, 4 * half:4 * half + 4, :], start=True, stop=True)\
                        .then_inc(products, 1)

            def stage1(k, u):
                i = 4 * k + u
                s = u % 2
                pk, pu = back(k, u, 1)
                if valid(pk, pu, EG):
                    pe.wait_ge(xg_t_ready, 4 * pk + pu + 1)
                    pair_products(pk, pu, 0, 0)
                    pair_products(pk, pu, 0, 1)
                    pair_products(pk, pu, 1, 0)
                if valid(k, u, EG):
                    pe.wait_ge(xg_loaded[u], 64 * (k + 1))
                    need(pe, xg_t_ready, i)
                    for j in range(T):
                        ins = pe.transpose(turned_bank[:, j * P:(j + 1) * P], xg[:, u, j, :], ident[:, :])
                    ins.then_inc(xg_turned, 1)
                    pe.wait_ge(hot_types, i + 1)
                    pe.wait_ge(place_marks, i + 1)
                    pe.wait_ge(taken_copied, i + 1)
                    need(pe, placed, i)
                    for j in range(T):
                        ins = pe.matmul(coef_bank[:, j * B:(j + 1) * B], type_hot[:, s, j * P:(j + 1) * P],
                                        w_comp_sb[:, :], start=True, stop=True)
                    for j in range(T + 1):
                        part = taken_bank[:, 32 * j:32 * (j + 1)]
                        ins = pe.matmul(part, ident[0:A_OF, 0:A_OF], taken[:, 1 - s, T, :],
                                        start=True, stop=(j == 0))
                        for m in range(j):
                            ins = pe.matmul(part, a_step[:, s, m, :], b_bf[:, s, m, :],
                                            start=False, stop=(m == j - 1))
                    ins.then_inc(coef_done, 1)
                if valid(pk, pu, EG):
                    pair_products(pk, pu, 1, 1)
                if valid(k, u, EG):
                    pe.wait_ge(taken_copied, i + 2)
                    pe.wait_ge(coef_ready, i + 1)
                    for j in range(T):
                        pe.matmul(ranks_bank[:, j:j + 1], same_tile[:, s, j, :], ones_bf[:, 0:1],
                                  start=True, stop=True)
                        ins = pe.matmul(looked_bank[:, 32 * j:32 * (j + 1)],
                                        a_ge[:, s, j * P:(j + 1) * P], taken[:, s, j, :], start=True, stop=True)
                    ins.then_inc(looked_up, 1)

            each(pe, EG, 1, stage1)

            def general(n):
                b_key, b_attr, b_msg, b_sum, b_count = bank[0:5]

                def tile(t):
                    pe.wait_ge(g_cols_set[n], t + 1)
                    need(pe, g_added[n], t)
                    ins = pe.transpose(b_key[:, 0:P], g_key_wide[:, :], ident[:, :])
                    if n == 1:
                        ins = pe.transpose(b_attr[0:ED + 1, 0:P], g_attr[:, :], ident[:, :])
                    ins.then_inc(g_turned[n], 1)
                    pe.wait_ge(g_marked[n], t + 1)
                    if n == 1:
                        pe.matmul(b_msg[:, 0:D], g_attr_t[:, :], we_sb[:, :], start=True, stop=True)\
                            .then_inc(g_attr_out, 1)
                        pe.wait_ge(g_msg_made, t + 1)
                    else:
                        pe.wait_ge(g_msg_in, 16 * (t + 1))
                    pe.matmul(b_sum[:, 0:D], g_same[:, :], g_msg[:, :], start=True, stop=True)
                    pe.matmul(b_count[:, 0:1], g_earlier[:, :], ones_col[:, :], start=True, stop=True)\
                        .then_inc(g_combined[n], 1)

                g_tiles(pe, tile)
                pe.wait_ge(g_added[n], ET)

            pe.wait_ge(windows_ready, 1)
            ok = pe.value_load(ok_i[0:1, 0:1], min_val=0, max_val=1)
            with pe.If(ok < 1):
                general(0)

            def stage2(k, u):
                if valid(k, u, NG, U):
                    i = U * k + u
                    pe.wait_ge(in2[u], rows_count(k, u))
                    need(pe, lhs2, i - 1)
                    for j in range(T):
                        ins = pe.transpose(bank[0 + u % 2][:, j * P:(j + 1) * P], xin[:, u, j, :], ident[:, :])
                    ins.then_inc(turned2, 1)
                pk, pu, p, ok = node_group(k, u, 1)
                if ok:
                    s = pu % 2
                    pe.wait_ge(hot2, p + 1)
                    need(pe, act2, p - 1)
                    pe.wait_ge(lhs2, p + 1)
                    pe.matmul(bank[2 + s][:, :], loop_sb[:, :], lhs_t[:, s, :], start=True, stop=False,
                              skip_group_check=True)
                    for j in range(T):
                        ins = pe.matmul(bank[2 + s][:, j * P:(j + 1) * P], mwin[:, pu, j, 0:D],
                                        hot[:, pu % 3, j, :], start=False, stop=(j == T - 1),
                                        skip_group_check=True)
                    ins.then_inc(sum2, 1)
                pk, pu, p, ok = node_group(k, u, 2)
                if ok:
                    s = pu % 2
                    need(pe, y2, p - 1)
                    pe.wait_ge(act2, p + 1)
                    for j in range(T):
                        ins = pe.transpose(bank[4 + s][:, j * P:(j + 1) * P], act_t[:, s, j * P:(j + 1) * P],
                                           ident[:, :])
                    ins.then_inc(back2, 1)

            each(pe, NG, 2, stage2, U)

            ok1 = pe.value_load(ok_i[0:1, 1:2], min_val=0, max_val=1)
            with pe.If(ok1 < 1):
                general(1)

            def stage3(k, u):
                pk, pu, p, ok = node_group(k, u, 1)
                if ok:
                    b = bank[0 + pu % 2]
                    need(pe, lhs3, p - 1)
                    pe.wait_ge(in3[pu], rows_count(pk, pu))
                    pe.wait_ge(ea3_copied, p + 1)
                    pe.matmul(b[:, :], we_sb[:, :], ea_t[:, pu % 2, :], start=True, stop=False,
                              skip_group_check=True)
                    for j in range(T):
                        pe.matmul(b[:, j * P:(j + 1) * P], xin[:, pu, j, :], self_diag[:, :],
                                  start=False, stop=False, skip_group_check=True)
                    pe.wait_ge(xg3_loaded[pu % 3], 64 * (U // 3 * pk + pu // 3 + 1))
                    for j in range(T):
                        ins = pe.matmul(b[:, j * P:(j + 1) * P], xg[:, pu % 3, j, :], hot[:, pu % 3, j, :],
                                        start=False, stop=(j == T - 1), skip_group_check=True)
                    ins.then_inc(sum3, 1)
                pk, pu, p, ok = node_group(k, u, 2)
                ps = pu % 2
                if ok:
                    need(pe, act3, p - 1)
                    pe.wait_ge(lhs3, p + 1)
                    pe.matmul(bank[3 + ps][:, :], w1_sb[:, :], lhs_t[:, ps, :], start=True, stop=True)\
                        .then_inc(mid3, 1)
                if valid(k, u, NG, U):
                    i = U * k + u
                    need(pe, ea3_copied, i)
                    pe.wait_ge(hot3, i + 1)
                    for j in range(T):
                        ins = pe.matmul(bank[2][0:ED + 1, j * P:(j + 1) * P], ewin[:, u, j, 0:ED + 1],
                                        hot[:, u % 3, j, :], start=True, stop=True)
                    ins.then_inc(ea3, 1)
                bk, bu, g, turns = node_group(k, u, 3)
                if turns:
                    bs = bu % 2
                    need(pe, z3, g - 1)
                    pe.wait_ge(o3_copied, g + 1)
                    for j in range(T):
                        ins = pe.transpose(bank[6 + bs][:, j * P:(j + 1) * P], out_t[:, bs, j * P:(j + 1) * P],
                                           ident[:, :])
                    ins.then_inc(back3, 1)
                if ok:
                    need(pe, o3_copied, p)
                    pe.wait_ge(act3, p + 1)
                    pe.matmul(bank[5][:, :], w2_sb[:, :], act_t[:, ps, :], start=True, stop=True).then_inc(o3, 1)

            each(pe, NG, 3, stage3, U)

        @block.scalar
        def _(act):
            def pair_seeds(k, u, h):
                i = 4 * k + u
                for w in range(2):
                    j = 2 * h + w
                    act.wait_ge(products, 4 * (2 * i + h) + w + 1)
                    need(act, seeds_added, i * T + j - T + 1)
                    for b in range(SEED):
                        ins = act.activation(seeds[:, j, b, :], first_half[j][:, b * D:(b + 1) * D], ACT.Copy,
                                             scale=coef[:, u % 2, j, b:b + 1])
                    ins.then_inc(seeds_ready, 1)

            def stage1(k, u):
                i = 4 * k + u
                s = u % 2
                pk, pu = back(k, u, 1)
                if valid(pk, pu, EG):
                    pair_seeds(pk, pu, 0)
                    pair_seeds(pk, pu, 1)
                if valid(k, u, EG):
                    act.wait_ge(xg_turned, i + 1)
                    need(act, products, 8 * (i - 1))
                    act.activation(xg_t[:, s, :], turned_bank[:, :], ACT.Copy).then_inc(xg_t_ready, 1)
                if valid(k, u, EG):
                    act.wait_ge(coef_ready, i + 1)
                    need(act, looked_up, i - 1)
                    act.activation(taken[:, s, :, :], taken_bank.rearrange("a (t b) -> a t b", b=32),
                                   ACT.Copy).then_inc(taken_copied, 1)

            each(act, EG, 1, stage1)

            act.wait_ge(consts_loaded, 16 * CONSTS)

            def normalise(u, m, ys, tiles, done):
                for j in tiles:
                    ins = act.activation(res[:, u % 2, j, :], y[:, ys, j, :], ACT.Identity,
                                         scale=rstd[:, m, 0, j:j + 1], bias=shift[:, m, j:j + 1])
                ins.then_inc(done, 1)

            def load_x(k, u):
                need(act, y2, U * k + u - U + 1)
                load_nodes(act, k, u, x, in2[u])

            for i in range(AHEAD):
                load_x(0, i)

            def stage2(k, u):
                pk, pu, p, ok = node_group(k, u, 5)
                if ok:
                    act.wait_ge(x1_halved, p + 1)
                    act.wait_ge(x1_done, p + 1)
                    for rows, tiles in rows_and_tiles(x1_rows, res[:, pu % 2, :, :], pk, pu):
                        act.dma_start(rows, tiles).then_inc(x1_stored[pu % 2], 16)
                if valid(k, u, NG, U):
                    i = U * k + u
                    need(act, sum2, i - 1)
                    act.wait_ge(turned2, i + 1)
                    act.activation(lhs_t[:, u % 2, :], bank[0 + u % 2][:, :], ACT.Copy).then_inc(lhs2, 1)
                pk, pu, p, ok = node_group(k, u, 1)
                if ok:
                    s = pu % 2
                    need(act, back2, p - 1)
                    act.wait_ge(sum2, p + 1)
                    act.activation(act_t[:, s, :], bank[2 + s][:, :], ACT.Relu, bias=h_bias_sb[:, 0:1])\
                        .then_inc(act2, 1)
                pk, pu, p, ok = node_group(k, u, 4)
                if ok:
                    need(act, x1_stored[pu % 2], stored_before(pk, pu))
                    act.wait_ge(norm2, p + 1)
                    normalise(pu, pu % 2, pu % 3, range(ACT_TILES), x1_halved)
                pk, pu, p, ok = node_group(k, u, 3)
                if ok:
                    s = pu % 2
                    need(act, rstd2_done, p - 1)
                    act.wait_ge(mv2_done, p + 1)
                    act.activation(sd[:, s, 0, :].unsqueeze(2), mv[:, s, 0, :, 1:2], ACT.Sqrt, bias=ln_eps[:, 0:1])\
                        .then_inc(sd2_done, 1)
                if valid(*back(k, u, -AHEAD, U), NG, U):
                    load_x(*back(k, u, -AHEAD, U))

            each(act, NG, 5, stage2, U, AHEAD)
            for s in range(2):
                act.wait_ge(x1_stored[s], 16 * (NG // 2 + s))

            def stage3(k, u):
                pk, pu, p, ok = node_group(k, u, 1)
                if ok:
                    s = pu % 2
                    need(act, mid3, p - 1)
                    act.wait_ge(sum3, p + 1)
                    act.activation(lhs_t[:, s, :], bank[0 + s][:, :], ACT.Copy).then_inc(lhs3, 1)
                pk, pu, p, ok = node_group(k, u, 2)
                s = pu % 2
                if ok:
                    need(act, o3, p - 1)
                    act.wait_ge(mid3, p + 1)
                    act.activation(act_t[:, s, :], bank[3 + s][:, :], ACT.Relu, bias=b1_sb[:, 0:1])\
                        .then_inc(act3, 1)
                if valid(k, u, NG, U):
                    i = U * k + u
                    need(act, sum3, i - 1)
                    act.wait_ge(ea3, i + 1)
                    act.activation(ea_t[:, u % 2, :], bank[2][0:ED + 1, :], ACT.Copy).then_inc(ea3_copied, 1)
                ek, eu, e, ends = node_group(k, u, 7)
                if ends:
                    act.wait_ge(out_done, e + 1)
                    for rows, tiles in rows_and_tiles(out, res[:, eu % 2, :, :], ek, eu):
                        act.dma_start(rows, tiles).then_inc(out_stored[eu % 2], 16)
                if ok:
                    need(act, back3, p - 1)
                    act.wait_ge(o3, p + 1)
                    act.activation(out_t[:, s, :], bank[5][:, :], ACT.Identity, bias=b2_sb[:, 0:1])\
                        .then_inc(o3_copied, 1)
                pk, pu, p, inner_ok = node_group(k, u, 4)
                s = pu % 2
                if inner_ok or node_group(k, u, 5)[3]:
                    need(act, rstd3, p - 1)
                    act.wait_ge(mv3, p + 1)
                    act.activation(sd[:, s, :, :].unsqueeze(3), mv[:, s, :, :, 1:2], ACT.Sqrt, bias=ln_eps[:, 0:1])\
                        .then_inc(sd3, 1)
                pk, pu, p, ok = node_group(k, u, 6)
                if ok:
                    need(act, out_stored[pu % 2], stored_before(pk, pu))
                    act.wait_ge(norm3, p + 1)
                    normalise(pu, (pu + 1) % 2, pu % 2, range(T), out_done)

            each(act, NG, 7, stage3, U)


_INS = ['x', 'src', 'dst', 'edge_attr_32', 'edge_type_32', 'edge_weight1', 'L0_gnn_weight', 'L0_gnn_w_comp',
        'L0_gnn_loop_weight', 'L0_gnn_h_bias', 'L1_gnn_We', 'L1_gnn_be', 'L1_gnn_W1', 'L1_gnn_b1', 'L1_gnn_W2',
        'L1_gnn_b2', 'L1_gnn_eps', 'L1_gnn_gamma', 'L1_gnn_beta']


def kernel(**inputs):
    import numpy as _np
    import concourse.bacc as _bacc
    from concourse import mybir as _mybir
    from concourse.bass_utils import run_bass_kernel_spmd as _run

    nc = _bacc.Bacc("TRN2", target_bir_lowering=False, num_devices=1)
    arrays, args = {}, []
    for name in _INS:
        a = _np.ascontiguousarray(inputs[name])
        arrays[f"in_{name}"] = a
        args.append(nc.dram_tensor(f"in_{name}", a.shape, _mybir.dt.from_np(a.dtype), kind="ExternalInput").ap())
    out = nc.dram_tensor("out_0", arrays["in_x"].shape, _mybir.dt.float32, kind="ExternalOutput").ap()
    gnn_two_layers(nc, *args, out)
    r = _run(nc, [arrays], core_ids=[0])
    return r.results[0]["out_0"]
```
